# Optimizing a Trainium2 kernel written in Bass

```python
import numpy as np
import jax
import jax.numpy as jnp

def _softmax(x, axis=-1):
    return jax.nn.softmax(x, axis=axis)

def _gelu(x):
    return jax.nn.gelu(x, approximate=True)

def _silu(x):
    return jax.nn.silu(x)

def _sigmoid(x):
    return jax.nn.sigmoid(x)

def _layernorm(x, axis=-1, eps=1e-05):
    m = jnp.mean(x, axis=axis, keepdims=True)
    v = jnp.var(x, axis=axis, keepdims=True)
    return (x - m) / jnp.sqrt(v + eps)

def _scatter_add(tgt, idx, src, axis=0):
    return tgt.at[idx].add(src)

def _segment_sum(src, seg, n):
    return jax.ops.segment_sum(src, seg, n)
kernel_name = 'mk_gnn_ffn_d1_gnn_r8_0301cf'

def setup_inputs(seed: int=0):
    np.random.seed(seed)
    _w = jnp.asarray

    def _rec_inputs():
        import jax
        import jax.numpy as jnp
        _gk = jax.random.key(seed)
        x = -0.0003713 + 1 * jax.random.normal(jax.random.fold_in(_gk, 1), (6250, 256), jnp.float32)
        src = jax.random.randint(jax.random.fold_in(_gk, 2), (100000,), 0, 6250, jnp.int32)
        dst = jax.random.randint(jax.random.fold_in(_gk, 3), (100000,), 0, 6250, jnp.int32)
        _o = jnp.argsort(dst, stable=True)
        src = src[_o]
        dst = dst[_o]
        edge_weight1 = jax.random.uniform(jax.random.fold_in(_gk, 12), (100000, 1), jnp.float32, 0.0, 0.999998)
        return (x, src, dst, edge_weight1)
    x, src, dst, edge_weight1 = _rec_inputs()

    def _L0_gnn_setup():
        import jax, jax.numpy as jnp
        import numpy as np
        N_NODES = 6250
        DIM_H = 256
        N_EDGES = 100000
        LN_EPS = 1e-05

        def _layer_norm(x, g, b):
            mu = jnp.mean(x, axis=-1, keepdims=True)
            var = jnp.mean(jnp.square(x - mu), axis=-1, keepdims=True)
            return (x - mu) * jax.lax.rsqrt(var + LN_EPS) * g + b
        key = jax.random.key(seed)
        ks = jax.random.split(key, 12)
        d = DIM_H

        def lin(k, fan_in, fan_out):
            lim = 1.0 / np.sqrt(fan_in)
            kw, kb = jax.random.split(k)
            W = jax.random.uniform(kw, (fan_in, fan_out), jnp.float32, -lim, lim)
            b = jax.random.uniform(kb, (fan_out,), jnp.float32, -lim, lim)
            return (W, b)
        h = jax.random.normal(ks[0], (N_NODES, d), jnp.float32)
        e = jax.random.randint(ks[1], (2, N_EDGES), 0, N_NODES, jnp.int64)
        d2 = jax.random.uniform(ks[2], (N_EDGES, 1), jnp.float32)
        mW1, mb1 = lin(ks[3], 2 * d + 1, d)
        mW2, mb2 = lin(ks[4], d, d)
        ln_g = jnp.ones((d,), jnp.float32)
        ln_b = jnp.zeros((d,), jnp.float32)
        uW1, ub1 = lin(ks[5], 2 * d, d)
        uW2, ub2 = lin(ks[6], d, d)
        return {'h': h, 'e': e, 'd2': d2, 'mW1': mW1, 'mb1': mb1, 'ln_g': ln_g, 'ln_b': ln_b, 'mW2': mW2, 'mb2': mb2, 'uW1': uW1, 'ub1': ub1, 'uW2': uW2, 'ub2': ub2}
    _L0_gnn_all = _L0_gnn_setup()
    _L0_gnn_in = {k: v for k, v in _L0_gnn_all.items() if k in ('mW1', 'mb1', 'ln_g', 'ln_b', 'mW2', 'mb2', 'uW1', 'ub1', 'uW2', 'ub2')}
    del _L0_gnn_all

    def _L0_ffn_setup():
        import jax, jax.numpy as jnp
        import numpy as np
        NUM_EXPERTS = 8
        TOP_K = 2
        B, S, D = (8, 1024, 256)

        def _moe(tokens, router_w, w1, b1, w2, b2):
            N = tokens.shape[0]
            E = router_w.shape[0]
            logits = tokens.astype(jnp.float32) @ router_w.astype(jnp.float32).T
            probs = jax.nn.softmax(logits, axis=-1)
            rw, re = jax.lax.top_k(probs, TOP_K)
            if TOP_K > 1:
                rw = rw / jnp.maximum(rw.sum(-1, keepdims=True), 1e-12)
            rw = rw.astype(tokens.dtype)
            combine = jnp.zeros((N, E), tokens.dtype).at[jnp.arange(N)[:, None], re].set(rw)
            out = tokens
            for e in range(E):
                h = jax.nn.gelu(tokens @ w1[e] + b1[e], approximate=False)
                y = h @ w2[e] + b2[e]
                out = out + combine[:, e:e + 1] * y
            return out
        key = jax.random.key(seed)
        ks = jax.random.split(key, 4)
        scale = 1.0 / np.sqrt(D).astype(np.float32)
        return {'input_embeddings': jax.random.normal(ks[0], (B, S, D), jnp.float32), 'router_w': jax.random.normal(ks[1], (NUM_EXPERTS, D), jnp.float32) * scale, 'w1': jax.random.normal(ks[2], (NUM_EXPERTS, D, D), jnp.float32) * scale, 'b1': jnp.zeros((NUM_EXPERTS, D), jnp.float32), 'w2': jax.random.normal(ks[3], (NUM_EXPERTS, D, D), jnp.float32) * scale, 'b2': jnp.zeros((NUM_EXPERTS, D), jnp.float32)}
    _L0_ffn_all = _L0_ffn_setup()
    _L0_ffn_in = {k: v for k, v in _L0_ffn_all.items() if k in ('router_w', 'w1', 'b1', 'w2', 'b2')}
    del _L0_ffn_all
    return {'x': x, 'src': src, 'dst': dst, 'edge_weight1': edge_weight1, 'L0_gnn_mW1': _L0_gnn_in['mW1'], 'L0_gnn_mb1': _L0_gnn_in['mb1'], 'L0_gnn_ln_g': _L0_gnn_in['ln_g'], 'L0_gnn_ln_b': _L0_gnn_in['ln_b'], 'L0_gnn_mW2': _L0_gnn_in['mW2'], 'L0_gnn_mb2': _L0_gnn_in['mb2'], 'L0_gnn_uW1': _L0_gnn_in['uW1'], 'L0_gnn_ub1': _L0_gnn_in['ub1'], 'L0_gnn_uW2': _L0_gnn_in['uW2'], 'L0_gnn_ub2': _L0_gnn_in['ub2'], 'L0_ffn_router_w': _L0_ffn_in['router_w'], 'L0_ffn_w1': _L0_ffn_in['w1'], 'L0_ffn_b1': _L0_ffn_in['b1'], 'L0_ffn_w2': _L0_ffn_in['w2'], 'L0_ffn_b2': _L0_ffn_in['b2']}

def reference(x, src, dst, edge_weight1, L0_gnn_mW1, L0_gnn_mb1, L0_gnn_ln_g, L0_gnn_ln_b, L0_gnn_mW2, L0_gnn_mb2, L0_gnn_uW1, L0_gnn_ub1, L0_gnn_uW2, L0_gnn_ub2, L0_ffn_router_w, L0_ffn_w1, L0_ffn_b1, L0_ffn_w2, L0_ffn_b2):
    import jax
    import jax.numpy as jnp

    def _L0_gnn_ref(h, e, d2, mW1, mb1, ln_g, ln_b, mW2, mb2, uW1, ub1, uW2, ub2):
        import jax, jax.numpy as jnp
        import numpy as np
        N_NODES = 6250
        DIM_H = 256
        N_EDGES = 100000
        LN_EPS = 1e-05

        def _layer_norm(x, g, b):
            mu = jnp.mean(x, axis=-1, keepdims=True)
            var = jnp.mean(jnp.square(x - mu), axis=-1, keepdims=True)
            return (x - mu) * jax.lax.rsqrt(var + LN_EPS) * g + b
        ei, ej = (e[0], e[1])
        hi = h[ei]
        hj = h[ej]
        x = jnp.concatenate((hi, hj, d2), axis=-1)
        msg = jax.nn.silu(x @ mW1 + mb1)
        msg = _layer_norm(msg, ln_g, ln_b)
        msg = jax.nn.silu(msg @ mW2 + mb2)
        agg = jax.ops.segment_sum(msg, ei, num_segments=h.shape[0])
        y = jnp.concatenate((h, agg), axis=-1)
        y = jax.nn.silu(y @ uW1 + ub1) @ uW2 + ub2
        return h + y

    def _L0_ffn_ref(input_embeddings, router_w, w1, b1, w2, b2):
        import jax, jax.numpy as jnp
        import numpy as np
        NUM_EXPERTS = 8
        TOP_K = 2
        B, S, D = (8, 1024, 256)

        def _moe(tokens, router_w, w1, b1, w2, b2):
            N = tokens.shape[0]
            E = router_w.shape[0]
            logits = tokens.astype(jnp.float32) @ router_w.astype(jnp.float32).T
            probs = jax.nn.softmax(logits, axis=-1)
            rw, re = jax.lax.top_k(probs, TOP_K)
            if TOP_K > 1:
                rw = rw / jnp.maximum(rw.sum(-1, keepdims=True), 1e-12)
            rw = rw.astype(tokens.dtype)
            combine = jnp.zeros((N, E), tokens.dtype).at[jnp.arange(N)[:, None], re].set(rw)
            out = tokens
            for e in range(E):
                h = jax.nn.gelu(tokens @ w1[e] + b1[e], approximate=False)
                y = h @ w2[e] + b2[e]
                out = out + combine[:, e:e + 1] * y
            return out
        b, s, d = input_embeddings.shape
        tokens = input_embeddings.reshape(b * s, d)
        return _moe(tokens, router_w, w1, b1, w2, b2).reshape(b, s, d)
    edge_index = jnp.stack([src, dst])
    x = x + _L0_gnn_ref(_layernorm(x, axis=-1), edge_index, edge_weight1, L0_gnn_mW1, L0_gnn_mb1, L0_gnn_ln_g, L0_gnn_ln_b, L0_gnn_mW2, L0_gnn_mb2, L0_gnn_uW1, L0_gnn_ub1, L0_gnn_uW2, L0_gnn_ub2)
    x = x + _L0_ffn_ref(_layernorm(x, axis=-1)[None], L0_ffn_router_w, L0_ffn_w1, L0_ffn_b1, L0_ffn_w2, L0_ffn_b2)[0]
    return x

_drawn_inputs = setup_inputs


def setup_inputs(seed=0):
    import zlib

    import numpy as np

    out = dict(_drawn_inputs(seed))
    spreads = {'L0_gnn_ln_g': (1.0, 0.2),
     'L0_gnn_ln_b': (0.0, 0.1),
     'L0_ffn_b1': (0.0, 0.49),
     'L0_ffn_b2': (0.0, 0.333)}
    factors = {'edge_weight1': 28.211, 'L0_gnn_ub1': 7.107}
    for name, (base, spread) in spreads.items():
        noise = np.random.default_rng([zlib.crc32(name.encode()), seed]).standard_normal(out[name].shape)
        drawn = base * np.exp(spread * noise) if base else spread * noise
        out[name] = jnp.asarray(drawn.astype(out[name].dtype))
    for name, factor in factors.items():
        out[name] = (out[name] * factor).astype(out[name].dtype)
    return out
```

```python
from contextlib import ExitStack

import numpy as np

import concourse.bass as bass
from concourse import mybir
from concourse.alu_op_type import AluOpType as ALU

f32, bf16, i32 = mybir.dt.float32, mybir.dt.bfloat16, mybir.dt.int32
i16 = mybir.dt.int16
ACT = mybir.ActivationFunctionType
AX = mybir.AxisListType

P = 128
N, D, E, X = 6250, 256, 100000, 8
KC = D // P
NB = 125
BK = N // NB
EC = E // NB
PAIRS = 416
G = 2 * PAIRS
TABK = 7
PADT = 16
EPS = 1e-5
RND = 12582912.0
assert BK * NB == N and EC * NB == E
assert G * P >= E + BK * (P - 1) - P + 1 and P * TABK >= G
SC = 8
NP2 = BK // 2


class Step:

    def __init__(self, it, unroll, c):
        self.it, self.unroll, self.c = it, unroll, c

    def __sub__(self, lag):
        return Step(self.it, self.unroll, self.c - lag)

    def of(self, scale=1, add=0):
        const = scale * self.c + add
        return const if isinstance(self.it, int) else self.it * (scale * self.unroll) + const

    def per(self, d, scale=1, add=0):
        const = scale * (self.c // d) + add
        return const if isinstance(self.it, int) else self.it * (scale * self.unroll // d) + const

    def mod(self, k):
        return self.c % k

    def within(self, n):
        return not isinstance(self.it, int) or 0 <= self.c < n


def pipeline(eng, n, depth, unroll, step, enter=None, peel=1):
    first = max(peel, -(-depth // unroll))
    last = n // unroll
    assert last > first
    for b in range(first):
        if enter:
            enter(b)
        for c in range(unroll):
            step(Step(0, unroll, b * unroll + c))
    with eng.Fori(0, last - first) as it:
        if enter:
            enter(it + first)
        for c in range(unroll):
            step(Step(it, unroll, first * unroll + c))
    for m in range(last * unroll, n + depth):
        if enter and m % unroll == 0:
            enter(m // unroll)
        step(Step(0, unroll, m))


def wait(eng, sem, value):
    if isinstance(value, int) and value <= 0:
        return
    eng.wait_ge(sem, value)


def wait_apart(eng, sem, value, passed):
    wait(eng, sem, value)
    if not isinstance(value, int):
        eng.sem_inc(passed, 1)


def gnn_moe_kernel(nc, x, src, dst, edge_w, mW1, mb1, ln_g, ln_b, mW2, mb2, uW1, ub1, uW2, ub2,
                   router_w, w1, b1, w2, b2, out):
    ctx = ExitStack()
    with ctx:
        def sb(name, shape, dt=f32):
            return ctx.enter_context(nc.sbuf_tensor(name, shape, dt))

        def sem(name):
            return ctx.enter_context(nc.semaphore(name))

        ctx.enter_context(nc.allow_non_contiguous_dma(reason="small vectors laid along partitions"))

        recd = nc.dram_tensor("edge_records", (P * G, 4), f32).ap()
        dstd = nc.dram_tensor("dst_half", (N, D), f32).ap()
        wcd = nc.dram_tensor("edge_weight_column", (3, D), bf16).ap()
        tabd = nc.dram_tensor("tile_blocks", (P, TABK), i32).ap()

        ablk = sb("ablk", [P, 3, BK * D], bf16)
        agg = sb("agg", [P, BK, D])
        rec = sb("rec", [P, G, 4])
        dpart = sb("dpart", [P, G, 3], bf16)
        idx = sb("idx", [P, G], i32)
        work = sb("work", [P, 12800])
        W2c = sb("W2c", [P, KC, D])
        b2c = sb("b2c", [P, D])
        ub2b = sb("ub2b", [P, D])
        mv1 = sb("mv1", [P, BK, 2])
        ident = sb("ident", [P, P])
        iota_n = sb("iota_n", [P, NB])
        tabrow = sb("tabrow", [1, PADT + P * TABK], i32)
        stage_i = sb("stage_i", [P, 2 * SC], i32)
        ps = ctx.enter_context(nc.psum_tensor("ps", [P, 8, 512], f32))

        at = [0]

        def cut(floats, shape=None, dt=f32, restart=False, **dims):
            if restart:
                at[0] = 0
            a = work[:, at[0]:at[0] + floats]
            at[0] += floats
            assert at[0] <= 12800
            a = a if dt == f32 else a.bitcast(dt)
            return a.rearrange(shape, **dims) if shape else a

        srci = cut(EC, dt=i32, restart=True)
        dsti = cut(EC, dt=i32)
        dwt = cut(EC)
        srcf = cut(EC)
        blkf = cut(EC)
        blkh = cut(EC // 2, dt=bf16)
        ones = cut(EC // 2, dt=bf16)
        mask = [cut(EC // 2, dt=bf16) for _ in range(2)]
        rank = [cut(EC) for _ in range(2)]
        pos = cut(EC)
        posi = cut(EC, dt=i32)
        lowi = cut(EC, dt=i32)
        cnt = cut(BK)
        iota_b = cut(BK + 1)
        tri = cut(P)
        onesf = cut(P)
        ntile = cut(BK)
        ntilei = cut(BK, dt=i32)
        start = cut(BK)
        base = cut(BK + 1)
        gidx = cut(TABK)
        cmp = cut(TABK * BK, "p (k b) -> p k b", k=TABK)
        tblk = cut(TABK)
        tblki = cut(TABK, dt=i32)
        W1ab = cut(KC * 2 * D, "p (k n) -> p k n", k=KC)
        mb1b = cut(D)
        lng = cut(KC)
        lnb = cut(KC)
        w1c = cut(D)
        wcp = cut(3 * D // 2, "p (k n) -> p k n", dt=bf16, k=3)
        stage = srci.bitcast(f32)[:, 0:2 * SC * 4].rearrange("p (h c f) -> p h c f", h=2, f=4)
        hn = [blkf[:, 0:D], blkf[:, D:2 * D]]
        hnT = [rank[0][:, 0:KC * NB].rearrange("p (k n) -> p k n", k=KC),
               rank[1][:, 0:KC * NB].rearrange("p (k n) -> p k n", k=KC)]
        bout = [pos[:, 0:D], pos[:, D:2 * D]]
        atmp = [lowi.bitcast(f32)[:, 0:D], lowi.bitcast(f32)[:, D:2 * D]]
        W2raw = dwt
        W2g = srcf[:, 0:KC * D].rearrange("p (k n) -> p k n", k=KC)
        lnbb = posi.bitcast(f32)[:, 0:KC * P].rearrange("p (k n) -> p k n", k=KC)
        bns = cmp
        recE = rec[0:NB].rearrange("p g f -> p (g f)")[:, 0:EC * 4].rearrange("p (c f) -> p c f", f=4)

        passed_pool = sem("passed_pool")
        passed_dve = sem("passed_dve")
        edges_in = sem("edges_in")
        x_in = sem("x_in")
        w_in = sem("w_in")
        w2_in = sem("w2_in")
        consts = sem("consts")
        pads_set = sem("pads_set")
        pads_out = sem("pads_out")
        rk = sem("rank_chain")
        cnt_ready = sem("cnt_ready")
        pre_ready = sem("pre_ready")
        blk_ready = sem("blk_ready")
        blk_out = sem("blk_out")
        blk_in = sem("blk_in")
        recs_ready = sem("recs_ready")
        staged = sem("staged")
        scat = [sem("scattered0"), sem("scattered1")]
        scat_done = sem("scat_done")
        rec_in = sem("rec_in")
        var_ready = sem("var_ready")
        std_ready = sem("std_ready")
        nd = sem("node_chain")
        wcol_ready = sem("wcol_ready")
        wcol_out = sem("wcol_out")
        wcol_in = sem("wcol_in")
        w2g_ready = sem("w2g_ready")
        w2m_ready = sem("w2m_ready")
        hn_ready = sem("hn_ready")
        hn_tr = sem("hn_tr")
        hnT_ready = sem("hnT_ready")
        ab_ready = sem("ab_ready")
        b_copied = sem("b_copied")
        a_taken = sem("a_taken")
        b_stored = [sem("b_stored0"), sem("b_stored1")]

        with nc.Block() as block:
            @block.sync
            def _(sp):
                sp.dma_start(srci[0:NB], src.rearrange("(p c) -> p c", p=NB)).then_inc(edges_in, 16)
                sp.dma_start(dsti[0:NB], dst.rearrange("(p c) -> p c", p=NB)).then_inc(edges_in, 16)
                sp.dma_start(dwt[0:NB], edge_w.rearrange("(p c) o -> p (c o)", p=NB)).then_inc(edges_in, 16)
                xv = x.rearrange("(t p) f -> p t f", p=NB)
                for t in range(0, BK, 10):
                    sp.dma_start(agg[0:NB, t:t + 10, :], xv[:, t:t + 10, :]).then_inc(x_in, 16)
                for h in range(2):
                    sp.dma_start(W1ab[:, :, h * D:(h + 1) * D],
                                 mW1[h * D:(h + 1) * D, :].rearrange("(k p) n -> p k n", p=P)).then_inc(w_in, 16)
                sp.dma_start(mb1b, mb1.partition_broadcast(P)).then_inc(w_in, 16)
                sp.dma_start(b2c[:, :], mb2.partition_broadcast(P)).then_inc(w_in, 16)
                sp.dma_start(ub2b[:, :], ub2.partition_broadcast(P)).then_inc(w_in, 16)
                sp.dma_start(lng, ln_g.rearrange("(k p) -> p k", p=P)).then_inc(w_in, 16)
                sp.dma_start(lnb, ln_b.rearrange("(k p) -> p k", p=P)).then_inc(w_in, 16)
                sp.dma_start(w1c[0:1], mW1[2 * D:2 * D + 1, :]).then_inc(w_in, 16)
                sp.wait_ge(pads_set, 3)
                sp.dma_start(recd.rearrange("(p g) f -> p (g f)", p=P),
                             rec[:, :, :].rearrange("p g f -> p (g f)")).then_inc(pads_out, 16)
                sp.wait_ge(blk_ready, 1)
                sp.dma_start(tabd, tblki).then_inc(blk_out, 16)
                sp.wait_ge(blk_out, 16)
                sp.dma_start(tabrow[0:1, PADT:PADT + P * TABK],
                             tabd.rearrange("p k -> (p k)").rearrange("(a n) -> a n", a=1)).then_inc(blk_in, 16)
                sp.wait_ge(recs_ready, 1)
                sp.dma_start(W2raw[:, 0:KC * D].rearrange("p (k n) -> p k n", k=KC),
                             mW2.rearrange("(k p) n -> p k n", p=P)).then_inc(w2_in, 16)
                sp.wait_ge(wcol_ready, 1)
                sp.dma_start(wcd.rearrange("k n -> (k n)").rearrange("(a n) -> a n", a=1),
                             wcp[0:1].rearrange("p k n -> p (k n)")).then_inc(wcol_out, 16)
                sp.wait_ge(wcol_out, 16)
                for k in range(3):
                    row = wcd[k, :].partition_broadcast(BK).partition_broadcast(P - NB)
                    sp.dma_start(ablk[NB:P, k, :].rearrange("p (b n) -> p b n", b=BK), row).then_inc(wcol_in, 16)

                def step(m):
                    sp.wait_ge(b_copied, m.of(1, 1))
                    rows = m.of(NB)
                    sp.dma_start(dstd[bass.ds(rows, NB), :], bout[m.mod(2)][0:NB]).then_inc(b_stored[m.mod(2)], 16)
                with sp.Fori(0, BK // 2) as it:
                    for c in range(2):
                        step(Step(it, 2, c))
                for h in range(2):
                    sp.wait_ge(b_stored[h], 16 * (BK // 2))
                sp.wait_ge(wcol_in, 48)
                sp.wait_ge(blk_in, 16)
                sp.wait_ge(scat_done, 1)
                sp.dma_start(rec[:, :, :].rearrange("p g f -> p (g f)"),
                             recd.rearrange("(p g) f -> p (g f)", p=P)).then_inc(rec_in, 16)
                sp.wait_ge(rec_in, 16)

            @block.gpsimd
            def _(pool):
                nc.gpsimd.memset(rec[:, :, :], 0.0).then_inc(pads_set, 1)
                nc.gpsimd.memset(tabrow[:, 0:PADT], 0).then_inc(pads_set, 1)
                pool.wait_ge(pads_set, 2)
                nc.gpsimd.memset(rec[:, :, 0:1], -1.0).then_inc(pads_set, 1)
                nc.gpsimd.memset(ident[:, :], 0.0).then_inc(consts, 1)
                nc.gpsimd.memset(onesf, 1.0).then_inc(consts, 1)
                nc.gpsimd.memset(ones, 1.0).then_inc(consts, 1)
                nc.gpsimd.iota(iota_n[:, :], pattern=[[1, NB]], base=0, channel_multiplier=0,
                               allow_small_or_imprecise_dtypes=True).then_inc(consts, 1)
                nc.gpsimd.iota(iota_b, pattern=[[1, BK + 1]], base=0, channel_multiplier=0,
                               allow_small_or_imprecise_dtypes=True).then_inc(consts, 1)
                nc.gpsimd.iota(gidx, pattern=[[1, TABK]], base=0, channel_multiplier=TABK,
                               allow_small_or_imprecise_dtypes=True).then_inc(consts, 1)
                pool.wait_ge(consts, 6)
                nc.gpsimd.affine_select(out=ident[:, :], in_=ident[:, :], compare_op=ALU.not_equal, fill=1.0,
                                        base=0, pattern=[[-1, P]], channel_multiplier=1).then_inc(consts, 1)
                nc.gpsimd.affine_select(out=tri, in_=onesf, compare_op=ALU.is_gt, fill=0.0,
                                        base=0, pattern=[[1, P]], channel_multiplier=-1).then_inc(consts, 1)
                pool.wait_ge(recs_ready, 1)

                def step(m):
                    h = m.mod(2)
                    wait(pool, scat[h], m.per(2, 16 * SC, 0))
                    cols = bass.ds(m.of(SC), SC)
                    nc.gpsimd.tensor_copy(stage[0:NB, h], recE[:, cols, :]).then_inc(staged, 1)
                    nc.gpsimd.tensor_copy(stage_i[0:NB, h * SC:(h + 1) * SC], recE[:, cols, 3]).then_inc(staged, 1)
                    wait_apart(pool, staged, m.of(2, 2), passed_pool)
                    for c in range(SC):
                        pool.indirect_dma_start(
                            recd, bass.IndirectOffsetOnAxis(ap=stage_i[0:NB, h * SC + c:h * SC + c + 1], axis=0),
                            stage[0:NB, h, c, :], None).then_inc(scat[h], 16)
                pipeline(pool, EC // SC, 0, 2, step)
                for h in range(2):
                    pool.wait_ge(scat[h], 16 * EC // 2)
                pool.sem_inc(scat_done, 1)

            @block.vector
            def _(dve):
                done = [0]

                def link(ins):
                    done[0] += 1
                    ins.then_inc(rk, 1)
                    dve.wait_ge(rk, done[0])

                v = nc.vector
                e = slice(0, NB)
                dve.wait_ge(edges_in, 48)
                link(v.tensor_copy(srcf[e], srci[e]))
                link(v.tensor_scalar(blkf[e], srcf[e], -float(NB // 2), 1.0 / NB, ALU.add, ALU.mult))
                link(v.tensor_scalar(blkf[e], blkf[e], RND, None, ALU.add))
                link(v.tensor_scalar(blkf[e], blkf[e], RND, None, ALU.subtract))
                link(v.tensor_copy(blkh[e], blkf[e]))
                dve.wait_ge(pads_out, 16)
                link(v.scalar_tensor_tensor(out=recE[:, :, 0], in0=blkf[e], scalar=-float(NB), in1=srcf[e],
                                            op0=ALU.mult, op1=ALU.add))
                link(v.tensor_copy(recE[:, :, 1], dsti[e]))
                link(v.tensor_copy(recE[:, :, 2], dwt[e]))
                link(v.memset(pos[e], 0.0))
                dve.wait_ge(consts, 8)
                v.memset(base[e, BK:BK + 1], 0.0).then_inc(cnt_ready, 1)
                with dve.Fori(0, BK // 2) as it:
                    for c in range(2):
                        v.tensor_scalar(mask[c][e], blkh[e], iota_b[e, bass.ds(it * 2 + c, 1)], 0.0, ALU.is_equal, ALU.add,
                                        accum_out=cnt[e, bass.ds(it * 2 + c, 1)]).then_inc(cnt_ready, 1)
                        dve.wait_ge(cnt_ready, it * 2 + c + 1)
                dve.wait_ge(pre_ready, 2)
                link(v.tensor_scalar(ntilei, ps[:, 1, 0:BK], float(P - 1), None, ALU.add))
                link(v.tensor_scalar(ntilei, ntilei, 7, None, ALU.arith_shift_right))
                link(v.tensor_copy(ntile, ntilei))
                link(v.tensor_tensor_scan(start, ones[:, 0:BK], ntile, 0.0, ALU.mult, ALU.add))
                link(v.tensor_tensor(start, start, ntile, ALU.subtract))
                link(v.tensor_scalar(base[e, 0:BK], start[e], float(P), -1.0, ALU.mult, ALU.add))
                link(v.tensor_tensor(base[e, 0:BK], base[e, 0:BK], ps[e, 0, 0:BK], ALU.add))
                link(v.tensor_tensor(cmp, start.unsqueeze(1).to_broadcast([P, TABK, BK]),
                                     gidx.unsqueeze(2).to_broadcast([P, TABK, BK]), ALU.is_le))
                link(v.tensor_reduce(out=tblk, in_=cmp, axis=AX.X, op=ALU.add))
                v.tensor_scalar(tblki, tblk, -1.0, float(D), ALU.add, ALU.mult).then_inc(blk_ready, 1)

                def match(b, c):
                    return v.tensor_scalar(mask[c][e], blkh[e], iota_b[e, b], None, ALU.is_equal)

                def count(b, c):
                    return v.tensor_tensor_scan(rank[c][e], ones[e], mask[c][e], base[e, b], ALU.mult, ALU.add)

                link(match(bass.ds(0, 1), 0))
                link(count(bass.ds(0, 1), 0))
                before = done[0]
                with dve.Fori(0, BK // 2) as it:
                    for c in range(2):
                        nxt = bass.ds(it * 2 + c + 1, 1)
                        match(nxt, 1 - c).then_inc(rk, 1)
                        v.copy_predicated(pos[e], mask[c][e].bitcast(i16), rank[c][e]).then_inc(rk, 1)
                        dve.wait_ge(rk, it * 6 + before + 3 * c + 1)
                        count(nxt, 1 - c).then_inc(rk, 1)
                        wait_apart(dve, rk, it * 6 + before + 3 * c + 3, passed_dve)
                done[0] += 3 * BK
                link(v.tensor_copy(posi[e], pos[e]))
                link(v.tensor_scalar(lowi[e], posi[e], P - 1, None, ALU.bitwise_and))
                link(v.tensor_scalar(posi[e], posi[e], 7, None, ALU.arith_shift_right))
                v.scalar_tensor_tensor(out=recE[:, :, 3], in0=lowi[e], scalar=float(G), in1=posi[e],
                                       op0=ALU.mult, op1=ALU.add).then_inc(recs_ready, 1)

                dve.wait_ge(x_in, 80)
                stats = rank[0][:, 0:12].rearrange("p (h s) -> p h s", h=2)
                pair = rank[0][:, 12:16].rearrange("p (h s) -> p h s", h=2)
                before = done[0]
                with dve.Fori(0, BK // 2) as it:
                    for h in range(2):
                        v.bn_stats(stats[e, h], agg[e, bass.ds(it * 2 + h, 1), :].rearrange("p t f -> p (t f)")).then_inc(rk, 1)
                    wait_apart(dve, rk, it * 5 + before + 2, passed_dve)
                    for h in range(2):
                        v.bn_aggr(pair[e, h], stats[e, h]).then_inc(rk, 1)
                    dve.wait_ge(rk, it * 5 + before + 4)
                    v.tensor_copy(mv1[e, bass.ds(it * 2, 2), :], pair[e]).then_inc(rk, 1)
                    dve.wait_ge(rk, it * 5 + before + 5)
                done[0] += 5 * (BK // 2)
                v.tensor_scalar(mv1[e, :, 1], mv1[e, :, 1], EPS, None, ALU.add).then_inc(var_ready, 1)
                dve.wait_ge(w_in, 16 * 8)
                o = slice(0, 1)
                link(v.tensor_copy(wcp[o, 0], w1c[o]))
                link(v.tensor_tensor(w1c[o], w1c[o], wcp[o, 0], ALU.subtract))
                link(v.tensor_copy(wcp[o, 1], w1c[o]))
                link(v.tensor_tensor(w1c[o], w1c[o], wcp[o, 1], ALU.subtract))
                v.tensor_copy(wcp[o, 2], w1c[o]).then_inc(wcol_ready, 1)
                dve.wait_ge(w2_in, 16)
                for k in range(KC):
                    v.tensor_scalar(W2g[:, k], W2raw[:, k * D:(k + 1) * D], lng[:, k:k + 1], None,
                                    ALU.mult).then_inc(w2g_ready, 1)
                    v.tensor_scalar(lnbb[:, k], onesf, lnb[:, k:k + 1], None, ALU.mult).then_inc(w2g_ready, 1)
                dve.wait_ge(w2m_ready, 1)
                for k in range(KC):
                    v.scalar_tensor_tensor(out=W2c[:, k], in0=ps[:, 0, 0:D], scalar=-1.0 / D, in1=W2g[:, k],
                                           op0=ALU.mult, op1=ALU.add)
                link(v.tensor_tensor(b2c[:, :], b2c[:, :], ps[:, 1, 0:D], ALU.add))
                dve.wait_ge(std_ready, 1)
                link(v.reciprocal(mv1[e, :, 1], mv1[e, :, 1]))

                def step(m):
                    if m.within(BK):
                        s = m.mod(2)
                        wait(dve, hn_tr, m.of(1, -1))
                        t = bass.ds(m.of(), 1)
                        v.tensor_scalar(hn[s][e], agg[e, t, :].rearrange("p t f -> p (t f)"),
                                        mv1[e, t, 0], mv1[e, t, 1], ALU.subtract, ALU.mult).then_inc(hn_ready, 1)
                    a = m - 1
                    if a.within(BK):
                        s = a.mod(2)
                        dve.wait_ge(ab_ready, a.of(1, 1))
                        t = bass.ds(a.of(D), D)
                        tmp = atmp[s][e]
                        v.tensor_tensor(tmp, ps[e, 2 + s, 0:D], mb1b[e], ALU.add).then_inc(a_taken, 1)
                        dve.wait_ge(a_taken, a.of(1, 1))
                        for k in range(2):
                            v.tensor_copy(ablk[e, k, t], tmp).then_inc(nd, 1)
                            dve.wait_ge(nd, a.of(5, 2 * k + 1))
                            v.tensor_tensor(tmp, tmp, ablk[e, k, t], ALU.subtract).then_inc(nd, 1)
                            dve.wait_ge(nd, a.of(5, 2 * k + 2))
                        v.tensor_copy(ablk[e, 2, t], tmp).then_inc(nd, 1)

                pipeline(dve, BK, 1, 2, step)

            @block.scalar
            def _(act):
                act.wait_ge(var_ready, 1)
                nc.scalar.activation(mv1[0:NB, :, 1], mv1[0:NB, :, 1], ACT.Sqrt).then_inc(std_ready, 1)

                def step(m):
                    s = m.mod(2)
                    if m.within(BK):
                        act.wait_ge(hn_tr, m.of(1, 1))
                        wait(act, ab_ready, m.of(1, -1))
                        nc.scalar.activation(hnT[s], ps[:, 4 + s, 0:KC * NB].rearrange("p (k n) -> p k n", k=KC),
                                             ACT.Copy).then_inc(hnT_ready, 1)
                    b = m - 1
                    if b.within(BK):
                        act.wait_ge(a_taken, b.of(1, 1))
                        wait(act, b_stored[b.mod(2)], b.per(2, 16, 0))
                        nc.scalar.activation(bout[b.mod(2)][0:NB], ps[0:NB, 2 + b.mod(2), D:2 * D],
                                             ACT.Copy).then_inc(b_copied, 1)

                pipeline(act, BK, 1, 2, step)

            @block.tensor
            def _(pe):
                pe.wait_ge(cnt_ready, BK + 1)
                nc.tensor.matmul(ps[:, 0, 0:BK], tri[0:NB, :], cnt[0:NB], start=True, stop=True).then_inc(pre_ready, 1)
                nc.tensor.matmul(ps[:, 1, 0:BK], onesf[0:NB], cnt[0:NB], start=True, stop=True).then_inc(pre_ready, 1)
                pe.wait_ge(w2g_ready, 2 * KC)
                for k in range(KC):
                    nc.tensor.matmul(ps[:, 0, 0:D], onesf, W2g[:, k], start=(k == 0), stop=(k == KC - 1))
                for k in range(KC):
                    last = nc.tensor.matmul(ps[:, 1, 0:D], lnbb[:, k], W2raw[:, k * D:(k + 1) * D],
                                            start=(k == 0), stop=(k == KC - 1))
                last.then_inc(w2m_ready, 1)

                def step(m):
                    if m.within(BK):
                        s = m.mod(2)
                        pe.wait_ge(hn_ready, m.of(1, 1))
                        wait(pe, hnT_ready, m.of(1, -1))
                        for k in range(KC):
                            last = nc.tensor.transpose(ps[:, 4 + s, k * NB:(k + 1) * NB],
                                                       hn[s][0:NB, k * P:(k + 1) * P], ident[0:NB, 0:NB])
                        last.then_inc(hn_tr, 1)
                    a = m - 1
                    if a.within(BK):
                        s = a.mod(2)
                        pe.wait_ge(hnT_ready, a.of(1, 1))
                        wait(pe, a_taken, a.of(1, -1))
                        wait(pe, b_copied, a.of(1, -1))
                        for k in range(KC):
                            last = nc.tensor.matmul(ps[0:NB, 2 + s, :], hnT[s][:, k, :], W1ab[:, k, :],
                                                    start=(k == 0), stop=(k == KC - 1))
                        last.then_inc(ab_ready, 1)

                pipeline(pe, BK, 1, 2, step)

        RE, RB, RT = 8, 8, 4
        eh = cut(RE * 2 * P, "p (r u n) -> p r u n", restart=True, r=RE, u=2)
        bg = cut(RB * 2 * D, "p (r u n) -> p r u n", r=RB, u=2)
        sa = cut(RT * 2 * D, "p (r u n) -> p r u n", r=RT, u=2)
        sT = cut(RT * 2 * D, "p (r u k n) -> p r u k n", r=RT, u=2, k=KC)
        zb = cut(2 * D, "p (u n) -> p u n", u=2)
        junk = cut(D)
        msg = cut(2 * 2 * D, "p (r u n) -> p r u n", r=2, u=2)
        ohT = cut(2 * P, "p (r u n) -> p r u n", dt=bf16, r=2, u=2)
        ssum = cut(RE * 2, "p (r u) -> p r u", r=RE)
        ssq = cut(RE * 2, "p (r u) -> p r u", r=RE)
        rstd = cut(RE * 2, "p (r u) -> p r u", r=RE)
        mean = cut(4, "p (r u) -> p r u", r=2)
        var = cut(4, "p (r u) -> p r u", r=2)
        half = cut(4, "p (r u) -> p r u", r=2)
        dres = agg[:, 0:4, :].rearrange("p t f -> p (t f)")[:, 0:G]

        LT, LA, LS, LM, LZ, LG = 1, 2, 3, 5, 6, 7
        split = sem("split_chain")
        slots_ready = sem("slots_ready")
        agg_zero = sem("agg_zero")
        oh_ready = sem("oh_ready")
        oh_tr = sem("oh_tr")
        ohT_ready = sem("ohT_ready")
        pre_ps = sem("pre_ps")
        pre_sb = sem("pre_sb")
        idx_st = sem("idx_staged")
        gath = [sem(f"gathered{r}") for r in range(RB)]
        s_ready = sem("s_ready")
        s_tr = sem("s_tr")
        sT_ready = sem("sT_ready")
        sq_done = sem("squares_done")
        half_ready = sem("half_ready")
        nrm = sem("norm_chain")
        rstd_ready = sem("rstd_ready")
        z_ps = sem("z_ps")
        z_sb = sem("z_sb")
        msg_ready = sem("msg_ready")
        agg_ps = sem("agg_ps")
        agg_add = sem("agg_add")

        with nc.Block() as block:
            @block.gpsimd
            def _(pool):
                nc.gpsimd.memset(half[:, :, :], -0.5).then_inc(half_ready, 1)
                pool.wait_ge(half_ready, 1)
                pool.wait_ge(slots_ready, 1)

                def stage_idx(m):
                    h = (m.mod(RB)) // 4
                    if not isinstance(m.it, int) or m.c >= RB:
                        for r in range(4 * h, 4 * h + 4):
                            pool.wait_ge(gath[r], m.per(RB, 32, 0))
                    nc.gpsimd.tensor_copy(stage_i[:, h * 8:h * 8 + 8], idx[:, bass.ds(m.of(2), 8)]).then_inc(idx_st, 1)
                    wait_apart(pool, idx_st, m.per(4, 1, 1), passed_pool)

                def gather(m):
                    r = m.mod(RB)
                    wait_apart(pool, s_ready, m.of(2, 2 - 2 * RB), passed_pool)
                    for u in range(2):
                        c = (r * 2 + u)
                        pool.indirect_dma_start(bg[:, r, u, :], None, dstd,
                                                bass.IndirectOffsetOnAxis(ap=stage_i[:, c:c + 1], axis=0)).then_inc(gath[r], 16)

                def norm(m):
                    r = m.mod(RE)
                    pool.wait_ge(sq_done, m.of(2, 4))
                    wait(pool, z_sb, m.of(1, 2 - RE))
                    wait_apart(pool, rstd_ready, m.per(2, 1, 0), passed_pool)
                    nc.gpsimd.tensor_scalar(mean[:, :, :], ssum[:, r:r + 2, :], 1.0 / D, None, ALU.mult).then_inc(nrm, 1)
                    nc.gpsimd.tensor_scalar(var[:, :, :], ssq[:, r:r + 2, :], 1.0 / D, None, ALU.mult).then_inc(nrm, 1)
                    pool.wait_ge(nrm, m.per(2, 5, 2))
                    nc.gpsimd.tensor_tensor(mean[:, :, :], mean[:, :, :], mean[:, :, :], ALU.mult).then_inc(nrm, 1)
                    pool.wait_ge(nrm, m.per(2, 5, 3))
                    nc.gpsimd.tensor_tensor(var[:, :, :], var[:, :, :], mean[:, :, :], ALU.subtract).then_inc(nrm, 1)
                    wait_apart(pool, nrm, m.per(2, 5, 4), passed_pool)
                    nc.gpsimd.tensor_scalar(var[:, :, :], var[:, :, :], 0.0, EPS, ALU.max, ALU.add).then_inc(nrm, 1)
                    pool.wait_ge(nrm, m.per(2, 5, 5))
                    nc.gpsimd.tensor_tensor(rstd[:, r:r + 2, :], var[:, :, :], half[:, :, :], ALU.pow).then_inc(rstd_ready, 1)

                AHEAD = 5

                def step(m):
                    if m.within(PAIRS):
                        if m.mod(4) == 0:
                            stage_idx(m)
                        gather(m)
                    q = m - AHEAD
                    if q.within(PAIRS) and q.mod(2) == 0:
                        norm(q)

                pipeline(pool, PAIRS, AHEAD, RE, step, peel=2)

            @block.vector
            def _(dve):
                v = nc.vector
                done = [0]

                def link(ins):
                    done[0] += 1
                    ins.then_inc(split, 1)
                    dve.wait_ge(split, done[0])

                v.tensor_copy(idx[:, :], rec[:, :, 1]).then_inc(slots_ready, 1)
                link(v.tensor_copy(dpart[:, :, 0], rec[:, :, 2]))
                link(v.tensor_tensor(dres, rec[:, :, 2], dpart[:, :, 0], ALU.subtract))
                link(v.tensor_copy(dpart[:, :, 1], dres))
                link(v.tensor_tensor(dres, dres, dpart[:, :, 1], ALU.subtract))
                link(v.tensor_copy(dpart[:, :, 2], dres))
                link(v.memset(agg[:, :, :], 0.0))
                regs = [v.alloc_register(f"block_of_tile{j}") for j in range(16)]
                offs = [None] * 16

                def enter(it):
                    if isinstance(it, int) and it == 0:
                        return
                    v.load(regs, tabrow[0:1, bass.ds(it * 16 + PADT - 16, 16)])
                    offs[:] = [v.snap(r, min_val=0, max_val=(BK - 1) * D) for r in regs]

                aggf = agg[:, :, :].rearrange("p t f -> p (t f)")

                def add_sums(a, u):
                    wait(dve, agg_add, a.of(2, u))
                    d = aggf[0:NB, bass.ds(offs[2 * a.mod(RE) + u], D)]
                    v.tensor_tensor(d, d, ps[0:NB, 7, u * D:(u + 1) * D], ALU.add).then_inc(agg_add, 1)

                def step(m):
                    g, z, b = m - RE, m - LZ, m - LA
                    if g.within(PAIRS):
                        dve.wait_ge(agg_ps, g.of(1, 1))
                        add_sums(g, 0)
                    if m.within(PAIRS):
                        r = m.mod(RE)
                        wait(dve, agg_ps, m.of(1, 1 - RE))
                        t = bass.ds(m.of(2), 2)
                        v.tensor_tensor(eh[:, r, :, 0:NB], iota_n[:, :].unsqueeze(1).to_broadcast([P, 2, NB]),
                                        rec[:, t, 0:1].to_broadcast([P, 2, NB]), ALU.is_equal)
                        v.tensor_copy(eh[:, r, :, NB:P], dpart[:, t, :]).then_inc(oh_ready, 1)
                    if g.within(PAIRS):
                        add_sums(g, 1)
                    if z.within(PAIRS):
                        s = z.mod(2)
                        dve.wait_ge(z_ps, z.of(1, 1))
                        dve.wait_ge(rstd_ready, z.per(2, 1, 1))
                        wait(dve, msg_ready, z.of(1, 0))
                        for u in range(2):
                            last = v.scalar_tensor_tensor(out=zb[:, u], in0=ps[:, 5 + s, u * D:(u + 1) * D],
                                                          scalar=rstd[:, z.mod(RE), u:u + 1], in1=b2c[:, :],
                                                          op0=ALU.mult, op1=ALU.add)
                        last.then_inc(z_sb, 1)
                    if b.within(PAIRS):
                        r, s = b.mod(RB), b.mod(2)
                        dve.wait_ge(pre_ps, b.of(1, 1))
                        dve.wait_ge(gath[r], b.per(RB, 32, 32))
                        v.tensor_tensor(bg[:, r].rearrange("p u n -> p (u n)"), ps[:, 1 + s, :],
                                        bg[:, r].rearrange("p u n -> p (u n)"), ALU.add).then_inc(pre_sb, 1)

                pipeline(dve, PAIRS, RE, RE, step, enter, peel=2)

            @block.scalar
            def _(act):
                def step(m):
                    a = m - LT
                    if a.within(PAIRS):
                        act.wait_ge(oh_tr, a.of(1, 1))
                        wait(act, pre_ps, a.of(1, -1))
                        nc.scalar.activation(ohT[:, a.mod(2)], ps[:, 0, 0:D].rearrange("p (u n) -> p u n", u=2),
                                             ACT.Copy).then_inc(ohT_ready, 1)
                    a = m - LZ
                    if a.within(PAIRS):
                        act.wait_ge(z_sb, a.of(1, 1))
                        wait(act, agg_ps, a.of(1, -1))
                        nc.scalar.activation(msg[:, a.mod(2)], zb[:, :, :], ACT.Silu).then_inc(msg_ready, 1)
                    a = m - LS
                    if a.within(PAIRS):
                        act.wait_ge(s_ready, a.of(2, 2))
                        for u in range(2):
                            wait(act, sq_done, a.of(2, u))
                            nc.scalar.activation(junk, sa[:, a.mod(RT), u], ACT.Square,
                                                 accum_out=ssq[:, a.mod(RE), u:u + 1]).then_inc(sq_done, 1)
                        act.wait_ge(s_tr, a.of(1, 1))
                        wait(act, z_ps, a.of(1, 1 - RT))
                        nc.scalar.activation(sT[:, a.mod(RT)].rearrange("p u k n -> p (u k n)"), ps[:, 3 + a.mod(2), :],
                                             ACT.Copy).then_inc(sT_ready, 1)
                    a = m - LA
                    if a.within(PAIRS):
                        act.wait_ge(pre_sb, a.of(1, 1))
                        wait(act, s_tr, a.of(1, 1 - RT))
                        wait(act, sq_done, a.of(2, 2 - 2 * RT))
                        wait(act, rstd_ready, a.per(2, 1, 1 - RE // 2))
                        for u in range(2):
                            nc.scalar.activation(sa[:, a.mod(RT), u], bg[:, a.mod(RB), u], ACT.Silu,
                                                 accum_out=ssum[:, a.mod(RE), u:u + 1]).then_inc(s_ready, 1)

                pipeline(act, PAIRS, RE, RE, step, peel=2)

            @block.tensor
            def _(pe):
                t_ = nc.tensor
                regs = [t_.alloc_register(f"block_of_tile{j}") for j in range(16)]
                offs = [None] * 16

                def enter(it):
                    t_.load(regs, tabrow[0:1, bass.ds(it * 16 + PADT - 2 * LA, 16)])
                    offs[:] = [t_.snap(r, min_val=0, max_val=(BK - 1) * D) for r in regs]

                def step(m):
                    a = m - LT
                    if a.within(PAIRS):
                        s = a.mod(2)
                        pe.wait_ge(oh_ready, a.of(1, 1))
                        wait(pe, ohT_ready, a.of(1, 0))
                        for u in range(2):
                            last = t_.transpose(ps[:, 0, u * P:(u + 1) * P], eh[:, a.mod(RE), u], ident[:, :])
                        last.then_inc(oh_tr, 1)
                    a = m - LA
                    if a.within(PAIRS):
                        s = a.mod(2)
                        pe.wait_ge(ohT_ready, a.of(1, 1))
                        wait(pe, pre_sb, a.of(1, -1))
                        for u in range(2):
                            o = offs[(2 * (a.mod(RE) + LA) + u) % 16]
                            for k in range(3):
                                last = t_.matmul(ps[:, 1 + s, u * D:(u + 1) * D], ohT[:, s, u], ablk[:, k, bass.ds(o, D)],
                                                 start=(k == 0), stop=(k == 2))
                        last.then_inc(pre_ps, 1)
                    a = m - LS
                    if a.within(PAIRS):
                        s = a.mod(2)
                        pe.wait_ge(s_ready, a.of(2, 2))
                        wait(pe, sT_ready, a.of(1, -1))
                        for u in range(2):
                            for k in range(KC):
                                c = (u * KC + k) * P
                                last = t_.transpose(ps[:, 3 + s, c:c + P], sa[:, a.mod(RT), u, k * P:(k + 1) * P], ident[:, :])
                        last.then_inc(s_tr, 1)
                    a = m - LM
                    if a.within(PAIRS):
                        s = a.mod(2)
                        pe.wait_ge(sT_ready, a.of(1, 1))
                        wait(pe, z_sb, a.of(1, -1))
                        for u in range(2):
                            for k in range(KC):
                                last = t_.matmul(ps[:, 5 + s, u * D:(u + 1) * D], sT[:, a.mod(RT), u, k], W2c[:, k],
                                                 start=(k == 0), stop=(k == KC - 1))
                        last.then_inc(z_ps, 1)
                    a = m - LG
                    if a.within(PAIRS):
                        pe.wait_ge(msg_ready, a.of(1, 1))
                        wait(pe, agg_add, a.of(2, 0))
                        for u in range(2):
                            last = t_.matmul(ps[0:NB, 7, u * D:(u + 1) * D], eh[:, a.mod(RE), u, 0:NB], msg[:, a.mod(2), u],
                                             start=True, stop=True)
                        last.then_inc(agg_ps, 1)

                pipeline(pe, PAIRS, RE, RE, step, enter)

        wts = ablk[:, :, :].rearrange("p k n -> p (k n)").bitcast(f32)
        wat = [0]

        def wcut(floats, shape=None, **dims):
            a = wts[:, wat[0]:wat[0] + floats]
            wat[0] += floats
            assert wat[0] <= 3 * BK * D // 2
            return a.rearrange(shape, **dims) if shape else a

        uW1s = wcut(2 * KC * D, "p (k n) -> p k n", k=2 * KC)
        uW2s = wcut(KC * D, "p (k n) -> p k n", k=KC)
        w1s = wcut(X * KC * D, "p (e k n) -> p e k n", e=X, k=KC)
        w2s = wcut(X * KC * D, "p (e k n) -> p e k n", e=X, k=KC)
        rws = wcut(KC * X, "p (k e) -> p k e", k=KC)
        rwr = wcut(D)
        b2s = wcut(D)
        b1T = wcut(X * KC, "p (e k) -> p e k", e=X)
        ub1T = wcut(KC)
        lg = wcut(BK * X, "p (t e) -> p t e", t=BK)
        pr = wcut(BK * X, "p (t e) -> p t e", t=BK)
        oh1 = wcut(BK * X, "p (t e) -> p t e", t=BK)
        oh2 = wcut(BK * X, "p (t e) -> p t e", t=BK)
        cand = wcut(BK * X, "p (t e) -> p t e", t=BK)
        comb = wcut(BK * X, "p (t e) -> p t e", t=BK)
        iox = wcut(X)
        m1 = wcut(BK)
        m2 = wcut(BK)
        isel = wcut(BK)
        rsum = wcut(BK)
        mv3 = wcut(BK * 2, "p (t s) -> p t s", t=BK)

        def two(shape="p (u n) -> p u n", floats=2 * D, **dims):
            return [cut(floats, shape, **dims) for _ in range(2)]

        cut(0, restart=True)
        xp = two(u=2)
        hp = two(u=2)
        xh = two(u=2)
        catT = two("p (k n) -> p k n", 2 * KC * 2 * NB, k=2 * KC)
        y1T = two("p (k n) -> p k n", KC * 2 * NB, k=KC)
        aggcp = two(u=2)
        raw3 = cut(12, "p (u s) -> p u s", u=2)
        pair3 = cut(4, "p (u s) -> p u s", u=2)

        uw_in = sem("uw_in")
        fw_in = sem("fw_in")
        xp_in = [sem("xp_in0"), sem("xp_in1")]
        hp_ready = sem("hp_ready")
        xh_ready = sem("xh_ready")
        cat_tr = sem("cat_tr")
        catT_h = sem("catT_h")
        catT_a = sem("catT_a")
        y1_ps = sem("y1_ps")
        y1_ready = sem("y1_ready")
        y2_ps = sem("y2_ps")
        x1_ready = sem("x1_ready")
        raw3_ready = sem("raw3_ready")
        mv3_ready = sem("mv3_ready")
        pair3_ready = sem("pair3_ready")
        x1_kept = sem("x1_kept")
        sx = sem("xh_chain")
        aggcp_ready = sem("aggcp_ready")

        n_ = slice(0, NB)

        with nc.Block() as block:
            @block.sync
            def _(sp):
                sp.dma_start(uW1s, uW1.rearrange("(k p) n -> p k n", p=P)).then_inc(uw_in, 16)
                sp.dma_start(uW2s, uW2.rearrange("(k p) n -> p k n", p=P)).then_inc(uw_in, 16)
                sp.dma_start(ub1T, ub1.rearrange("(k p) -> p k", p=P)).then_inc(uw_in, 16)

                def step(m):
                    s = m.mod(2)
                    if m.within(NP2):
                        wait(sp, xh_ready, m.of(1, -1))
                        sp.dma_start(xp[s][n_], x[bass.ds(m.of(2 * NB), 2 * NB), :].rearrange("(u p) f -> p u f", p=NB)).then_inc(xp_in[s], 16)
                pipeline(sp, NP2, 0, 2, step)
                sp.dma_start(w1s, w1.rearrange("e (k p) n -> p e k n", p=P)).then_inc(fw_in, 16)
                sp.dma_start(w2s, w2.rearrange("e (k p) n -> p e k n", p=P)).then_inc(fw_in, 16)
                sp.dma_start(rwr[0:X], router_w).then_inc(fw_in, 16)
                sp.dma_start(b2s[0:X], b2).then_inc(fw_in, 16)
                for ex in range(X):
                    sp.dma_start(b1T[:, ex], b1[ex, :].rearrange("(k p) -> p k", p=P)).then_inc(fw_in, 16)
                sp.wait_ge(fw_in, 16 * (4 + X))

            @block.gpsimd
            def _(pool):
                def step(m):
                    s = m.mod(2)
                    if m.within(NP2):
                        wait(pool, cat_tr, m.of(1, -1))
                        nc.gpsimd.tensor_copy(aggcp[s][n_], agg[n_, bass.ds(m.of(2), 2), :]).then_inc(aggcp_ready, 1)
                        pool.wait_ge(hp_ready, m.of(1, 1))
                        wait(pool, x1_kept, m.of(1, -1))
                        wait(pool, mv3_ready, m.of(1, -1))
                        nc.gpsimd.tensor_tensor(xh[s][n_], xp[s][n_], hp[s][n_], ALU.add).then_inc(sx, 1)
                        pool.wait_ge(sx, m.of(1, 1))
                        nc.gpsimd.tensor_tensor(xh[s][n_], xh[s][n_],
                                                ub2b[n_, :].unsqueeze(1).to_broadcast([NB, 2, D]), ALU.add).then_inc(xh_ready, 1)
                pipeline(pool, NP2, 0, 2, step)

            @block.vector
            def _(dve):
                v = nc.vector

                def step(m):
                    s = m.mod(2)
                    if m.within(NP2):
                        dve.wait_ge(xp_in[s], m.per(2, 16, 16))
                        wait(dve, cat_tr, m.of(1, -1))
                        wait(dve, xh_ready, m.of(1, -1))
                        for u in range(2):
                            t = bass.ds(m.of(2, u), 1)
                            last = v.tensor_scalar(hp[s][n_, u], xp[s][n_, u], mv1[n_, t, 0], mv1[n_, t, 1],
                                                   ALU.subtract, ALU.mult)
                        last.then_inc(hp_ready, 1)
                    if m.within(NP2):
                        dve.wait_ge(cat_tr, m.of(1, 1))
                        wait(dve, y1_ps, m.of(1, -1))
                        v.tensor_copy(catT[s][:, KC:2 * KC, :],
                                      ps[:, 1, 0:4 * NB].rearrange("p (k n) -> p k n", k=KC)).then_inc(catT_a, 1)
                    a = m - 1
                    if a.within(NP2):
                        r = a.mod(2)
                        dve.wait_ge(y2_ps, a.of(1, 1))
                        dve.wait_ge(xh_ready, a.of(1, 1))
                        v.tensor_tensor(xh[r][n_].rearrange("p u n -> p (u n)"), ps[n_, 4, :],
                                        xh[r][n_].rearrange("p u n -> p (u n)"), ALU.add).then_inc(x1_ready, 1)
                        dve.wait_ge(x1_ready, a.of(1, 1))
                        for u in range(2):
                            v.bn_stats(raw3[n_, u], xh[r][n_, u]).then_inc(raw3_ready, 1)
                        wait_apart(dve, raw3_ready, a.of(2, 2), passed_dve)
                        for u in range(2):
                            v.bn_aggr(pair3[n_, u], raw3[n_, u]).then_inc(pair3_ready, 1)
                        dve.wait_ge(pair3_ready, a.of(2, 2))
                        v.tensor_copy(mv3[n_, bass.ds(a.of(2), 2), :], pair3[n_]).then_inc(mv3_ready, 1)
                        dve.wait_ge(mv3_ready, a.of(1, 1))

                pipeline(dve, NP2, 1, 2, step)

            @block.scalar
            def _(act):
                act.wait_ge(uw_in, 48)

                def step(m):
                    s = m.mod(2)
                    if m.within(NP2):
                        act.wait_ge(cat_tr, m.of(1, 1))
                        wait(act, y1_ps, m.of(1, -1))
                        nc.scalar.activation(catT[s][:, 0:KC, :], ps[:, 0, 0:4 * NB].rearrange("p (k n) -> p k n", k=KC),
                                             ACT.Copy).then_inc(catT_h, 1)
                        act.wait_ge(y1_ps, m.of(1, 1))
                        wait(act, y2_ps, m.of(1, -1))
                        for k in range(KC):
                            last = nc.scalar.activation(y1T[s][:, k], ps[:, 2 + k, 0:2 * NB], ACT.Silu,
                                                        bias=ub1T[:, k:k + 1])
                        last.then_inc(y1_ready, 1)
                    a = m - 1
                    if a.within(NP2):
                        act.wait_ge(x1_ready, a.of(1, 1))
                        nc.scalar.activation(agg[n_, bass.ds(a.of(2), 2), :], xh[a.mod(2)][n_], ACT.Copy).then_inc(x1_kept, 1)
                pipeline(act, NP2, 1, 2, step)

            @block.tensor
            def _(pe):
                t_ = nc.tensor
                pe.wait_ge(uw_in, 48)
                aggf = agg[:, :, :].rearrange("p t f -> p (t f)")

                def step(m):
                    s = m.mod(2)
                    if m.within(NP2):
                        pe.wait_ge(hp_ready, m.of(1, 1))
                        wait(pe, catT_h, m.of(1, 0))
                        wait(pe, catT_a, m.of(1, 0))
                        for u in range(2):
                            for k in range(KC):
                                c = k * 2 * NB + u * NB
                                t_.transpose(ps[:, 0, c:c + NB], hp[s][n_, u, k * P:(k + 1) * P], ident[n_, n_])
                        pe.wait_ge(aggcp_ready, m.of(1, 1))
                        for u in range(2):
                            for k in range(KC):
                                c = k * 2 * NB + u * NB
                                last = t_.transpose(ps[:, 1, c:c + NB], aggcp[s][n_, u, k * P:(k + 1) * P], ident[n_, n_])
                        last.then_inc(cat_tr, 1)
                    a = m - 1
                    if a.within(NP2):
                        r = a.mod(2)
                        pe.wait_ge(y1_ready, a.of(1, 1))
                        wait(pe, x1_ready, a.of(1, 0))
                        for u in range(2):
                            for k in range(KC):
                                last = t_.matmul(ps[n_, 4, u * D:(u + 1) * D], y1T[r][:, k, u * NB:(u + 1) * NB], uW2s[:, k],
                                                 start=(k == 0), stop=(k == KC - 1))
                        last.then_inc(y2_ps, 1)
                    if m.within(NP2):
                        pe.wait_ge(catT_h, m.of(1, 1))
                        pe.wait_ge(catT_a, m.of(1, 1))
                        wait(pe, y1_ready, m.of(1, 0))
                        for f in range(KC):
                            for k in range(2 * KC):
                                last = t_.matmul(ps[:, 2 + f, 0:2 * NB], uW1s[:, k, f * P:(f + 1) * P], catT[s][:, k],
                                                 start=(k == 0), stop=(k == 2 * KC - 1))
                        last.then_inc(y1_ps, 1)
                pipeline(pe, NP2, 1, 2, step)

        cut(0, restart=True)
        tb = two(u=2)
        tT = two("p (k n) -> p k n", KC * 2 * NB, k=KC)
        hT = two("p (k n) -> p k n", KC * 2 * NB, k=KC)
        acc = two(u=2)
        cc = two("p (u e) -> p u e", 2 * X, u=2)
        ccT = two("p (u n) -> p u n", 2 * NB, u=2)

        var3 = sem("var3_ready")
        std3 = sem("std3_ready")
        rstd3 = sem("rstd3_ready")
        rw_tr = sem("rw_tr")
        rwT_ready = sem("rwT_ready")
        tb_ready = sem("tb_ready")
        tb_tr = sem("tb_tr")
        tT_ready = sem("tT_ready")
        lg_ps = sem("lg_ps")
        lg_ready = sem("lg_ready")
        iox_ready = sem("iox_ready")
        tk = sem("top2_chain")
        sh_ready = sem("shifted_ready")
        ex_ready = sem("exp_ready")

        with nc.Block() as block:
            @block.gpsimd
            def _(pool):
                nc.gpsimd.iota(iox, pattern=[[1, X]], base=0, channel_multiplier=0,
                               allow_small_or_imprecise_dtypes=True).then_inc(iox_ready, 1)

            @block.vector
            def _(dve):
                v = nc.vector
                v.tensor_scalar(mv3[n_, :, 1], mv3[n_, :, 1], EPS, None, ALU.add).then_inc(var3, 1)
                dve.wait_ge(std3, 1)
                v.reciprocal(mv3[n_, :, 1], mv3[n_, :, 1]).then_inc(rstd3, 1)
                dve.wait_ge(rstd3, 1)

                def step(m):
                    s = m.mod(2)
                    if m.within(NP2):
                        wait(dve, tb_tr, m.of(1, -1))
                        for u in range(2):
                            t = bass.ds(m.of(2, u), 1)
                            last = v.tensor_scalar(tb[s][n_, u], agg[n_, t, :].rearrange("p t f -> p (t f)"),
                                                   mv3[n_, t, 0], mv3[n_, t, 1], ALU.subtract, ALU.mult)
                        last.then_inc(tb_ready, 1)
                pipeline(dve, NP2, 0, 2, step)

                done = [0]

                def link(ins):
                    done[0] += 1
                    ins.then_inc(tk, 1)
                    dve.wait_ge(tk, done[0])

                def wide(a):
                    return a[n_].unsqueeze(2).to_broadcast([NB, BK, X])

                iow = iox[n_].unsqueeze(1).to_broadcast([NB, BK, X])
                dve.wait_ge(lg_ready, NP2)
                dve.wait_ge(iox_ready, 1)
                link(v.tensor_reduce(out=m1[n_], in_=lg[n_], axis=AX.X, op=ALU.max))
                v.tensor_tensor(lg[n_], lg[n_], wide(m1), ALU.subtract).then_inc(sh_ready, 1)
                dve.wait_ge(ex_ready, 1)
                link(v.tensor_reduce(out=rsum[n_], in_=pr[n_], axis=AX.X, op=ALU.add))
                link(v.reciprocal(rsum[n_], rsum[n_]))
                link(v.tensor_tensor(pr[n_], pr[n_], wide(rsum), ALU.mult))
                for top, oh in ((m1, oh1), (m2, oh2)):
                    link(v.tensor_reduce(out=top[n_], in_=pr[n_], axis=AX.X, op=ALU.max))
                    link(v.tensor_tensor(cand[n_], pr[n_], wide(top), ALU.is_lt))
                    link(v.scalar_tensor_tensor(out=cand[n_], in0=cand[n_], scalar=float(X), in1=iow,
                                                op0=ALU.mult, op1=ALU.add))
                    link(v.tensor_reduce(out=isel[n_], in_=cand[n_], axis=AX.X, op=ALU.min))
                    link(v.tensor_tensor(oh[n_], iow, wide(isel), ALU.is_equal))
                    if oh is oh1:
                        link(v.scalar_tensor_tensor(out=pr[n_], in0=oh[n_], scalar=-2.0, in1=pr[n_],
                                                    op0=ALU.mult, op1=ALU.add))
                link(v.tensor_tensor(rsum[n_], m1[n_], m2[n_], ALU.add))
                link(v.tensor_scalar(rsum[n_], rsum[n_], 1e-12, None, ALU.max))
                link(v.reciprocal(rsum[n_], rsum[n_]))
                link(v.tensor_tensor(m1[n_], m1[n_], rsum[n_], ALU.mult))
                link(v.tensor_tensor(m2[n_], m2[n_], rsum[n_], ALU.mult))
                link(v.tensor_tensor(oh1[n_], oh1[n_], wide(m1), ALU.mult))
                link(v.tensor_tensor(oh2[n_], oh2[n_], wide(m2), ALU.mult))
                link(v.tensor_tensor(comb[n_], oh1[n_], oh2[n_], ALU.add))

            @block.scalar
            def _(act):
                act.wait_ge(var3, 1)
                nc.scalar.activation(mv3[n_, :, 1], mv3[n_, :, 1], ACT.Sqrt).then_inc(std3, 1)
                act.wait_ge(rw_tr, 1)
                nc.scalar.activation(rws, ps[:, 7, 0:KC * X].rearrange("p (k e) -> p k e", k=KC), ACT.Copy).then_inc(rwT_ready, 1)

                def step(m):
                    if m.within(NP2):
                        s = m.mod(2)
                        act.wait_ge(tb_tr, m.of(1, 1))
                        wait(act, lg_ps, m.of(1, -1))
                        nc.scalar.activation(tT[s], ps[:, s, 0:4 * NB].rearrange("p (k n) -> p k n", k=KC),
                                             ACT.Copy).then_inc(tT_ready, 1)
                    a = m - 1
                    if a.within(NP2):
                        s = a.mod(2)
                        act.wait_ge(lg_ps, a.of(1, 1))
                        nc.scalar.activation(lg[n_, bass.ds(a.of(2), 2), :],
                                             ps[n_, 2 + s, 0:2 * X].rearrange("p (u e) -> p u e", u=2), ACT.Copy).then_inc(lg_ready, 1)
                pipeline(act, NP2, 1, 2, step)
                act.wait_ge(sh_ready, 1)
                nc.scalar.activation(pr[n_], lg[n_], ACT.Exp).then_inc(ex_ready, 1)

            @block.tensor
            def _(pe):
                t_ = nc.tensor
                for k in range(KC):
                    last = t_.transpose(ps[:, 7, k * X:(k + 1) * X], rwr[0:X, k * P:(k + 1) * P], ident[0:X, 0:X])
                last.then_inc(rw_tr, 1)
                pe.wait_ge(rwT_ready, 1)

                def step(m):
                    if m.within(NP2):
                        s = m.mod(2)
                        pe.wait_ge(tb_ready, m.of(1, 1))
                        wait(pe, tT_ready, m.of(1, -1))
                        for u in range(2):
                            for k in range(KC):
                                c = k * 2 * NB + u * NB
                                last = t_.transpose(ps[:, s, c:c + NB], tb[s][n_, u, k * P:(k + 1) * P], ident[n_, n_])
                        last.then_inc(tb_tr, 1)
                    a = m - 1
                    if a.within(NP2):
                        s = a.mod(2)
                        pe.wait_ge(tT_ready, a.of(1, 1))
                        wait(pe, lg_ready, a.of(1, -1))
                        for u in range(2):
                            for k in range(KC):
                                last = t_.matmul(ps[n_, 2 + s, u * X:(u + 1) * X], tT[s][:, k, u * NB:(u + 1) * NB], rws[:, k],
                                                 start=(k == 0), stop=(k == KC - 1))
                        last.then_inc(lg_ps, 1)
                pipeline(pe, NP2, 1, 2, step)

        NQ = NP2 * X
        LH, LY = 4, 5
        tb2 = sem("tb2_ready")
        xt_ready = sem("xt_ready")
        t2_tr = sem("t2_tr")
        cT_tr = sem("cT_tr")
        t2T = sem("t2T_ready")
        ccT_r = sem("ccT_ready")
        b2_ps = sem("b2_ps")
        acc0 = sem("acc_started")
        h_ps = sem("h_ps")
        h_ready = sem("h_ready")
        y_ps = sem("y_ps")
        y_add = sem("y_added")
        o_out = [sem("o_out0"), sem("o_out1")]

        with nc.Block() as block:
            @block.sync
            def _(sp):
                def step(m):
                    s = m.mod(2)
                    sp.wait_ge(y_add, m.of(2 * X, 2 * X))
                    sp.dma_start(out[bass.ds(m.of(2 * NB), 2 * NB), :].rearrange("(u p) f -> p u f", p=NB), acc[s][n_]).then_inc(o_out[s], 16)
                pipeline(sp, NP2, 0, 2, step)
                sp.wait_ge(o_out[0], 16 * ((NP2 + 1) // 2))
                sp.wait_ge(o_out[1], 16 * (NP2 // 2))

            @block.vector
            def _(dve):
                v = nc.vector

                def step(m):
                    if m.within(NQ) and m.mod(X) == 0:
                        s = (m.c // X) % 2
                        wait(dve, t2_tr, m.per(X, 1, -1))
                        wait(dve, xt_ready, m.per(X, 1, -1))
                        for u in range(2):
                            t = bass.ds(m.per(X, 2, u), 1)
                            v.tensor_scalar(tb[s][n_, u], agg[n_, t, :].rearrange("p t f -> p (t f)"),
                                            mv3[n_, t, 0], mv3[n_, t, 1], ALU.subtract, ALU.mult)
                        wait(dve, y_add, m.per(X, 2 * X, -2 * X))
                        v.tensor_copy(cc[s][n_], comb[n_, bass.ds(m.per(X, 2), 2), :]).then_inc(tb2, 1)
                    a = m - LH
                    if a.within(NQ) and a.mod(X) == 0:
                        s = (a.c // X) % 2
                        dve.wait_ge(b2_ps, a.per(X, 1, 1))
                        dve.wait_ge(xt_ready, a.per(X, 1, 1))
                        v.tensor_tensor(acc[s][n_].rearrange("p u n -> p (u n)"), acc[s][n_].rearrange("p u n -> p (u n)"),
                                        ps[n_, 7, :], ALU.add).then_inc(acc0, 1)
                        dve.wait_ge(acc0, a.per(X, 1, 1))
                    a = m - LY
                    if a.within(NQ):
                        s, ex = (a.c // X) % 2, a.mod(X)
                        dve.wait_ge(y_ps, a.of(1, 1))
                        for u in range(2):
                            wait(dve, y_add, a.of(2, u - 1))
                            v.scalar_tensor_tensor(out=acc[s][n_, u], in0=ps[n_, 4 + a.mod(2), u * D:(u + 1) * D],
                                                   scalar=cc[s][n_, u, ex:ex + 1], in1=acc[s][n_, u],
                                                   op0=ALU.mult, op1=ALU.add).then_inc(y_add, 1)
                pipeline(dve, NQ, LY, 2 * X, step)

            @block.gpsimd
            def _(pool):
                def step(m):
                    s = m.mod(2)
                    pool.wait_ge(tb2, m.of(1, 1))
                    wait(pool, o_out[s], m.per(2, 16, 0))
                    nc.gpsimd.tensor_tensor(acc[s][n_], agg[n_, bass.ds(m.of(2), 2), :], tb[s][n_], ALU.add).then_inc(xt_ready, 1)
                pipeline(pool, NP2, 0, 2, step)

            @block.scalar
            def _(act):
                def step(m):
                    if m.within(NQ) and m.mod(X) == 0:
                        s = (m.c // X) % 2
                        act.wait_ge(t2_tr, m.per(X, 1, 1))
                        wait(act, h_ps, m.of(1, -X))
                        nc.scalar.activation(tT[s], ps[:, 0, 0:4 * NB].rearrange("p (k n) -> p k n", k=KC), ACT.Copy).then_inc(t2T, 1)
                        wait(act, b2_ps, m.per(X, 1, -1))
                        nc.scalar.activation(ccT[s][0:X], ps[0:X, 1, 0:2 * NB].rearrange("p (u n) -> p u n", u=2), ACT.Copy).then_inc(ccT_r, 1)
                    a = m - LH
                    if a.within(NQ):
                        ex, s = a.mod(X), a.mod(2)
                        act.wait_ge(h_ps, a.of(1, 1))
                        wait(act, y_ps, a.of(1, -1))
                        for k in range(KC):
                            last = nc.scalar.activation(hT[s][:, k], ps[:, 2 + k, 0:2 * NB], ACT.Gelu, bias=b1T[:, ex, k:k + 1])
                        last.then_inc(h_ready, 1)
                pipeline(act, NQ, LH, 2 * X, step)

            @block.tensor
            def _(pe):
                t_ = nc.tensor

                def step(m):
                    if m.within(NQ) and m.mod(X) == 0:
                        s = (m.c // X) % 2
                        pe.wait_ge(tb2, m.per(X, 1, 1))
                        wait(pe, ccT_r, m.per(X, 1, 0))
                        wait(pe, t2T, m.per(X, 1, 0))
                        for u in range(2):
                            for k in range(KC):
                                c = k * 2 * NB + u * NB
                                t_.transpose(ps[:, 0, c:c + NB], tb[s][n_, u, k * P:(k + 1) * P], ident[n_, n_])
                        for u in range(2):
                            last = t_.transpose(ps[0:X, 1, u * NB:(u + 1) * NB], cc[s][n_, u], ident[n_, n_])
                        last.then_inc(t2_tr, 1)
                    if m.within(NQ) and m.mod(X) == 2:
                        b = m - 2
                        s = (b.c // X) % 2
                        pe.wait_ge(ccT_r, b.per(X, 1, 1))
                        wait(pe, acc0, b.per(X, 1, 0))
                        for u in range(2):
                            last = t_.matmul(ps[n_, 7, u * D:(u + 1) * D], ccT[s][0:X, u], b2s[0:X], start=True, stop=True)
                        last.then_inc(b2_ps, 1)
                    a = m - LH
                    if a.within(NQ):
                        s, ex = (a.c // X) % 2, a.mod(X)
                        pe.wait_ge(t2T, a.per(X, 1, 1))
                        wait(pe, h_ready, a.of(1, 0))
                        for f in range(KC):
                            for k in range(KC):
                                last = t_.matmul(ps[:, 2 + f, 0:2 * NB], w1s[:, ex, k, f * P:(f + 1) * P], tT[s][:, k],
                                                 start=(k == 0), stop=(k == KC - 1))
                        last.then_inc(h_ps, 1)
                    a = m - LY
                    if a.within(NQ):
                        s, ex = a.mod(2), a.mod(X)
                        pe.wait_ge(h_ready, a.of(1, 1))
                        wait(pe, y_add, a.of(2, -2))
                        for u in range(2):
                            for k in range(KC):
                                last = t_.matmul(ps[n_, 4 + s, u * D:(u + 1) * D], hT[s][:, k, u * NB:(u + 1) * NB], w2s[:, ex, k],
                                                 start=(k == 0), stop=(k == KC - 1))
                        last.then_inc(y_ps, 1)
                pipeline(pe, NQ, LY, 2 * X, step)


_INS = ["x", "src", "dst", "edge_weight1", "L0_gnn_mW1", "L0_gnn_mb1", "L0_gnn_ln_g", "L0_gnn_ln_b", "L0_gnn_mW2",
        "L0_gnn_mb2", "L0_gnn_uW1", "L0_gnn_ub1", "L0_gnn_uW2", "L0_gnn_ub2", "L0_ffn_router_w", "L0_ffn_w1",
        "L0_ffn_b1", "L0_ffn_w2", "L0_ffn_b2"]


def kernel(**inputs):
    import concourse.bacc as bacc
    from concourse.bass_utils import run_bass_kernel_spmd

    nc = bacc.Bacc("TRN2", target_bir_lowering=False, num_devices=1)
    arrays, args = {}, []
    for name in _INS:
        a = np.ascontiguousarray(inputs[name])
        arrays[f"in_{name}"] = a
        args.append(nc.dram_tensor(f"in_{name}", a.shape, mybir.dt.from_np(a.dtype), kind="ExternalInput").ap())
    args.append(nc.dram_tensor("out", (N, D), f32, kind="ExternalOutput").ap())
    gnn_moe_kernel(nc, *args)
    r = run_bass_kernel_spmd(nc, [arrays], core_ids=[0])
    return r.results[0]["out"]
```

```python
from contextlib import ExitStack

import numpy as np

import concourse.bass as bass
from concourse import mybir
from concourse.alu_op_type import AluOpType as ALU

f32, bf16, i32 = mybir.dt.float32, mybir.dt.bfloat16, mybir.dt.int32
i16 = mybir.dt.int16
ACT = mybir.ActivationFunctionType
AX = mybir.AxisListType

P = 128
N, D, E, X = 6250, 256, 100000, 8
KC = D // P
NB = 125
BK = N // NB
EC = E // NB
ECP = [480, 320]
EC0 = [0, ECP[0]]
PAIRS = [-(-((n * NB + BK * (P - 1)) // P) // 2) for n in ECP]
GP = [2 * n for n in PAIRS]
G0 = [0, GP[0]]
G = sum(GP)
TABP = [-(-g // P) for g in GP]
PADT = 16
UB = 10
EPS = 1e-5
RND = 12582912.0
assert BK * NB == N and EC * NB == E
assert sum(ECP) == EC and all(n <= 4 * g for n, g in zip(ECP, GP))
SC = [10, 5]
assert ECP[0] % (2 * SC[0]) == 0 and ECP[1] == 2 * SC[1] * (PAIRS[0] // 8)
NP2 = BK // 2
K2 = 2
XT = 2 * -(-(K2 * N + X * (P - 1)) // (2 * P))
XW = D + 1
XD = 8
assert XT + 16 <= P


class Step:

    def __init__(self, it, unroll, c):
        self.it, self.unroll, self.c = it, unroll, c

    def __sub__(self, lag):
        return Step(self.it, self.unroll, self.c - lag)

    def of(self, scale=1, add=0):
        const = scale * self.c + add
        return const if isinstance(self.it, int) else self.it * (scale * self.unroll) + const

    def per(self, d, scale=1, add=0):
        const = scale * (self.c // d) + add
        return const if isinstance(self.it, int) else self.it * (scale * self.unroll // d) + const

    def mod(self, k):
        return self.c % k

    def within(self, n):
        return not isinstance(self.it, int) or 0 <= self.c < n


def pipeline(eng, n, depth, unroll, step, enter=None, peel=1):
    first = max(peel, -(-depth // unroll))
    last = n // unroll
    assert last > first
    for b in range(first):
        if enter:
            enter(b)
        for c in range(unroll):
            step(Step(0, unroll, b * unroll + c))
    with eng.Fori(0, last - first) as it:
        if enter:
            enter(it + first)
        for c in range(unroll):
            step(Step(it, unroll, first * unroll + c))
    for m in range(last * unroll, n + depth):
        if enter and m % unroll == 0:
            enter(m // unroll)
        step(Step(0, unroll, m))


def wait(eng, sem, value):
    if isinstance(value, int) and value <= 0:
        return
    eng.wait_ge(sem, value)


def wait_apart(eng, sem, value, passed):
    wait(eng, sem, value)
    if not isinstance(value, int):
        eng.sem_inc(passed, 1)


def gnn_moe_kernel(nc, x, src, dst, edge_w, mW1, mb1, ln_g, ln_b, mW2, mb2, uW1, ub1, uW2, ub2,
                   router_w, w1, b1, w2, b2, out):
    ctx = ExitStack()
    with ctx:
        def sb(name, shape, dt=f32):
            return ctx.enter_context(nc.sbuf_tensor(name, shape, dt))

        def sem(name):
            return ctx.enter_context(nc.semaphore(name))

        ctx.enter_context(nc.allow_non_contiguous_dma(reason="small vectors laid along partitions"))

        recd = [nc.dram_tensor(f"edge_records{h}", (P * GP[h], 4), f32).ap() for h in range(2)]
        dstd = nc.dram_tensor("dst_half", (N, D), f32).ap()
        wcd = nc.dram_tensor("edge_weight_column", (3, D), bf16).ap()
        xsd = nc.dram_tensor("routed_tokens", (XT * P, XW), f32).ap()
        yd = nc.dram_tensor("expert_rows", (K2 * N + XD * P, D), f32).ap()
        xtabd = nc.dram_tensor("tile_experts", (P, 1), i32).ap()
        tabd = [nc.dram_tensor(f"tile_blocks{h}", (P, TABP[h]), i32).ap() for h in range(2)]

        ablk = sb("ablk", [P, 3, BK * D], bf16)
        agg = sb("agg", [P, BK, D])
        rec = sb("rec", [P, G, 4])
        dpart = sb("dpart", [P, G, 3], bf16)
        idx = sb("idx", [P, G], i32)
        work = sb("work", [P, 12800])
        W2c = sb("W2c", [P, KC, D])
        b2c = sb("b2c", [P, D])
        ub2b = sb("ub2b", [P, D])
        mv1 = sb("mv1", [P, BK, 2])
        ident = sb("ident", [P, P])
        iota_n = sb("iota_n", [P, NB])
        tabrows = [sb(f"tabrow{h}", [1, PADT + P * TABP[h]], i32) for h in range(2)]
        stage_i = sb("stage_i", [P, 16], i32)
        stage_s = sb("stage_s", [P, 2 * SC[0]], i32)
        stage = sb("stage", [P, 2, SC[0], 4])
        ps = ctx.enter_context(nc.psum_tensor("ps", [P, 8, 512], f32))

        at = [0]

        def cut(floats, shape=None, dt=f32, restart=False, **dims):
            if restart:
                at[0] = 0
            a = work[:, at[0]:at[0] + floats]
            at[0] += floats
            assert at[0] <= 12800
            a = a if dt == f32 else a.bitcast(dt)
            return a.rearrange(shape, **dims) if shape else a

        srci = cut(EC, dt=i32, restart=True)
        dsti = cut(EC, dt=i32)
        dwt = cut(EC)
        srcf = cut(EC)
        blkf = cut(EC)
        blkh = cut(EC // 2, dt=bf16)
        ones = cut(EC // 2, dt=bf16)
        mask = [cut(EC // 2, dt=bf16) for _ in range(2)]
        rank = [cut(EC) for _ in range(2)]
        pos = cut(EC)
        posi = cut(EC, dt=i32)
        lowi = cut(EC, dt=i32)
        cnt = cut(BK)
        iota_b = cut(BK + 2)
        tri = cut(P)
        onesf = cut(P)
        ntile = cut(BK)
        ntilei = cut(BK, dt=i32)
        start = cut(BK)
        base = cut(BK + 1)
        gidx = [cut(k) for k in TABP]
        cmp = cut(max(TABP) * BK)
        tblk = cut(max(TABP))
        tblki = [cut(k, dt=i32) for k in TABP]
        W1ab = cut(KC * 2 * D, "p (k n) -> p k n", k=KC)
        mb1b = cut(D)
        lng = cut(KC)
        lnb = cut(KC)
        w1c = cut(D)
        wcp = cut(3 * D // 2, "p (k n) -> p k n", dt=bf16, k=3)
        hn = [blkf[:, 0:D], blkf[:, D:2 * D]]
        hnT = [rank[0][:, 0:KC * NB].rearrange("p (k n) -> p k n", k=KC),
               rank[1][:, 0:KC * NB].rearrange("p (k n) -> p k n", k=KC)]
        bout = [pos[:, 0:D], pos[:, D:2 * D]]
        atmp = [lowi.bitcast(f32)[:, 0:D], lowi.bitcast(f32)[:, D:2 * D]]
        W2raw = dwt
        W2g = srcf[:, 0:KC * D].rearrange("p (k n) -> p k n", k=KC)
        lnbb = posi.bitcast(f32)[:, 0:KC * P].rearrange("p (k n) -> p k n", k=KC)
        recE = [rec[0:NB, G0[h]:G0[h] + ECP[h], :] for h in range(2)]

        passed_pool = sem("passed_pool")
        passed_dve = sem("passed_dve")
        edges_in = sem("edges_in")
        x_in = sem("x_in")
        w_in = sem("w_in")
        w2_in = sem("w2_in")
        consts = sem("consts")
        pads_set = sem("pads_set")
        pads_out = sem("pads_out")
        rk = sem("rank_chain")
        cnt_ready = sem("cnt_ready")
        pre_ready = sem("pre_ready")
        blk_ready = sem("blk_ready")
        blk_out = sem("blk_out")
        blk_in = sem("blk_in")
        recs_ready = sem("recs_ready")
        staged = sem("staged")
        scat = [[sem(f"scattered{h}_{i}") for i in range(2)] for h in range(2)]
        scat_done = sem("scat_done")
        rec_in = sem("rec_in")

        def load_records(sp, h):
            sp.wait_ge(scat_done, h + 1)
            sp.dma_start(rec[:, G0[h]:G0[h] + GP[h], :].rearrange("p g f -> p (g f)"),
                         recd[h].rearrange("(p g) f -> p (g f)", p=P)).then_inc(rec_in, 16)
            sp.wait_ge(rec_in, 16 * h + 16)

        def stage_records(pool, h, m, i, done, staged, sems):
            n = SC[h]
            wait(pool, sems[i], done)
            cols = bass.ds(m.of(n) if m.unroll != 8 else m.per(4, n), n)
            nc.gpsimd.tensor_copy(stage[0:NB, i, 0:n], recE[h][:, cols, :]).then_inc(staged, 1)
            nc.gpsimd.tensor_copy(stage_s[0:NB, i * n:(i + 1) * n], recE[h][:, cols, 3]).then_inc(staged, 1)

        def scatter_column(pool, h, i, c, sems):
            n = SC[h]
            pool.indirect_dma_start(
                recd[h], bass.IndirectOffsetOnAxis(ap=stage_s[0:NB, i * n + c:i * n + c + 1], axis=0),
                stage[0:NB, i, c, :], None).then_inc(sems[i], 16)

        var_ready = sem("var_ready")
        std_ready = sem("std_ready")
        nd = sem("node_chain")
        wcol_ready = sem("wcol_ready")
        wcol_out = sem("wcol_out")
        wcol_in = sem("wcol_in")
        w2g_ready = sem("w2g_ready")
        w2m_ready = sem("w2m_ready")
        hn_ready = sem("hn_ready")
        hn_tr = sem("hn_tr")
        hnT_ready = sem("hnT_ready")
        ab_ready = sem("ab_ready")
        b_copied = sem("b_copied")
        a_taken = sem("a_taken")
        b_stored = [sem("b_stored0"), sem("b_stored1")]

        with nc.Block() as block:
            @block.sync
            def _(sp):
                sp.dma_start(srci[0:NB], src.rearrange("(p c) -> p c", p=NB)).then_inc(edges_in, 16)
                sp.dma_start(dsti[0:NB], dst.rearrange("(p c) -> p c", p=NB)).then_inc(edges_in, 16)
                sp.dma_start(dwt[0:NB], edge_w.rearrange("(p c) o -> p (c o)", p=NB)).then_inc(edges_in, 16)
                xv = x.rearrange("(t p) f -> p t f", p=NB)
                for t in range(0, BK, 10):
                    sp.dma_start(agg[0:NB, t:t + 10, :], xv[:, t:t + 10, :]).then_inc(x_in, 16)
                for h in range(2):
                    sp.dma_start(W1ab[:, :, h * D:(h + 1) * D],
                                 mW1[h * D:(h + 1) * D, :].rearrange("(k p) n -> p k n", p=P)).then_inc(w_in, 16)
                sp.dma_start(mb1b, mb1.partition_broadcast(P)).then_inc(w_in, 16)
                sp.dma_start(b2c[:, :], mb2.partition_broadcast(P)).then_inc(w_in, 16)
                sp.dma_start(ub2b[:, :], ub2.partition_broadcast(P)).then_inc(w_in, 16)
                sp.dma_start(lng, ln_g.rearrange("(k p) -> p k", p=P)).then_inc(w_in, 16)
                sp.dma_start(lnb, ln_b.rearrange("(k p) -> p k", p=P)).then_inc(w_in, 16)
                sp.dma_start(w1c[0:1], mW1[2 * D:2 * D + 1, :]).then_inc(w_in, 16)
                sp.wait_ge(pads_set, 4)
                for h in range(2):
                    sp.dma_start(recd[h].rearrange("(p g) f -> p (g f)", p=P),
                                 rec[:, G0[h]:G0[h] + GP[h], :].rearrange("p g f -> p (g f)")).then_inc(pads_out, 16)
                for h in range(2):
                    sp.wait_ge(blk_ready, h + 1)
                    sp.dma_start(tabd[h], tblki[h]).then_inc(blk_out, 16)
                    sp.wait_ge(blk_out, 16 * h + 16)
                    sp.dma_start(tabrows[h][0:1, PADT:PADT + P * TABP[h]],
                                 tabd[h].rearrange("p k -> (p k)").rearrange("(a n) -> a n", a=1)).then_inc(blk_in, 16)
                sp.wait_ge(recs_ready, 2)
                sp.dma_start(W2raw[:, 0:KC * D].rearrange("p (k n) -> p k n", k=KC),
                             mW2.rearrange("(k p) n -> p k n", p=P)).then_inc(w2_in, 16)
                sp.wait_ge(wcol_ready, 1)
                sp.dma_start(wcd.rearrange("k n -> (k n)").rearrange("(a n) -> a n", a=1),
                             wcp[0:1].rearrange("p k n -> p (k n)")).then_inc(wcol_out, 16)
                sp.wait_ge(wcol_out, 16)
                for k in range(3):
                    row = wcd[k, :].partition_broadcast(BK).partition_broadcast(P - NB)
                    sp.dma_start(ablk[NB:P, k, :].rearrange("p (b n) -> p b n", b=BK), row).then_inc(wcol_in, 16)

                def step(m):
                    sp.wait_ge(b_copied, m.of(1, 1))
                    rows = m.of(NB)
                    sp.dma_start(dstd[bass.ds(rows, NB), :], bout[m.mod(2)][0:NB]).then_inc(b_stored[m.mod(2)], 16)
                with sp.Fori(0, BK // 2) as it:
                    for c in range(2):
                        step(Step(it, 2, c))
                for h in range(2):
                    sp.wait_ge(b_stored[h], 16 * (BK // 2))
                sp.wait_ge(wcol_in, 48)
                sp.wait_ge(blk_in, 32)
                load_records(sp, 0)

            @block.gpsimd
            def _(pool):
                nc.gpsimd.memset(rec[:, :, :], 0.0).then_inc(pads_set, 1)
                for h in range(2):
                    nc.gpsimd.memset(tabrows[h][:, 0:PADT], 0).then_inc(pads_set, 1)
                pool.wait_ge(pads_set, 3)
                nc.gpsimd.memset(rec[:, :, 0:1], -1.0).then_inc(pads_set, 1)
                nc.gpsimd.memset(ident[:, :], 0.0).then_inc(consts, 1)
                nc.gpsimd.memset(onesf, 1.0).then_inc(consts, 1)
                nc.gpsimd.memset(ones, 1.0).then_inc(consts, 1)
                nc.gpsimd.iota(iota_n[:, :], pattern=[[1, NB]], base=0, channel_multiplier=0,
                               allow_small_or_imprecise_dtypes=True).then_inc(consts, 1)
                nc.gpsimd.iota(iota_b, pattern=[[1, BK + 2]], base=0, channel_multiplier=0,
                               allow_small_or_imprecise_dtypes=True).then_inc(consts, 1)
                for h in range(2):
                    nc.gpsimd.iota(gidx[h], pattern=[[1, TABP[h]]], base=0, channel_multiplier=TABP[h],
                                   allow_small_or_imprecise_dtypes=True).then_inc(consts, 1)
                pool.wait_ge(consts, 7)
                nc.gpsimd.affine_select(out=ident[:, :], in_=ident[:, :], compare_op=ALU.not_equal, fill=1.0,
                                        base=0, pattern=[[-1, P]], channel_multiplier=1).then_inc(consts, 1)
                nc.gpsimd.affine_select(out=tri, in_=onesf, compare_op=ALU.is_gt, fill=0.0,
                                        base=0, pattern=[[1, P]], channel_multiplier=-1).then_inc(consts, 1)
                pool.wait_ge(recs_ready, 1)

                def step(m):
                    i = m.mod(2)
                    stage_records(pool, 0, m, i, m.per(2, 16 * SC[0], 0), staged, scat[0])
                    wait_apart(pool, staged, m.of(2, 2), passed_pool)
                    for c in range(SC[0]):
                        scatter_column(pool, 0, i, c, scat[0])
                pipeline(pool, ECP[0] // SC[0], 0, 2, step)
                for i in range(2):
                    pool.wait_ge(scat[0][i], 16 * ECP[0] // 2)
                pool.sem_inc(scat_done, 1)

            @block.vector
            def _(dve):
                done = [0]

                def link(ins):
                    done[0] += 1
                    ins.then_inc(rk, 1)
                    dve.wait_ge(rk, done[0])

                v = nc.vector
                e = slice(0, NB)
                dve.wait_ge(edges_in, 48)
                link(v.tensor_copy(srcf[e], srci[e]))
                link(v.tensor_scalar(blkf[e], srcf[e], -float(NB // 2), 1.0 / NB, ALU.add, ALU.mult))
                link(v.tensor_scalar(blkf[e], blkf[e], RND, None, ALU.add))
                link(v.tensor_scalar(blkf[e], blkf[e], RND, None, ALU.subtract))
                link(v.tensor_copy(blkh[e], blkf[e]))
                link(v.memset(pos[e], 0.0))
                link(v.memset(base[e, BK:BK + 1], 0.0))
                dve.wait_ge(consts, 9)
                for h in range(2):
                    w = slice(EC0[h], EC0[h] + ECP[h])
                    def tally(b, c):
                        v.tensor_scalar(mask[c][e, w], blkh[e, w], iota_b[e, b], 0.0, ALU.is_equal, ALU.add,
                                        accum_out=cnt[e, b]).then_inc(cnt_ready, 1)

                    for c in range(2):
                        tally(bass.ds(c, 1), c)
                    with dve.Fori(0, BK // UB - 1) as it:
                        for c in range(UB):
                            dve.wait_ge(cnt_ready, it * UB + c + 1 + BK * h)
                            tally(bass.ds(it * UB + c + 2, 1), c % 2)
                    for c in range(BK - UB + 2, BK):
                        dve.wait_ge(cnt_ready, c - 1 + BK * h)
                        tally(bass.ds(c, 1), c % 2)
                    if h == 0:
                        dve.wait_ge(pads_out, 32)
                    link(v.scalar_tensor_tensor(out=recE[h][:, :, 0], in0=blkf[e, w], scalar=-float(NB), in1=srcf[e, w],
                                                op0=ALU.mult, op1=ALU.add))
                    link(v.tensor_copy(recE[h][:, :, 1], dsti[e, w]))
                    link(v.tensor_copy(recE[h][:, :, 2], dwt[e, w]))
                    dve.wait_ge(pre_ready, 2 * h + 2)
                    link(v.tensor_scalar(ntilei, ps[:, 1, 0:BK], float(P - 1), None, ALU.add))
                    link(v.tensor_scalar(ntilei, ntilei, 7, None, ALU.arith_shift_right))
                    link(v.tensor_copy(ntile, ntilei))
                    link(v.tensor_tensor_scan(start, ones[:, 0:BK], ntile, 0.0, ALU.mult, ALU.add))
                    link(v.tensor_tensor(start, start, ntile, ALU.subtract))
                    link(v.tensor_scalar(base[e, 0:BK], start[e], float(P), -1.0, ALU.mult, ALU.add))
                    link(v.tensor_tensor(base[e, 0:BK], base[e, 0:BK], ps[e, 0, 0:BK], ALU.add))
                    nt = TABP[h]
                    ge = cmp[:, 0:nt * BK].rearrange("p (k b) -> p k b", k=nt)
                    link(v.tensor_tensor(ge, start.unsqueeze(1).to_broadcast([P, nt, BK]),
                                         gidx[h].unsqueeze(2).to_broadcast([P, nt, BK]), ALU.is_le))
                    link(v.tensor_reduce(out=tblk[:, 0:nt], in_=ge, axis=AX.X, op=ALU.add))
                    v.tensor_scalar(tblki[h], tblk[:, 0:nt], -1.0, float(D), ALU.add, ALU.mult).then_inc(blk_ready, 1)

                    def match(b, c):
                        return v.tensor_scalar(mask[c][e, w], blkh[e, w], iota_b[e, b], None, ALU.is_equal)

                    def count(b, c):
                        return v.tensor_tensor_scan(rank[c][e, w], ones[e, w], mask[c][e, w], base[e, b], ALU.mult, ALU.add)

                    link(match(bass.ds(0, 1), 0))
                    link(count(bass.ds(0, 1), 0))
                    before = done[0]
                    link(match(bass.ds(1, 1), 1))
                    with dve.Fori(0, BK // UB) as it:
                        for j in range(UB):
                            c, at0 = j % 2, it * (3 * UB) + before + 3 * j
                            wait_apart(dve, rk, at0, passed_dve)
                            v.copy_predicated(pos[e, w], mask[c][e, w].bitcast(i16), rank[c][e, w]).then_inc(rk, 1)
                            dve.wait_ge(rk, at0 + 1)
                            count(bass.ds(it * UB + j + 1, 1), 1 - c).then_inc(rk, 1)
                            dve.wait_ge(rk, at0 + 2)
                            match(bass.ds(it * UB + j + 2, 1), c).then_inc(rk, 1)
                    done[0] += 3 * BK
                    link(v.tensor_copy(posi[e, w], pos[e, w]))
                    link(v.tensor_scalar(lowi[e, w], posi[e, w], P - 1, None, ALU.bitwise_and))
                    link(v.tensor_scalar(posi[e, w], posi[e, w], 7, None, ALU.arith_shift_right))
                    v.scalar_tensor_tensor(out=recE[h][:, :, 3], in0=lowi[e, w], scalar=float(GP[h]), in1=posi[e, w],
                                           op0=ALU.mult, op1=ALU.add).then_inc(recs_ready, 1)

                dve.wait_ge(x_in, 80)
                stats = rank[0][:, 0:12].rearrange("p (h s) -> p h s", h=2)
                pair = rank[0][:, 12:16].rearrange("p (h s) -> p h s", h=2)
                before = done[0]
                with dve.Fori(0, BK // 2) as it:
                    for h in range(2):
                        v.bn_stats(stats[e, h], agg[e, bass.ds(it * 2 + h, 1), :].rearrange("p t f -> p (t f)")).then_inc(rk, 1)
                    wait_apart(dve, rk, it * 5 + before + 2, passed_dve)
                    for h in range(2):
                        v.bn_aggr(pair[e, h], stats[e, h]).then_inc(rk, 1)
                    dve.wait_ge(rk, it * 5 + before + 4)
                    v.tensor_copy(mv1[e, bass.ds(it * 2, 2), :], pair[e]).then_inc(rk, 1)
                    dve.wait_ge(rk, it * 5 + before + 5)
                done[0] += 5 * (BK // 2)
                v.tensor_scalar(mv1[e, :, 1], mv1[e, :, 1], EPS, None, ALU.add).then_inc(var_ready, 1)
                dve.wait_ge(w_in, 16 * 8)
                o = slice(0, 1)
                link(v.tensor_copy(wcp[o, 0], w1c[o]))
                link(v.tensor_tensor(w1c[o], w1c[o], wcp[o, 0], ALU.subtract))
                link(v.tensor_copy(wcp[o, 1], w1c[o]))
                link(v.tensor_tensor(w1c[o], w1c[o], wcp[o, 1], ALU.subtract))
                v.tensor_copy(wcp[o, 2], w1c[o]).then_inc(wcol_ready, 1)
                dve.wait_ge(w2_in, 16)
                for k in range(KC):
                    v.tensor_scalar(W2g[:, k], W2raw[:, k * D:(k + 1) * D], lng[:, k:k + 1], None,
                                    ALU.mult).then_inc(w2g_ready, 1)
                    v.tensor_scalar(lnbb[:, k], onesf, lnb[:, k:k + 1], None, ALU.mult).then_inc(w2g_ready, 1)
                dve.wait_ge(w2m_ready, 1)
                for k in range(KC):
                    v.scalar_tensor_tensor(out=W2c[:, k], in0=ps[:, 0, 0:D], scalar=-1.0 / D, in1=W2g[:, k],
                                           op0=ALU.mult, op1=ALU.add)
                link(v.tensor_tensor(b2c[:, :], b2c[:, :], ps[:, 1, 0:D], ALU.add))
                dve.wait_ge(std_ready, 1)
                link(v.reciprocal(mv1[e, :, 1], mv1[e, :, 1]))

                def step(m):
                    if m.within(BK):
                        s = m.mod(2)
                        wait(dve, hn_tr, m.of(1, -1))
                        t = bass.ds(m.of(), 1)
                        v.tensor_scalar(hn[s][e], agg[e, t, :].rearrange("p t f -> p (t f)"),
                                        mv1[e, t, 0], mv1[e, t, 1], ALU.subtract, ALU.mult).then_inc(hn_ready, 1)
                    a = m - 2
                    if a.within(BK):
                        s = a.mod(2)
                        dve.wait_ge(ab_ready, a.of(1, 1))
                        t = bass.ds(a.of(D), D)
                        tmp = atmp[s][e]
                        v.tensor_tensor(tmp, ps[e, 2 + s, 0:D], mb1b[e], ALU.add).then_inc(a_taken, 1)
                        dve.wait_ge(a_taken, a.of(1, 1))
                        for k in range(2):
                            v.tensor_copy(ablk[e, k, t], tmp).then_inc(nd, 1)
                            dve.wait_ge(nd, a.of(5, 2 * k + 1))
                            v.tensor_tensor(tmp, tmp, ablk[e, k, t], ALU.subtract).then_inc(nd, 1)
                            dve.wait_ge(nd, a.of(5, 2 * k + 2))
                        v.tensor_copy(ablk[e, 2, t], tmp).then_inc(nd, 1)

                pipeline(dve, BK, 2, 2, step)

            @block.scalar
            def _(act):
                act.wait_ge(var_ready, 1)
                nc.scalar.activation(mv1[0:NB, :, 1], mv1[0:NB, :, 1], ACT.Sqrt).then_inc(std_ready, 1)

                def step(m):
                    s = m.mod(2)
                    if m.within(BK):
                        act.wait_ge(hn_tr, m.of(1, 1))
                        wait(act, ab_ready, m.of(1, -1))
                        nc.scalar.activation(hnT[s], ps[:, 4 + s, 0:KC * NB].rearrange("p (k n) -> p k n", k=KC),
                                             ACT.Copy).then_inc(hnT_ready, 1)
                    b = m - 2
                    if b.within(BK):
                        act.wait_ge(a_taken, b.of(1, 1))
                        wait(act, b_stored[b.mod(2)], b.per(2, 16, 0))
                        nc.scalar.activation(bout[b.mod(2)][0:NB], ps[0:NB, 2 + b.mod(2), D:2 * D],
                                             ACT.Copy).then_inc(b_copied, 1)

                pipeline(act, BK, 2, 2, step, peel=2)

            @block.tensor
            def _(pe):
                for h in range(2):
                    pe.wait_ge(cnt_ready, BK * (h + 1))
                    nc.tensor.matmul(ps[:, 0, 0:BK], tri[0:NB, :], cnt[0:NB], start=True, stop=True).then_inc(pre_ready, 1)
                    nc.tensor.matmul(ps[:, 1, 0:BK], onesf[0:NB], cnt[0:NB], start=True, stop=True).then_inc(pre_ready, 1)
                pe.wait_ge(w2g_ready, 2 * KC)
                for k in range(KC):
                    nc.tensor.matmul(ps[:, 0, 0:D], onesf, W2g[:, k], start=(k == 0), stop=(k == KC - 1))
                for k in range(KC):
                    last = nc.tensor.matmul(ps[:, 1, 0:D], lnbb[:, k], W2raw[:, k * D:(k + 1) * D],
                                            start=(k == 0), stop=(k == KC - 1))
                last.then_inc(w2m_ready, 1)

                def step(m):
                    if m.within(BK):
                        s = m.mod(2)
                        pe.wait_ge(hn_ready, m.of(1, 1))
                        wait(pe, hnT_ready, m.of(1, -1))
                        for k in range(KC):
                            last = nc.tensor.transpose(ps[:, 4 + s, k * NB:(k + 1) * NB],
                                                       hn[s][0:NB, k * P:(k + 1) * P], ident[0:NB, 0:NB])
                        last.then_inc(hn_tr, 1)
                    a = m - 1
                    if a.within(BK):
                        s = a.mod(2)
                        pe.wait_ge(hnT_ready, a.of(1, 1))
                        wait(pe, a_taken, a.of(1, -1))
                        wait(pe, b_copied, a.of(1, -1))
                        for k in range(KC):
                            last = nc.tensor.matmul(ps[0:NB, 2 + s, :], hnT[s][:, k, :], W1ab[:, k, :],
                                                    start=(k == 0), stop=(k == KC - 1))
                        last.then_inc(ab_ready, 1)

                pipeline(pe, BK, 1, 2, step)

        RE, RB, RT = 8, 8, 4
        eh = cut(RE * 2 * P, "p (r u n) -> p r u n", restart=True, r=RE, u=2)
        bg = cut(RB * 2 * D, "p (r u n) -> p r u n", r=RB, u=2)
        sa = cut(RT * 2 * D, "p (r u n) -> p r u n", r=RT, u=2)
        sT = cut(RT * 2 * D, "p (r u k n) -> p r u k n", r=RT, u=2, k=KC)
        zb = cut(2 * D, "p (u n) -> p u n", u=2)
        junk = cut(D)
        msg = cut(2 * 2 * D, "p (r u n) -> p r u n", r=2, u=2)
        ohT = cut(2 * P, "p (r u n) -> p r u n", dt=bf16, r=2, u=2)
        ssum = cut(RE * 2, "p (r u) -> p r u", r=RE)
        ssq = cut(RE * 2, "p (r u) -> p r u", r=RE)
        rstd = cut(RE * 2, "p (r u) -> p r u", r=RE)
        mean = cut(4, "p (r u) -> p r u", r=2)
        var = cut(8, "p (i r u) -> p i r u", i=2, r=2)
        half = cut(4, "p (r u) -> p r u", r=2)
        dres = [agg[:, 0:4, :].rearrange("p t f -> p (t f)")[:, 0:GP[0]], cut(GP[1])]

        LT, LA, LS, LX, LQ, LM, LZ, LG = 1, 2, 3, 4, 5, 5, 6, 7
        staged1 = sem("staged1")

        def messages(h):
            n_pairs = PAIRS[h]
            mine = slice(G0[h], G0[h] + GP[h])
            rech, idxh, dparth, tabrow = rec[:, mine], idx[:, mine], dpart[:, mine], tabrows[h]
            own = []

            def sem(name):
                own.append(nc.alloc_semaphore(name=name))
                return own[-1]

            split = sem(f"split_chain{h}")
            slots_ready = sem(f"slots_ready{h}")
            oh_ready = sem(f"oh_ready{h}")
            oh_tr = sem(f"oh_tr{h}")
            ohT_ready = sem(f"ohT_ready{h}")
            pre_ps = sem(f"pre_ps{h}")
            pre_sb = sem(f"pre_sb{h}")
            idx_st = sem(f"idx_staged{h}")
            gath = [sem(f"gathered{h}_{r}") for r in range(RB)]
            s_ready = sem(f"s_ready{h}")
            s_tr = sem(f"s_tr{h}")
            sT_ready = sem(f"sT_ready{h}")
            sq_done = sem(f"squares_done{h}")
            half_ready = sem(f"half_ready{h}")
            var_ready = sem(f"var_ready{h}")
            nrm = sem(f"norm_chain{h}")
            rstd_ready = sem(f"rstd_ready{h}")
            z_ps = sem(f"z_ps{h}")
            z_sb = sem(f"z_sb{h}")
            msg_ready = sem(f"msg_ready{h}")
            agg_ps = sem(f"agg_ps{h}")
            agg_add = sem(f"agg_add{h}")

            with nc.Block() as block:
                if h == 0:
                    @block.sync
                    def _(sp):
                        load_records(sp, 1)

                @block.gpsimd
                def _(pool):
                    nc.gpsimd.memset(half[:, :, :], -0.5).then_inc(half_ready, 1)
                    pool.wait_ge(half_ready, 1)
                    pool.wait_ge(slots_ready, 1)

                    def stage_idx(m):
                        i = m.mod(RB) // 4
                        n = 8 if not isinstance(m.it, int) else min(8, 2 * (n_pairs - m.c))
                        if not isinstance(m.it, int) or m.c >= RB:
                            for r in range(4 * i, 4 * i + 4):
                                pool.wait_ge(gath[r], m.per(RB, 32, 0))
                        nc.gpsimd.tensor_copy(stage_i[:, i * 8:i * 8 + n], idxh[:, bass.ds(m.of(2), n)]).then_inc(idx_st, 1)
                        wait_apart(pool, idx_st, m.per(4, 1, 1), passed_pool)

                    def gather(m):
                        r = m.mod(RB)
                        wait_apart(pool, s_ready, m.of(2, 2 - 2 * RB), passed_pool)
                        for u in range(2):
                            c = (r * 2 + u)
                            pool.indirect_dma_start(bg[:, r, u, :], None, dstd,
                                                    bass.IndirectOffsetOnAxis(ap=stage_i[:, c:c + 1], axis=0)).then_inc(gath[r], 16)

                    def rsqrt(m):
                        r = m.mod(RE)
                        n = 2 if not isinstance(m.it, int) else min(2, n_pairs - m.c)
                        pool.wait_ge(var_ready, m.per(2, 1, 1))
                        nc.gpsimd.tensor_tensor(rstd[:, r:r + n, :], var[:, m.mod(4) // 2, 0:n, :], half[:, 0:n, :],
                                                ALU.pow).then_inc(rstd_ready, 1)

                    def place(m):
                        i, c = m.mod(8) // 4, m.mod(4)
                        if c == 0:
                            stage_records(pool, 1, m, i, m.per(8, 16 * SC[1], 0), staged1, scat[1])
                            wait_apart(pool, staged1, m.per(4, 2, 2), passed_pool)
                        for k in ((0, 1), (2,), (3,), (4,))[c]:
                            scatter_column(pool, 1, i, k, scat[1])

                    def step(m):
                        if m.within(n_pairs):
                            if m.mod(4) == 0:
                                stage_idx(m)
                            gather(m)
                            if h == 0 and m.within(n_pairs // 8 * 8):
                                place(m)
                        q = m - AHEAD
                        if q.within(n_pairs) and q.mod(2) == 0:
                            rsqrt(q)

                    AHEAD = 5
                    pipeline(pool, n_pairs, AHEAD, RE, step, peel=2)
                    if h == 0:
                        for i in range(2):
                            pool.wait_ge(scat[1][i], 16 * ECP[1] // 2)
                        pool.sem_inc(scat_done, 1)

                @block.vector
                def _(dve):
                    v = nc.vector
                    done = [0]

                    def link(ins):
                        done[0] += 1
                        ins.then_inc(split, 1)
                        dve.wait_ge(split, done[0])

                    v.tensor_copy(idxh, rech[:, :, 1]).then_inc(slots_ready, 1)
                    link(v.tensor_copy(dparth[:, :, 0], rech[:, :, 2]))
                    link(v.tensor_tensor(dres[h], rech[:, :, 2], dparth[:, :, 0], ALU.subtract))
                    link(v.tensor_copy(dparth[:, :, 1], dres[h]))
                    link(v.tensor_tensor(dres[h], dres[h], dparth[:, :, 1], ALU.subtract))
                    link(v.tensor_copy(dparth[:, :, 2], dres[h]))
                    if h == 0:
                        link(v.memset(agg[:, :, :], 0.0))
                    regs = [v.alloc_register(f"block_of_tile{h}_{j}") for j in range(16)]
                    offs = [None] * 16

                    def enter(it):
                        if isinstance(it, int) and it == 0:
                            return
                        v.load(regs, tabrow[0:1, bass.ds(it * 16 + PADT - 16, 16)])
                        offs[:] = [v.snap(r, min_val=0, max_val=(BK - 1) * D) for r in regs]

                    aggf = agg[:, :, :].rearrange("p t f -> p (t f)")

                    def add_sums(a, u):
                        wait(dve, agg_add, a.of(2, u))
                        d = aggf[0:NB, bass.ds(offs[2 * a.mod(RE) + u], D)]
                        v.tensor_tensor(d, d, ps[0:NB, 7, u * D:(u + 1) * D], ALU.add).then_inc(agg_add, 1)

                    def norm(m, part):
                        if not (m.within(n_pairs) and m.mod(2) == 0):
                            return
                        r = m.mod(RE)
                        n = 2 if not isinstance(m.it, int) else min(2, n_pairs - m.c)
                        me, va = mean[:, 0:n, :], var[:, m.mod(4) // 2, 0:n, :]
                        if part:
                            dve.wait_ge(nrm, m.per(2, 2, part))
                        else:
                            dve.wait_ge(sq_done, m.of(2, 2 * n))
                            wait(dve, rstd_ready, m.per(2, 1, -1))
                        if part == 0:
                            v.scalar_tensor_tensor(out=me, in0=ssum[:, r:r + n, :], scalar=1.0 / D ** 2, in1=ssum[:, r:r + n, :],
                                                   op0=ALU.mult, op1=ALU.mult).then_inc(nrm, 1)
                        elif part == 1:
                            v.scalar_tensor_tensor(out=va, in0=ssq[:, r:r + n, :], scalar=1.0 / D, in1=me,
                                                   op0=ALU.mult, op1=ALU.subtract).then_inc(nrm, 1)
                        else:
                            v.tensor_scalar(va, va, 0.0, EPS, ALU.max, ALU.add).then_inc(var_ready, 1)

                    def step(m):
                        g, z, b, q = m - RE, m - LZ, m - LA, m - LQ
                        norm(q, 0)
                        if g.within(n_pairs):
                            dve.wait_ge(agg_ps, g.of(1, 1))
                            add_sums(g, 0)
                        norm(q, 1)
                        if m.within(n_pairs):
                            r = m.mod(RE)
                            wait(dve, agg_ps, m.of(1, 1 - RE))
                            t = bass.ds(m.of(2), 2)
                            v.tensor_tensor(eh[:, r, :, 0:NB], iota_n[:, :].unsqueeze(1).to_broadcast([P, 2, NB]),
                                            rech[:, t, 0:1].to_broadcast([P, 2, NB]), ALU.is_equal)
                            norm(q, 2)
                            v.tensor_copy(eh[:, r, :, NB:P], dparth[:, t, :]).then_inc(oh_ready, 1)
                        else:
                            norm(q, 2)
                        if g.within(n_pairs):
                            add_sums(g, 1)
                        if z.within(n_pairs):
                            s = z.mod(2)
                            dve.wait_ge(z_ps, z.of(1, 1))
                            dve.wait_ge(rstd_ready, z.per(2, 1, 1))
                            wait(dve, msg_ready, z.of(1, 0))
                            for u in range(2):
                                last = v.scalar_tensor_tensor(out=zb[:, u], in0=ps[:, 5 + s, u * D:(u + 1) * D],
                                                              scalar=rstd[:, z.mod(RE), u:u + 1], in1=b2c[:, :],
                                                              op0=ALU.mult, op1=ALU.add)
                            last.then_inc(z_sb, 1)
                        if b.within(n_pairs):
                            r, s = b.mod(RB), b.mod(2)
                            dve.wait_ge(pre_ps, b.of(1, 1))
                            dve.wait_ge(gath[r], b.per(RB, 32, 32))
                            v.tensor_tensor(bg[:, r].rearrange("p u n -> p (u n)"), ps[:, 1 + s, :],
                                            bg[:, r].rearrange("p u n -> p (u n)"), ALU.add).then_inc(pre_sb, 1)

                    pipeline(dve, n_pairs, RE, RE, step, enter, peel=2)

                @block.scalar
                def _(act):
                    def step(m):
                        a = m - LT
                        if a.within(n_pairs):
                            act.wait_ge(oh_tr, a.of(1, 1))
                            wait(act, pre_ps, a.of(1, -1))
                            nc.scalar.activation(ohT[:, a.mod(2)], ps[:, 0, 0:D].rearrange("p (u n) -> p u n", u=2),
                                                 ACT.Copy).then_inc(ohT_ready, 1)
                        a = m - LZ
                        if a.within(n_pairs):
                            act.wait_ge(z_sb, a.of(1, 1))
                            wait(act, agg_ps, a.of(1, -1))
                            nc.scalar.activation(msg[:, a.mod(2)], zb[:, :, :], ACT.Silu).then_inc(msg_ready, 1)
                        a = m - LS
                        if a.within(n_pairs):
                            act.wait_ge(s_ready, a.of(2, 2))
                            for u in range(2):
                                wait(act, sq_done, a.of(2, u))
                                nc.scalar.activation(junk, sa[:, a.mod(RT), u], ACT.Square,
                                                     accum_out=ssq[:, a.mod(RE), u:u + 1]).then_inc(sq_done, 1)
                        a = m - LX
                        if a.within(n_pairs):
                            act.wait_ge(s_tr, a.of(1, 1))
                            wait(act, z_ps, a.of(1, 1 - RT))
                            nc.scalar.activation(sT[:, a.mod(RT)].rearrange("p u k n -> p (u k n)"), ps[:, 3 + a.mod(2), :],
                                                 ACT.Copy).then_inc(sT_ready, 1)
                        a = m - LA
                        if a.within(n_pairs):
                            act.wait_ge(pre_sb, a.of(1, 1))
                            wait(act, s_tr, a.of(1, 1 - RT))
                            wait(act, sq_done, a.of(2, 2 - 2 * RT))
                            wait(act, rstd_ready, a.per(2, 1, 1 - RE // 2))
                            for u in range(2):
                                nc.scalar.activation(sa[:, a.mod(RT), u], bg[:, a.mod(RB), u], ACT.Silu,
                                                     accum_out=ssum[:, a.mod(RE), u:u + 1]).then_inc(s_ready, 1)

                    pipeline(act, n_pairs, RE, RE, step, peel=2)

                @block.tensor
                def _(pe):
                    t_ = nc.tensor
                    regs = [t_.alloc_register(f"block_of_tile{h}_{j}") for j in range(16)]
                    offs = [None] * 16

                    def enter(it):
                        t_.load(regs, tabrow[0:1, bass.ds(it * 16 + PADT - 2 * LA, 16)])
                        offs[:] = [t_.snap(r, min_val=0, max_val=(BK - 1) * D) for r in regs]

                    def step(m):
                        a = m - LT
                        if a.within(n_pairs):
                            s = a.mod(2)
                            pe.wait_ge(oh_ready, a.of(1, 1))
                            wait(pe, ohT_ready, a.of(1, 0))
                            for u in range(2):
                                last = t_.transpose(ps[:, 0, u * P:(u + 1) * P], eh[:, a.mod(RE), u], ident[:, :])
                            last.then_inc(oh_tr, 1)
                        a = m - LA
                        if a.within(n_pairs):
                            s = a.mod(2)
                            pe.wait_ge(ohT_ready, a.of(1, 1))
                            wait(pe, pre_sb, a.of(1, -1))
                            for u in range(2):
                                o = offs[(2 * (a.mod(RE) + LA) + u) % 16]
                                for k in range(3):
                                    last = t_.matmul(ps[:, 1 + s, u * D:(u + 1) * D], ohT[:, s, u], ablk[:, k, bass.ds(o, D)],
                                                     start=(k == 0), stop=(k == 2))
                            last.then_inc(pre_ps, 1)
                        a = m - LX
                        if a.within(n_pairs):
                            s = a.mod(2)
                            pe.wait_ge(s_ready, a.of(2, 2))
                            wait(pe, sT_ready, a.of(1, -1))
                            for u in range(2):
                                for k in range(KC):
                                    c = (u * KC + k) * P
                                    last = t_.transpose(ps[:, 3 + s, c:c + P], sa[:, a.mod(RT), u, k * P:(k + 1) * P], ident[:, :])
                            last.then_inc(s_tr, 1)
                        a = m - LM
                        if a.within(n_pairs):
                            s = a.mod(2)
                            pe.wait_ge(sT_ready, a.of(1, 1))
                            wait(pe, z_sb, a.of(1, -1))
                            for u in range(2):
                                for k in range(KC):
                                    last = t_.matmul(ps[:, 5 + s, u * D:(u + 1) * D], sT[:, a.mod(RT), u, k], W2c[:, k],
                                                     start=(k == 0), stop=(k == KC - 1))
                            last.then_inc(z_ps, 1)
                        a = m - LG
                        if a.within(n_pairs):
                            pe.wait_ge(msg_ready, a.of(1, 1))
                            wait(pe, agg_add, a.of(2, 0))
                            for u in range(2):
                                last = t_.matmul(ps[0:NB, 7, u * D:(u + 1) * D], eh[:, a.mod(RE), u, 0:NB], msg[:, a.mod(2), u],
                                                 start=True, stop=True)
                            last.then_inc(agg_ps, 1)

                    pipeline(pe, n_pairs, RE, RE, step, enter)

            nc.clear_and_free_semaphores(own)
            nc.all_engine_barrier()

        for h in range(2):
            messages(h)

        wts = ablk[:, :, :].rearrange("p k n -> p (k n)").bitcast(f32)
        wat = [0]

        def wcut(floats, shape=None, **dims):
            a = wts[:, wat[0]:wat[0] + floats]
            wat[0] += floats
            assert wat[0] <= 3 * BK * D // 2
            return a.rearrange(shape, **dims) if shape else a

        uW1s = wcut(2 * KC * D, "p (k n) -> p k n", k=2 * KC)
        uW2s = wcut(KC * D, "p (k n) -> p k n", k=KC)
        w1s = wcut(X * KC * D, "p (k e n) -> p k e n", e=X, k=KC)
        w2s = wcut(X * KC * D, "p (k e n) -> p k e n", e=X, k=KC)
        b1b = wcut(X * D)
        b2b = wcut(X * D)
        rws = wcut(KC * X, "p (k e) -> p k e", k=KC)
        rwr = wcut(D)
        ub1T = wcut(KC)
        lg = wcut(BK * X, "p (t e) -> p t e", t=BK)
        pr = wcut(BK * X, "p (t e) -> p t e", t=BK)
        oh1 = wcut(BK * X, "p (t e) -> p t e", t=BK)
        oh2 = wcut(BK * X, "p (t e) -> p t e", t=BK)
        cand = wcut(BK * X, "p (t e) -> p t e", t=BK)
        iox = wcut(X)
        m1 = wcut(BK)
        m2 = wcut(BK)
        isel = wcut(BK)
        rsum = wcut(BK)
        mv3 = wcut(BK * 2, "p (t s) -> p t s", t=BK)

        def two(shape="p (u n) -> p u n", floats=2 * D, **dims):
            return [cut(floats, shape, **dims) for _ in range(2)]

        cut(0, restart=True)
        xp = two(u=2)
        hp = two(u=2)
        xh = two(u=2)
        catT = two("p (k n) -> p k n", 2 * KC * 2 * NB, k=2 * KC)
        y1T = two("p (k n) -> p k n", KC * 2 * NB, k=KC)
        aggcp = two(u=2)
        raw3 = cut(12, "p (u s) -> p u s", u=2)
        pair3 = cut(4, "p (u s) -> p u s", u=2)

        padrow = cut(XD * XW, "p (d w) -> p d w", d=XD)
        padrow_set = sem("padrow_set")
        xpads_out = sem("routed_pads_out")
        uw_in = sem("uw_in")
        fw_in = sem("fw_in")
        xp_in = [sem("xp_in0"), sem("xp_in1")]
        hp_ready = sem("hp_ready")
        xh_ready = sem("xh_ready")
        cat_tr = sem("cat_tr")
        catT_h = sem("catT_h")
        catT_a = sem("catT_a")
        y1_ps = sem("y1_ps")
        y1_ready = sem("y1_ready")
        y2_ps = sem("y2_ps")
        x1_ready = sem("x1_ready")
        raw3_ready = sem("raw3_ready")
        mv3_ready = sem("mv3_ready")
        pair3_ready = sem("pair3_ready")
        x1_kept = sem("x1_kept")
        sx = sem("xh_chain")
        aggcp_ready = sem("aggcp_ready")

        n_ = slice(0, NB)

        with nc.Block() as block:
            @block.sync
            def _(sp):
                sp.dma_start(uW1s, uW1.rearrange("(k p) n -> p k n", p=P)).then_inc(uw_in, 16)
                sp.dma_start(uW2s, uW2.rearrange("(k p) n -> p k n", p=P)).then_inc(uw_in, 16)
                sp.dma_start(ub1T, ub1.rearrange("(k p) -> p k", p=P)).then_inc(uw_in, 16)
                sp.wait_ge(padrow_set, 2)
                xsv = xsd.rearrange("(g p) f -> p g f", p=P)

                def empty_slots(m):
                    half = padrow[:, XD // 2 * m.mod(2):XD // 2 * (m.mod(2) + 1)]
                    sp.dma_start(xsv[:, bass.ds(m.of(XD // 2), XD // 2), :], half).then_inc(xpads_out, 16)

                def step(m):
                    s = m.mod(2)
                    if m.within(NP2):
                        wait(sp, xh_ready, m.of(1, -1))
                        sp.dma_start(xp[s][n_], x[bass.ds(m.of(2 * NB), 2 * NB), :].rearrange("(u p) f -> p u f", p=NB)).then_inc(xp_in[s], 16)
                        empty_slots(m)
                pipeline(sp, NP2, 0, 2, step)
                for g in range(NP2 * XD // 2, XT, XD // 2):
                    d, o = min(XD // 2, XT - g), g % XD
                    sp.dma_start(xsv[:, g:g + d, :], padrow[:, o:o + d]).then_inc(xpads_out, 16)
                for k in range(KC):
                    sp.dma_start(w1s[:, k], w1[:, k * P:(k + 1) * P, :].rearrange("e p n -> p e n")).then_inc(fw_in, 16)
                    sp.dma_start(w2s[:, k], w2[:, k * P:(k + 1) * P, :].rearrange("e p n -> p e n")).then_inc(fw_in, 16)
                sp.dma_start(rwr[0:X], router_w).then_inc(fw_in, 16)
                sp.dma_start(b1b, b1.rearrange("e n -> (e n)").partition_broadcast(P)).then_inc(fw_in, 16)
                sp.dma_start(b2b, b2.rearrange("e n -> (e n)").partition_broadcast(P)).then_inc(fw_in, 16)
                sp.wait_ge(fw_in, 16 * (2 * KC + 3))
                sp.wait_ge(xpads_out, 16 * -(-XT // (XD // 2)))


            @block.gpsimd
            def _(pool):
                nc.gpsimd.memset(padrow, 0.0).then_inc(padrow_set, 1)
                pool.wait_ge(padrow_set, 1)
                nc.gpsimd.iota(padrow[:, :, D].bitcast(i32), pattern=[[P, XD]], base=K2 * N,
                               channel_multiplier=1).then_inc(padrow_set, 1)

                def step(m):
                    s = m.mod(2)
                    if m.within(NP2):
                        wait(pool, cat_tr, m.of(1, -1))
                        nc.gpsimd.tensor_copy(aggcp[s][n_], agg[n_, bass.ds(m.of(2), 2), :]).then_inc(aggcp_ready, 1)
                        pool.wait_ge(hp_ready, m.of(1, 1))
                        wait(pool, x1_kept, m.of(1, -1))
                        wait(pool, mv3_ready, m.of(1, -1))
                        nc.gpsimd.tensor_tensor(xh[s][n_], xp[s][n_], hp[s][n_], ALU.add).then_inc(sx, 1)
                        pool.wait_ge(sx, m.of(1, 1))
                        nc.gpsimd.tensor_tensor(xh[s][n_], xh[s][n_],
                                                ub2b[n_, :].unsqueeze(1).to_broadcast([NB, 2, D]), ALU.add).then_inc(xh_ready, 1)
                pipeline(pool, NP2, 0, 2, step)

            @block.vector
            def _(dve):
                v = nc.vector

                def step(m):
                    s = m.mod(2)
                    if m.within(NP2):
                        dve.wait_ge(xp_in[s], m.per(2, 16, 16))
                        wait(dve, cat_tr, m.of(1, -1))
                        wait(dve, xh_ready, m.of(1, -1))
                        for u in range(2):
                            t = bass.ds(m.of(2, u), 1)
                            last = v.tensor_scalar(hp[s][n_, u], xp[s][n_, u], mv1[n_, t, 0], mv1[n_, t, 1],
                                                   ALU.subtract, ALU.mult)
                        last.then_inc(hp_ready, 1)
                    if m.within(NP2):
                        dve.wait_ge(cat_tr, m.of(1, 1))
                        wait(dve, y1_ps, m.of(1, -1))
                        v.tensor_copy(catT[s][:, KC:2 * KC, :],
                                      ps[:, 1, 0:4 * NB].rearrange("p (k n) -> p k n", k=KC)).then_inc(catT_a, 1)
                    a = m - 1
                    if a.within(NP2):
                        r = a.mod(2)
                        dve.wait_ge(y2_ps, a.of(1, 1))
                        dve.wait_ge(xh_ready, a.of(1, 1))
                        v.tensor_tensor(xh[r][n_].rearrange("p u n -> p (u n)"), ps[n_, 4, :],
                                        xh[r][n_].rearrange("p u n -> p (u n)"), ALU.add).then_inc(x1_ready, 1)
                        dve.wait_ge(x1_ready, a.of(1, 1))
                        for u in range(2):
                            v.bn_stats(raw3[n_, u], xh[r][n_, u]).then_inc(raw3_ready, 1)
                        wait_apart(dve, raw3_ready, a.of(2, 2), passed_dve)
                        for u in range(2):
                            v.bn_aggr(pair3[n_, u], raw3[n_, u]).then_inc(pair3_ready, 1)
                        dve.wait_ge(pair3_ready, a.of(2, 2))
                        v.tensor_copy(mv3[n_, bass.ds(a.of(2), 2), :], pair3[n_]).then_inc(mv3_ready, 1)
                        dve.wait_ge(mv3_ready, a.of(1, 1))

                pipeline(dve, NP2, 1, 2, step)

            @block.scalar
            def _(act):
                act.wait_ge(uw_in, 48)

                def step(m):
                    s = m.mod(2)
                    if m.within(NP2):
                        act.wait_ge(cat_tr, m.of(1, 1))
                        wait(act, y1_ps, m.of(1, -1))
                        nc.scalar.activation(catT[s][:, 0:KC, :], ps[:, 0, 0:4 * NB].rearrange("p (k n) -> p k n", k=KC),
                                             ACT.Copy).then_inc(catT_h, 1)
                        act.wait_ge(y1_ps, m.of(1, 1))
                        wait(act, y2_ps, m.of(1, -1))
                        for k in range(KC):
                            last = nc.scalar.activation(y1T[s][:, k], ps[:, 2 + k, 0:2 * NB], ACT.Silu,
                                                        bias=ub1T[:, k:k + 1])
                        last.then_inc(y1_ready, 1)
                    a = m - 1
                    if a.within(NP2):
                        act.wait_ge(x1_ready, a.of(1, 1))
                        nc.scalar.activation(agg[n_, bass.ds(a.of(2), 2), :], xh[a.mod(2)][n_], ACT.Copy).then_inc(x1_kept, 1)
                pipeline(act, NP2, 1, 2, step)

            @block.tensor
            def _(pe):
                t_ = nc.tensor
                pe.wait_ge(uw_in, 48)
                aggf = agg[:, :, :].rearrange("p t f -> p (t f)")

                def step(m):
                    s = m.mod(2)
                    if m.within(NP2):
                        pe.wait_ge(hp_ready, m.of(1, 1))
                        wait(pe, catT_h, m.of(1, 0))
                        wait(pe, catT_a, m.of(1, 0))
                        for u in range(2):
                            for k in range(KC):
                                c = k * 2 * NB + u * NB
                                t_.transpose(ps[:, 0, c:c + NB], hp[s][n_, u, k * P:(k + 1) * P], ident[n_, n_])
                        pe.wait_ge(aggcp_ready, m.of(1, 1))
                        for u in range(2):
                            for k in range(KC):
                                c = k * 2 * NB + u * NB
                                last = t_.transpose(ps[:, 1, c:c + NB], aggcp[s][n_, u, k * P:(k + 1) * P], ident[n_, n_])
                        last.then_inc(cat_tr, 1)
                    a = m - 1
                    if a.within(NP2):
                        r = a.mod(2)
                        pe.wait_ge(y1_ready, a.of(1, 1))
                        wait(pe, x1_ready, a.of(1, 0))
                        for u in range(2):
                            for k in range(KC):
                                last = t_.matmul(ps[n_, 4, u * D:(u + 1) * D], y1T[r][:, k, u * NB:(u + 1) * NB], uW2s[:, k],
                                                 start=(k == 0), stop=(k == KC - 1))
                        last.then_inc(y2_ps, 1)
                    if m.within(NP2):
                        pe.wait_ge(catT_h, m.of(1, 1))
                        pe.wait_ge(catT_a, m.of(1, 1))
                        wait(pe, y1_ready, m.of(1, 0))
                        for f in range(KC):
                            for k in range(2 * KC):
                                last = t_.matmul(ps[:, 2 + f, 0:2 * NB], uW1s[:, k, f * P:(f + 1) * P], catT[s][:, k],
                                                 start=(k == 0), stop=(k == 2 * KC - 1))
                        last.then_inc(y1_ps, 1)
                pipeline(pe, NP2, 1, 2, step)

        cut(0, restart=True)
        tb = two(u=2)
        tT = two("p (k n) -> p k n", KC * 2 * NB, k=KC)
        taken = cut(X * K2 * BK, "p (e k t) -> p e k t", e=X, k=K2)
        slot = cut(X * K2 * BK, "p (e k t) -> p e k t", e=X, k=K2)
        onex = cut(X * K2 * BK)
        tri2 = cut(P)
        ones2 = cut(P)
        xcnt = cut(X)
        xtiles = cut(X)
        xtilesi = cut(X, dt=i32)
        xstart = cut(X)
        xbase = cut(X)
        xcmp = cut(X)
        xtab = cut(1)
        xtabi = cut(1, dt=i32)
        pidx = cut(1)
        xposf = cut(K2 * BK, "p (k t) -> p k t", k=K2)
        xposi = rec[:, :, :].rearrange("p g f -> p (g f)")[:, 0:K2 * BK].bitcast(i32).rearrange("p (t k) -> p t k", k=K2)
        home = idx[:, 0:K2 * BK].rearrange("p (t k) -> p t k", k=K2)

        var3 = sem("var3_ready")
        std3 = sem("std3_ready")
        rstd3 = sem("rstd3_ready")
        rw_tr = sem("rw_tr")
        rwT_ready = sem("rwT_ready")
        tb_ready = sem("tb_ready")
        tb_tr = sem("tb_tr")
        tT_ready = sem("tT_ready")
        lg_ps = sem("lg_ps")
        lg_ready = sem("lg_ready")
        iox_ready = sem("iox_ready")
        tk = sem("top2_chain")
        sh_ready = sem("shifted_ready")
        ex_ready = sem("exp_ready")
        xcnt_ready = sem("xcnt_ready")
        xpre_ready = sem("xpre_ready")
        xtab_ready = sem("xtab_ready")
        xtab_out = sem("xtab_out")
        xtab_in = sem("xtab_in")

        with nc.Block() as block:
            @block.gpsimd
            def _(pool):
                nc.gpsimd.iota(iox, pattern=[[1, X]], base=0, channel_multiplier=0,
                               allow_small_or_imprecise_dtypes=True).then_inc(iox_ready, 1)
                nc.gpsimd.iota(pidx, pattern=[[1, 1]], base=0, channel_multiplier=1,
                               allow_small_or_imprecise_dtypes=True).then_inc(iox_ready, 1)
                nc.gpsimd.iota(home, pattern=[[K2 * NB, BK], [1, K2]], base=0, channel_multiplier=K2).then_inc(iox_ready, 1)
                nc.gpsimd.memset(onex, 1.0).then_inc(iox_ready, 1)
                nc.gpsimd.memset(ones2, 1.0).then_inc(iox_ready, 1)
                pool.wait_ge(iox_ready, 5)
                nc.gpsimd.affine_select(out=tri2, in_=ones2, compare_op=ALU.is_gt, fill=0.0,
                                        base=0, pattern=[[1, P]], channel_multiplier=-1).then_inc(iox_ready, 1)

            @block.sync
            def _(sp):
                sp.wait_ge(xtab_ready, 1)
                sp.dma_start(xtabd, xtabi).then_inc(xtab_out, 16)
                sp.wait_ge(xtab_out, 16)
                sp.dma_start(tabrows[0][0:1, PADT:PADT + P],
                             xtabd.rearrange("p k -> (p k)").rearrange("(a n) -> a n", a=1)).then_inc(xtab_in, 16)
                sp.wait_ge(xtab_in, 16)

            @block.vector
            def _(dve):
                v = nc.vector
                v.tensor_scalar(mv3[n_, :, 1], mv3[n_, :, 1], EPS, None, ALU.add).then_inc(var3, 1)
                dve.wait_ge(std3, 1)
                v.reciprocal(mv3[n_, :, 1], mv3[n_, :, 1]).then_inc(rstd3, 1)
                dve.wait_ge(rstd3, 1)

                def step(m):
                    s = m.mod(2)
                    if m.within(NP2):
                        wait(dve, tb_tr, m.of(1, -1))
                        for u in range(2):
                            t = bass.ds(m.of(2, u), 1)
                            last = v.tensor_scalar(tb[s][n_, u], agg[n_, t, :].rearrange("p t f -> p (t f)"),
                                                   mv3[n_, t, 0], mv3[n_, t, 1], ALU.subtract, ALU.mult)
                        last.then_inc(tb_ready, 1)
                pipeline(dve, NP2, 0, 2, step)

                done = [0]

                def link(ins):
                    done[0] += 1
                    ins.then_inc(tk, 1)
                    dve.wait_ge(tk, done[0])

                def wide(a):
                    return a[n_].unsqueeze(2).to_broadcast([NB, BK, X])

                iow = iox[n_].unsqueeze(1).to_broadcast([NB, BK, X])
                dve.wait_ge(lg_ready, NP2)
                dve.wait_ge(iox_ready, 6)
                link(v.tensor_reduce(out=m1[n_], in_=lg[n_], axis=AX.X, op=ALU.max))
                v.tensor_tensor(lg[n_], lg[n_], wide(m1), ALU.subtract).then_inc(sh_ready, 1)
                dve.wait_ge(ex_ready, 1)
                link(v.tensor_reduce(out=rsum[n_], in_=pr[n_], axis=AX.X, op=ALU.add))
                link(v.reciprocal(rsum[n_], rsum[n_]))
                link(v.tensor_tensor(pr[n_], pr[n_], wide(rsum), ALU.mult))
                for top, oh in ((m1, oh1), (m2, oh2)):
                    link(v.tensor_reduce(out=top[n_], in_=pr[n_], axis=AX.X, op=ALU.max))
                    link(v.tensor_tensor(cand[n_], pr[n_], wide(top), ALU.is_lt))
                    link(v.scalar_tensor_tensor(out=cand[n_], in0=cand[n_], scalar=float(X), in1=iow,
                                                op0=ALU.mult, op1=ALU.add))
                    link(v.tensor_reduce(out=isel[n_], in_=cand[n_], axis=AX.X, op=ALU.min))
                    link(v.tensor_tensor(oh[n_], iow, wide(isel), ALU.is_equal))
                    if oh is oh1:
                        link(v.scalar_tensor_tensor(out=pr[n_], in0=oh[n_], scalar=-2.0, in1=pr[n_],
                                                    op0=ALU.mult, op1=ALU.add))
                link(v.tensor_tensor(rsum[n_], m1[n_], m2[n_], ALU.add))
                link(v.tensor_scalar(rsum[n_], rsum[n_], 1e-12, None, ALU.max))
                link(v.reciprocal(rsum[n_], rsum[n_]))
                link(v.tensor_tensor(m1[n_], m1[n_], rsum[n_], ALU.mult))
                link(v.tensor_tensor(m2[n_], m2[n_], rsum[n_], ALU.mult))
                for k, oh in ((0, oh1), (1, oh2)):
                    link(v.tensor_copy(taken[n_, :, k, :], oh[n_].rearrange("p t e -> p e t")))
                v.tensor_reduce(out=xcnt[n_], in_=taken[n_].rearrange("p e k t -> p e (k t)"), axis=AX.X,
                                op=ALU.add).then_inc(xcnt_ready, 1)
                takf, slotf = (a.rearrange("p e k t -> p (e k t)") for a in (taken[n_], slot[n_]))
                link(v.tensor_tensor_scan(slotf, onex[n_], takf, 0.0, ALU.mult, ALU.add))
                dve.wait_ge(xpre_ready, 2)
                link(v.tensor_scalar(xtilesi, ps[:, 5, 0:X], float(P - 1), None, ALU.add))
                link(v.tensor_scalar(xtilesi, xtilesi, 7, None, ALU.arith_shift_right))
                link(v.tensor_copy(xtiles, xtilesi))
                link(v.tensor_tensor_scan(xstart, onex[:, 0:X], xtiles, 0.0, ALU.mult, ALU.add))
                link(v.tensor_tensor(xstart, xstart, xtiles, ALU.subtract))
                link(v.tensor_scalar(xcmp, xstart, pidx, None, ALU.is_le))
                link(v.tensor_reduce(out=xtab, in_=xcmp, axis=AX.X, op=ALU.add))
                v.tensor_scalar(xtabi, xtab, -1.0, float(D), ALU.add, ALU.mult).then_inc(xtab_ready, 1)
                link(v.tensor_scalar(xbase[n_], xstart[n_], float(P), -1.0, ALU.mult, ALU.add))
                link(v.tensor_tensor(xbase[n_], xbase[n_], ps[n_, 4, 0:X], ALU.add))
                link(v.tensor_tensor(xbase[n_], xbase[n_], slot[n_, :, 0, 0], ALU.subtract))
                link(v.tensor_tensor(xbase[n_], xbase[n_], taken[n_, :, 0, 0], ALU.add))
                link(v.tensor_tensor(slot[n_].rearrange("p e k t -> p e (k t)"), slot[n_].rearrange("p e k t -> p e (k t)"),
                                     xbase[n_].unsqueeze(2).to_broadcast([NB, X, K2 * BK]), ALU.add))
                link(v.tensor_tensor(slotf, slotf, takf, ALU.mult))
                link(v.tensor_reduce(out=xposf[n_].rearrange("p k t -> p (k t)"),
                                     in_=slot[n_].rearrange("p e k t -> p (k t) e"), axis=AX.X, op=ALU.add))
                link(v.tensor_copy(xposi[n_], xposf[n_].rearrange("p k t -> p t k")))

            @block.scalar
            def _(act):
                act.wait_ge(var3, 1)
                nc.scalar.activation(mv3[n_, :, 1], mv3[n_, :, 1], ACT.Sqrt).then_inc(std3, 1)
                act.wait_ge(rw_tr, 1)
                nc.scalar.activation(rws, ps[:, 7, 0:KC * X].rearrange("p (k e) -> p k e", k=KC), ACT.Copy).then_inc(rwT_ready, 1)

                def step(m):
                    if m.within(NP2):
                        s = m.mod(2)
                        act.wait_ge(tb_tr, m.of(1, 1))
                        wait(act, lg_ps, m.of(1, -1))
                        nc.scalar.activation(tT[s], ps[:, s, 0:4 * NB].rearrange("p (k n) -> p k n", k=KC),
                                             ACT.Copy).then_inc(tT_ready, 1)
                    a = m - 1
                    if a.within(NP2):
                        s = a.mod(2)
                        act.wait_ge(lg_ps, a.of(1, 1))
                        nc.scalar.activation(lg[n_, bass.ds(a.of(2), 2), :],
                                             ps[n_, 2 + s, 0:2 * X].rearrange("p (u e) -> p u e", u=2), ACT.Copy).then_inc(lg_ready, 1)
                pipeline(act, NP2, 1, 2, step)
                act.wait_ge(sh_ready, 1)
                nc.scalar.activation(pr[n_], lg[n_], ACT.Exp).then_inc(ex_ready, 1)

            @block.tensor
            def _(pe):
                t_ = nc.tensor
                for k in range(KC):
                    last = t_.transpose(ps[:, 7, k * X:(k + 1) * X], rwr[0:X, k * P:(k + 1) * P], ident[0:X, 0:X])
                last.then_inc(rw_tr, 1)
                pe.wait_ge(rwT_ready, 1)

                def step(m):
                    if m.within(NP2):
                        s = m.mod(2)
                        pe.wait_ge(tb_ready, m.of(1, 1))
                        wait(pe, tT_ready, m.of(1, -1))
                        for u in range(2):
                            for k in range(KC):
                                c = k * 2 * NB + u * NB
                                last = t_.transpose(ps[:, s, c:c + NB], tb[s][n_, u, k * P:(k + 1) * P], ident[n_, n_])
                        last.then_inc(tb_tr, 1)
                    a = m - 1
                    if a.within(NP2):
                        s = a.mod(2)
                        pe.wait_ge(tT_ready, a.of(1, 1))
                        wait(pe, lg_ready, a.of(1, -1))
                        for u in range(2):
                            for k in range(KC):
                                last = t_.matmul(ps[n_, 2 + s, u * X:(u + 1) * X], tT[s][:, k, u * NB:(u + 1) * NB], rws[:, k],
                                                 start=(k == 0), stop=(k == KC - 1))
                        last.then_inc(lg_ps, 1)
                pipeline(pe, NP2, 1, 2, step)
                pe.wait_ge(xcnt_ready, 1)
                t_.matmul(ps[:, 4, 0:X], tri2[n_, :], xcnt[n_], start=True, stop=True).then_inc(xpre_ready, 1)
                t_.matmul(ps[:, 5, 0:X], ones2[n_], xcnt[n_], start=True, stop=True).then_inc(xpre_ready, 1)

        XP = XT // 2
        RX, RY, RS = 8, 4, 4
        L1, L2H, L2 = 1, 2, 3
        cut(0, restart=True)
        ts = cut(RS * K2 * XW, "p (r k w) -> p r k w", r=RS, k=K2)
        tslot = cut(RS * K2, "p (r k) -> p r k", dt=i32, r=RS)
        xs = cut(RX * 2 * XW, "p (r u w) -> p r u w", r=RX, u=2)
        yb = cut(RY * 2 * D, "p (r u n) -> p r u n", r=RY, u=2)
        xsT = cut(2 * 2 * D, "p (r n) -> p r n", r=2)
        hb = cut(2 * D, "p (u n) -> p u n", u=2)
        hg = cut(2 * 2 * D, "p (r u n) -> p r u n", r=2, u=2)
        hT = cut(2 * 2 * D, "p (r n) -> p r n", r=2)
        tsr = ts.bitcast(i32)
        xsr = xs.bitcast(i32)
        w1f = w1s.rearrange("p k e n -> p k (e n)")
        w2f = w2s.rearrange("p k e n -> p k (e n)")

        ts_parts = sem("ts_parts")
        ts_ready = sem("ts_ready")
        xt_added = sem("xt_added")
        ts_out = [sem(f"ts_out{r}") for r in range(RS)]
        xs_in = [sem(f"xs_in{r}") for r in range(RX)]
        xs_tr = sem("xs_tr")
        xsT_ready = sem("xsT_ready")
        h_ps = sem("h_ps")
        hb_ready = sem("hb_ready")
        hg_ready = sem("hg_ready")
        h_tr = sem("h_tr")
        hT_ready = sem("hT_ready")
        y_ps = sem("y_ps")
        yb_ready = sem("yb_ready")
        y_out = [sem(f"y_out{r}") for r in range(RY)]

        with nc.Block() as block:
            @block.sync
            def _(sp):
                for r in range(RS):
                    sp.wait_ge(ts_out[r], 16 * K2 * len(range(r, BK, RS)))

                def step(m):
                    r = m.mod(RX)
                    wait(sp, y_out[m.mod(RY)], m.per(RY, 32, -32))
                    sp.dma_start(xs[:, r], xsd[bass.ds(m.of(2 * P), 2 * P), :].rearrange("(u p) w -> p u w", p=P)).then_inc(xs_in[r], 16)
                pipeline(sp, XP, 0, RX, step)

            @block.gpsimd
            def _(pool):
                def route(m):
                    r = m.mod(RS)
                    wait_apart(pool, ts_ready, m.of(1, 1), passed_pool)
                    for k in range(K2):
                        pool.indirect_dma_start(xsd, bass.IndirectOffsetOnAxis(ap=tslot[n_, r, k:k + 1], axis=0),
                                                ts[n_, r, k], None).then_inc(ts_out[r], 16)
                pipeline(pool, BK, 0, RS, route)

                def step(m):
                    y = m - L2
                    if y.within(XP):
                        r = y.mod(RY)
                        wait_apart(pool, yb_ready, y.of(1, 1), passed_pool)
                        for u in range(2):
                            pool.indirect_dma_start(yd, bass.IndirectOffsetOnAxis(ap=xsr[:, y.mod(RX), u, D:XW], axis=0),
                                                    yb[:, r, u], None).then_inc(y_out[r], 16)
                pipeline(pool, XP, L2, RX, step)
                for r in range(RY):
                    pool.wait_ge(y_out[r], 32 * len(range(r, XP, RY)))

            @block.vector
            def _(dve):
                v = nc.vector

                def route(m):
                    r = m.mod(RS)
                    wait(dve, ts_out[r], m.per(RS, 16 * K2, 0))
                    wait(dve, xt_added, m.of(1, 1 - RS))
                    t = bass.ds(m.of(), 1)
                    v.tensor_scalar(ts[n_, r, :, 0:D], agg[n_, t, :].to_broadcast([NB, K2, D]),
                                    mv3[n_, t, 0], mv3[n_, t, 1], ALU.subtract, ALU.mult).then_inc(ts_parts, 1)
                    v.tensor_copy(tsr[n_, r, :, D], home[n_, t, :].rearrange("p t k -> p (t k)"))
                    v.tensor_copy(tslot[n_, r], xposi[n_, t, :].rearrange("p t k -> p (t k)")).then_inc(ts_ready, 1)
                    dve.wait_ge(ts_parts, m.of(1, 1))
                    v.tensor_tensor(agg[n_, t, :].rearrange("p t f -> p (t f)"), agg[n_, t, :].rearrange("p t f -> p (t f)"),
                                    ts[n_, r, 0, 0:D], ALU.add).then_inc(xt_added, 1)
                pipeline(dve, BK, 0, RS, route)

                regs = [v.alloc_register(f"expert_of_tile{j}") for j in range(2 * (RX + L2))]
                offs = [None] * (2 * (RX + L2))

                def enter(it):
                    v.load(regs, tabrows[0][0:1, bass.ds(it * (2 * RX) + PADT - 2 * L2, 2 * (RX + L2))])
                    offs[:] = [v.snap(r, min_val=0, max_val=(X - 1) * D) for r in regs]

                def step(m):
                    b = m.c % RX if isinstance(m.it, int) else m.c - RX
                    a = m - L1
                    if a.within(XP):
                        dve.wait_ge(h_ps, a.of(1, 1))
                        wait(dve, hg_ready, a.of(1, 0))
                        for u in range(2):
                            o = offs[2 * (b + L2 - L1) + u]
                            last = v.tensor_tensor(hb[:, u], ps[:, 1, u * D:(u + 1) * D], b1b[:, bass.ds(o, D)], ALU.add)
                        last.then_inc(hb_ready, 1)
                    a = m - L2
                    if a.within(XP):
                        r = a.mod(RY)
                        dve.wait_ge(y_ps, a.of(1, 1))
                        wait(dve, y_out[r], a.per(RY, 32, 0))
                        for u in range(2):
                            o = offs[2 * b + u]
                            last = v.tensor_tensor(yb[:, r, u], ps[:, 3, u * D:(u + 1) * D], b2b[:, bass.ds(o, D)], ALU.add)
                        last.then_inc(yb_ready, 1)
                pipeline(dve, XP, L2, RX, step, enter)

            @block.scalar
            def _(act):
                def step(m):
                    if m.within(XP):
                        act.wait_ge(xs_tr, m.of(1, 1))
                        wait(act, h_ps, m.of(1, -1))
                        nc.scalar.activation(xsT[:, m.mod(2)], ps[:, 0, :], ACT.Copy).then_inc(xsT_ready, 1)
                    a = m - L1
                    if a.within(XP):
                        act.wait_ge(hb_ready, a.of(1, 1))
                        wait(act, h_tr, a.of(1, -1))
                        nc.scalar.activation(hg[:, a.mod(2)], hb, ACT.Gelu).then_inc(hg_ready, 1)
                    a = m - L2H
                    if a.within(XP):
                        act.wait_ge(h_tr, a.of(1, 1))
                        wait(act, y_ps, a.of(1, -1))
                        nc.scalar.activation(hT[:, a.mod(2)], ps[:, 2, :], ACT.Copy).then_inc(hT_ready, 1)
                pipeline(act, XP, L2, RX, step)

            @block.tensor
            def _(pe):
                t_ = nc.tensor
                regs = [t_.alloc_register(f"expert_of_tile{j}") for j in range(2 * (RX + L2))]
                offs = [None] * (2 * (RX + L2))

                def enter(it):
                    t_.load(regs, tabrows[0][0:1, bass.ds(it * (2 * RX) + PADT - 2 * L2, 2 * (RX + L2))])
                    offs[:] = [t_.snap(r, min_val=0, max_val=(X - 1) * D) for r in regs]

                def step(m):
                    b = m.c % RX if isinstance(m.it, int) else m.c - RX
                    if m.within(XP):
                        r = m.mod(RX)
                        pe.wait_ge(xs_in[r], m.per(RX, 16, 16))
                        wait(pe, xsT_ready, m.of(1, 0))
                        for u in range(2):
                            for k in range(KC):
                                c = (u * KC + k) * P
                                last = t_.transpose(ps[:, 0, c:c + P], xs[:, r, u, k * P:(k + 1) * P], ident[:, :])
                        last.then_inc(xs_tr, 1)
                    a = m - L1
                    if a.within(XP):
                        pe.wait_ge(xsT_ready, a.of(1, 1))
                        wait(pe, hb_ready, a.of(1, 0))
                        for u in range(2):
                            o = offs[2 * (b + L2 - L1) + u]
                            for k in range(KC):
                                c = (u * KC + k) * P
                                last = t_.matmul(ps[:, 1, u * D:(u + 1) * D], xsT[:, a.mod(2), c:c + P], w1f[:, k, bass.ds(o, D)],
                                                 start=(k == 0), stop=(k == KC - 1))
                        last.then_inc(h_ps, 1)
                    a = m - L2
                    if a.within(XP):
                        pe.wait_ge(hT_ready, a.of(1, 1))
                        wait(pe, yb_ready, a.of(1, 0))
                        for u in range(2):
                            o = offs[2 * b + u]
                            for k in range(KC):
                                c = (u * KC + k) * P
                                last = t_.matmul(ps[:, 3, u * D:(u + 1) * D], hT[:, a.mod(2), c:c + P], w2f[:, k, bass.ds(o, D)],
                                                 start=(k == 0), stop=(k == KC - 1))
                        last.then_inc(y_ps, 1)
                    a = m - L2H
                    if a.within(XP):
                        pe.wait_ge(hg_ready, a.of(1, 1))
                        wait(pe, hT_ready, a.of(1, 0))
                        for u in range(2):
                            for k in range(KC):
                                c = (u * KC + k) * P
                                last = t_.transpose(ps[:, 2, c:c + P], hg[:, a.mod(2), u, k * P:(k + 1) * P], ident[:, :])
                        last.then_inc(h_tr, 1)
                pipeline(pe, XP, L2, RX, step, enter)

        RF = 4
        cut(0, restart=True)
        yin = cut(RF * 2 * K2 * D, "p (r u k n) -> p r u k n", r=RF, u=2, k=K2)
        acc = cut(RF * 2 * D, "p (r u n) -> p r u n", r=RF, u=2)
        yin_in = [sem(f"yin_in{r}") for r in range(RF)]
        acc_add = sem("acc_added")
        o_out = [sem(f"o_out{r}") for r in range(RF)]

        with nc.Block() as block:
            @block.sync
            def _(sp):
                def step(m):
                    r = m.mod(RF)
                    wait(sp, acc_add, m.of(4, 4 - 4 * RF))
                    rows = yd[bass.ds(m.of(2 * NB * K2), 2 * NB * K2), :]
                    sp.dma_start(yin[n_, r], rows.rearrange("(u p k) n -> p u k n", p=NB, k=K2)).then_inc(yin_in[r], 16)
                pipeline(sp, NP2, 0, RF, step)

            @block.scalar
            def _(act):
                def step(m):
                    r = m.mod(RF)
                    act.wait_ge(acc_add, m.of(4, 4))
                    act.dma_start(out[bass.ds(m.of(2 * NB), 2 * NB), :].rearrange("(u p) f -> p u f", p=NB), acc[n_, r]).then_inc(o_out[r], 16)
                pipeline(act, NP2, 0, RF, step)
                for r in range(RF):
                    act.wait_ge(o_out[r], 16 * len(range(r, NP2, RF)))

            @block.vector
            def _(dve):
                v = nc.vector

                def step(m):
                    r = m.mod(RF)
                    dve.wait_ge(yin_in[r], m.per(RF, 16, 16))
                    wait(dve, o_out[r], m.per(RF, 16, 0))
                    for k in range(K2):
                        for u in range(2):
                            t = bass.ds(m.of(2, u), 1)
                            if k:
                                dve.wait_ge(acc_add, m.of(4, u + 1))
                            before = acc[n_, r, u] if k else agg[n_, t, :].rearrange("p t f -> p (t f)")
                            v.scalar_tensor_tensor(out=acc[n_, r, u], in0=yin[n_, r, u, k], scalar=(m1, m2)[k][n_, t],
                                                   in1=before, op0=ALU.mult, op1=ALU.add).then_inc(acc_add, 1)
                pipeline(dve, NP2, 0, RF, step)


_INS = ["x", "src", "dst", "edge_weight1", "L0_gnn_mW1", "L0_gnn_mb1", "L0_gnn_ln_g", "L0_gnn_ln_b", "L0_gnn_mW2",
        "L0_gnn_mb2", "L0_gnn_uW1", "L0_gnn_ub1", "L0_gnn_uW2", "L0_gnn_ub2", "L0_ffn_router_w", "L0_ffn_w1",
        "L0_ffn_b1", "L0_ffn_w2", "L0_ffn_b2"]


def kernel(**inputs):
    import concourse.bacc as bacc
    from concourse.bass_utils import run_bass_kernel_spmd

    nc = bacc.Bacc("TRN2", target_bir_lowering=False, num_devices=1)
    arrays, args = {}, []
    for name in _INS:
        a = np.ascontiguousarray(inputs[name])
        arrays[f"in_{name}"] = a
        args.append(nc.dram_tensor(f"in_{name}", a.shape, mybir.dt.from_np(a.dtype), kind="ExternalInput").ap())
    args.append(nc.dram_tensor("out", (N, D), f32, kind="ExternalOutput").ap())
    gnn_moe_kernel(nc, *args)
    r = run_bass_kernel_spmd(nc, [arrays], core_ids=[0])
    return r.results[0]["out"]
```

```python
from contextlib import ExitStack

import numpy as np

import concourse.bass as bass
from concourse import mybir
from concourse.alu_op_type import AluOpType as ALU

f32, bf16, i32 = mybir.dt.float32, mybir.dt.bfloat16, mybir.dt.int32
i16 = mybir.dt.int16
ACT = mybir.ActivationFunctionType
AX = mybir.AxisListType

P = 128
N, D, E, X = 6250, 256, 100000, 8
KC = D // P
NB = 125
BK = N // NB
EC = E // NB
ECP = [480, 320]
EC0 = [0, ECP[0]]
PAIRS = [-(-((n * NB + BK * (P - 1)) // P) // 2) for n in ECP]
GP = [2 * n for n in PAIRS]
G0 = [0, GP[0]]
G = sum(GP)
TABP = [-(-g // P) for g in GP]
PADT = 16
UB = 10
EPS = 1e-5
RND = 12582912.0
assert BK * NB == N and EC * NB == E
assert sum(ECP) == EC and all(n <= 4 * g for n, g in zip(ECP, GP))
SEGS = [[slice(0, 80), slice(80, ECP[0])], [slice(ECP[0], EC)]]
SC = [10, 5]
assert all((g.stop - g.start) % (2 * SC[0]) == 0 for g in SEGS[0]) and ECP[1] == 2 * SC[1] * (PAIRS[0] // 8)
NP2 = BK // 2
K2 = 2
XT = 2 * -(-(K2 * N + X * (P - 1)) // (2 * P))
XW = D + 1
XD = 8
assert XT + 16 <= P


class Step:

    def __init__(self, it, unroll, c):
        self.it, self.unroll, self.c = it, unroll, c

    def __sub__(self, lag):
        return Step(self.it, self.unroll, self.c - lag)

    def __add__(self, lead):
        return Step(self.it, self.unroll, self.c + lead)

    def of(self, scale=1, add=0):
        const = scale * self.c + add
        return const if isinstance(self.it, int) else self.it * (scale * self.unroll) + const

    def per(self, d, scale=1, add=0):
        const = scale * (self.c // d) + add
        return const if isinstance(self.it, int) else self.it * (scale * self.unroll // d) + const

    def mod(self, k):
        return self.c % k

    def within(self, n):
        return not isinstance(self.it, int) or 0 <= self.c < n


def pipeline(eng, n, depth, unroll, step, enter=None, peel=1):
    first = max(peel, -(-depth // unroll))
    last = n // unroll
    assert last > first
    for b in range(first):
        if enter:
            enter(b)
        for c in range(unroll):
            step(Step(0, unroll, b * unroll + c))
    with eng.Fori(0, last - first) as it:
        if enter:
            enter(it + first)
        for c in range(unroll):
            step(Step(it, unroll, first * unroll + c))
    for m in range(last * unroll, n + depth):
        if enter and m % unroll == 0:
            enter(m // unroll)
        step(Step(0, unroll, m))


def wait(eng, sem, value):
    if isinstance(value, int) and value <= 0:
        return
    eng.wait_ge(sem, value)


def wait_apart(eng, sem, value, passed):
    wait(eng, sem, value)
    if not isinstance(value, int):
        eng.sem_inc(passed, 1)


def gnn_moe_kernel(nc, x, src, dst, edge_w, mW1, mb1, ln_g, ln_b, mW2, mb2, uW1, ub1, uW2, ub2,
                   router_w, w1, b1, w2, b2, out):
    ctx = ExitStack()
    with ctx:
        def sb(name, shape, dt=f32):
            return ctx.enter_context(nc.sbuf_tensor(name, shape, dt))

        def sem(name):
            return ctx.enter_context(nc.semaphore(name))

        ctx.enter_context(nc.allow_non_contiguous_dma(reason="small vectors laid along partitions"))

        recd = [nc.dram_tensor(f"edge_records{h}", (P * GP[h], 4), f32).ap() for h in range(2)]
        dstd = nc.dram_tensor("dst_half", (N, D), f32).ap()
        wcd = nc.dram_tensor("edge_weight_column", (3, D), bf16).ap()
        xsd = nc.dram_tensor("routed_tokens", (XT * P, XW), f32).ap()
        yd = nc.dram_tensor("expert_rows", (K2 * N + XD * P, D), f32).ap()
        xtabd = nc.dram_tensor("tile_experts", (P, 1), i32).ap()
        ud = nc.dram_tensor("update_node_half", (NP2, P, KC, 2, NB), f32).ap()
        tabd = [nc.dram_tensor(f"tile_blocks{h}", (P, TABP[h]), i32).ap() for h in range(2)]

        ablk = sb("ablk", [P, 3, BK * D], bf16)
        agg = sb("agg", [P, BK, D])
        rec = sb("rec", [P, G, 4])
        dpart2 = sb("dpart", [P, G * 3], bf16)
        dpart = dpart2[:, :].rearrange("p (g k) -> p g k", k=3)
        work = sb("work", [P, 12800])
        W2c = sb("W2c", [P, KC, D])
        b2c = sb("b2c", [P, D])
        ub2b = sb("ub2b", [P, D])
        mv1 = sb("mv1", [P, BK, 2])
        ident = sb("ident", [P, P])
        identh = sb("identh", [P, P], bf16)
        ebf = sb("ebf", [P, 2, 2, P], bf16)
        iota_n = sb("iota_n", [P, NB])
        tabrows = [sb(f"tabrow{h}", [1, PADT + P * TABP[h]], i32) for h in range(2)]
        stage_i = sb("stage_i", [P, 16], i32)
        stage = sb("stage", [P, 2, SC[0], 4])
        ps = ctx.enter_context(nc.psum_tensor("ps", [P, 8, 512], f32))

        at = [0]

        def cut(floats, shape=None, dt=f32, restart=False, **dims):
            if restart:
                at[0] = 0
            a = work[:, at[0]:at[0] + floats]
            at[0] += floats
            assert at[0] <= 12800
            a = a if dt == f32 else a.bitcast(dt)
            return a.rearrange(shape, **dims) if shape else a

        srci = cut(EC, dt=i32, restart=True)
        dsti = cut(EC, dt=i32)
        dwt = cut(EC)
        srcf = cut(EC)
        blkf = cut(EC)
        blkh = cut(EC // 2, dt=bf16)
        ones = cut(EC // 2, dt=bf16)
        mask = [cut(EC // 2, dt=bf16) for _ in range(2)]
        rank = [cut(EC) for _ in range(2)]
        pos = cut(EC)
        posi = cut(EC, dt=i32)
        lowi = cut(EC, dt=i32)
        cnt = cut(BK)
        iota_b = cut(BK + 2)
        tri = cut(P)
        onesf = cut(P)
        ntile = cut(BK)
        ntilei = cut(BK, dt=i32)
        start = cut(BK)
        base = cut(BK + 1)
        gidx = [cut(k) for k in TABP]
        cmp = cut(max(TABP) * BK)
        tblk = cut(max(TABP))
        tblki = [cut(k, dt=i32) for k in TABP]
        W1ab = cut(KC * 2 * D, "p (k n) -> p k n", k=KC)
        mb1b = cut(D)
        lng = cut(KC)
        lnb = cut(KC)
        w1c = cut(D)
        wcp = cut(3 * D // 2, "p (k n) -> p k n", dt=bf16, k=3)
        hn = [blkf[:, 0:D], blkf[:, D:2 * D]]
        hnT = [rank[0][:, 0:KC * NB].rearrange("p (k n) -> p k n", k=KC),
               rank[1][:, 0:KC * NB].rearrange("p (k n) -> p k n", k=KC)]
        bout = [pos[:, 0:D], pos[:, D:2 * D]]
        atmp = [lowi.bitcast(f32)[:, 0:D], lowi.bitcast(f32)[:, D:2 * D]]
        W2raw = dwt
        W2g = srcf[:, 0:KC * D].rearrange("p (k n) -> p k n", k=KC)
        dpartf = dpart2[:, :].bitcast(f32)
        uW1h = dpartf[:, 0:KC * D].rearrange("p (k n) -> p k n", k=KC)
        uout = [dpartf[:, KC * D + i * KC * NB:KC * D + (i + 1) * KC * NB].rearrange("p (f n) -> p f n", f=KC) for i in range(2)]
        lnbb = posi.bitcast(f32)[:, 0:KC * P].rearrange("p (k n) -> p k n", k=KC)
        recE = [rec[0:NB, G0[h]:G0[h] + ECP[h], :] for h in range(2)]

        passed_pool = sem("passed_pool")
        passed_dve = sem("passed_dve")
        passed_act = sem("passed_act")
        edges_in = sem("edges_in")
        x_in = sem("x_in")
        w_in = sem("w_in")
        w2_in = sem("w2_in")
        consts = sem("consts")
        pads_set = sem("pads_set")
        pads_out = sem("pads_out")
        rk = sem("rank_chain")
        cnt_ready = sem("cnt_ready")
        pre_ready = sem("pre_ready")
        blk_ready = sem("blk_ready")
        blk_out = sem("blk_out")
        blk_in = sem("blk_in")
        recs_ready = sem("recs_ready")
        staged = sem("staged")
        scat = [[sem(f"scattered{h}_{i}") for i in range(2)] for h in range(2)]
        scat_done = sem("scat_done")
        rec_in = sem("rec_in")

        def load_records(sp, h):
            sp.wait_ge(scat_done, h + 1)
            sp.dma_start(rec[:, G0[h]:G0[h] + GP[h], :].rearrange("p g f -> p (g f)"),
                         recd[h].rearrange("(p g) f -> p (g f)", p=P)).then_inc(rec_in, 16)
            sp.wait_ge(rec_in, 16 * h + 16)

        def stage_records(pool, h, m, i, done, staged, sems):
            n = SC[h]
            wait(pool, sems[i], done)
            cols = bass.ds(m.of(n) if m.unroll != 8 else m.per(4, n), n)
            nc.gpsimd.tensor_copy(stage[0:NB, i, 0:n], recE[h][:, cols, :]).then_inc(staged, 1)

        def scatter_column(pool, h, i, c, sems):
            pool.indirect_dma_start(
                recd[h], bass.IndirectOffsetOnAxis(ap=stage[0:NB, i, c, 3:4].bitcast(i32), axis=0),
                stage[0:NB, i, c, :], None).then_inc(sems[i], 16)

        var_ready = sem("var_ready")
        std_ready = sem("std_ready")
        nd = sem("node_chain")
        wcol_ready = sem("wcol_ready")
        wcol_out = sem("wcol_out")
        wcol_in = sem("wcol_in")
        w2g_ready = sem("w2g_ready")
        w2m_ready = sem("w2m_ready")
        hn_ready = sem("hn_ready")
        hn_tr = sem("hn_tr")
        hnT_ready = sem("hnT_ready")
        ab_ready = sem("ab_ready")
        b_copied = sem("b_copied")
        a_taken = sem("a_taken")
        b_stored = [sem("b_stored0"), sem("b_stored1")]
        u_in = sem("u_in")
        u_ps = sem("u_ps")
        u_copied = sem("u_copied")
        u_stored = [sem("u_stored0"), sem("u_stored1")]

        with nc.Block() as block:
            @block.sync
            def _(sp):
                sp.dma_start(srci[0:NB], src.rearrange("(p c) -> p c", p=NB)).then_inc(edges_in, 16)
                sp.dma_start(dsti[0:NB], dst.rearrange("(p c) -> p c", p=NB)).then_inc(edges_in, 16)
                sp.dma_start(dwt[0:NB], edge_w.rearrange("(p c) o -> p (c o)", p=NB)).then_inc(edges_in, 16)
                xv = x.rearrange("(t p) f -> p t f", p=NB)
                for t in range(0, BK, 10):
                    sp.dma_start(agg[0:NB, t:t + 10, :], xv[:, t:t + 10, :]).then_inc(x_in, 16)
                for h in range(2):
                    sp.dma_start(W1ab[:, :, h * D:(h + 1) * D],
                                 mW1[h * D:(h + 1) * D, :].rearrange("(k p) n -> p k n", p=P)).then_inc(w_in, 16)
                sp.dma_start(mb1b, mb1.partition_broadcast(P)).then_inc(w_in, 16)
                sp.dma_start(b2c[:, :], mb2.partition_broadcast(P)).then_inc(w_in, 16)
                sp.dma_start(ub2b[:, :], ub2.partition_broadcast(P)).then_inc(w_in, 16)
                sp.dma_start(lng, ln_g.rearrange("(k p) -> p k", p=P)).then_inc(w_in, 16)
                sp.dma_start(lnb, ln_b.rearrange("(k p) -> p k", p=P)).then_inc(w_in, 16)
                sp.dma_start(w1c[0:1], mW1[2 * D:2 * D + 1, :]).then_inc(w_in, 16)
                sp.dma_start(uW1h, uW1[0:D, :].rearrange("(k p) n -> p k n", p=P)).then_inc(u_in, 16)
                sp.wait_ge(pads_set, 4)
                for h in range(2):
                    sp.dma_start(recd[h].rearrange("(p g) f -> p (g f)", p=P),
                                 rec[:, G0[h]:G0[h] + GP[h], :].rearrange("p g f -> p (g f)")).then_inc(pads_out, 16)
                for h in range(2):
                    sp.wait_ge(blk_ready, h + 1)
                    sp.dma_start(tabd[h], tblki[h]).then_inc(blk_out, 16)
                    sp.wait_ge(blk_out, 16 * h + 16)
                    sp.dma_start(tabrows[h][0:1, PADT:PADT + P * TABP[h]],
                                 tabd[h].rearrange("p k -> (p k)").rearrange("(a n) -> a n", a=1)).then_inc(blk_in, 16)
                sp.wait_ge(recs_ready, 3)
                sp.dma_start(W2raw[:, 0:KC * D].rearrange("p (k n) -> p k n", k=KC),
                             mW2.rearrange("(k p) n -> p k n", p=P)).then_inc(w2_in, 16)
                sp.wait_ge(wcol_ready, 1)
                sp.dma_start(wcd.rearrange("k n -> (k n)").rearrange("(a n) -> a n", a=1),
                             wcp[0:1].rearrange("p k n -> p (k n)")).then_inc(wcol_out, 16)
                sp.wait_ge(wcol_out, 16)
                for k in range(3):
                    row = wcd[k, :].partition_broadcast(BK).partition_broadcast(P - NB)
                    sp.dma_start(ablk[NB:P, k, :].rearrange("p (b n) -> p b n", b=BK), row).then_inc(wcol_in, 16)

                def step(m):
                    sp.wait_ge(b_copied, m.of(1, 1))
                    rows = m.of(NB)
                    sp.dma_start(dstd[bass.ds(rows, NB), :], bout[m.mod(2)][0:NB]).then_inc(b_stored[m.mod(2)], 16)
                    sp.wait_ge(u_copied, m.of(1, 1))
                    sp.dma_start(ud[bass.ds(m.per(2), 1), :, :, m.mod(2), :].rearrange("t p f n -> (t p) f n"),
                                 uout[m.mod(2)]).then_inc(u_stored[m.mod(2)], 16)
                with sp.Fori(0, BK // 2) as it:
                    for c in range(2):
                        step(Step(it, 2, c))
                for h in range(2):
                    sp.wait_ge(b_stored[h], 16 * (BK // 2))
                    sp.wait_ge(u_stored[h], 16 * (BK // 2))
                sp.wait_ge(wcol_in, 48)
                sp.wait_ge(blk_in, 32)
                load_records(sp, 0)

            @block.gpsimd
            def _(pool):
                nc.gpsimd.memset(rec[:, :, :], 0.0).then_inc(pads_set, 1)
                for h in range(2):
                    nc.gpsimd.memset(tabrows[h][:, 0:PADT], 0).then_inc(pads_set, 1)
                pool.wait_ge(pads_set, 3)
                nc.gpsimd.memset(rec[:, :, 0:1], -1.0).then_inc(pads_set, 1)
                nc.gpsimd.memset(ident[:, :], 0.0).then_inc(consts, 1)
                nc.gpsimd.memset(onesf, 1.0).then_inc(consts, 1)
                nc.gpsimd.memset(ones, 1.0).then_inc(consts, 1)
                nc.gpsimd.iota(iota_n[:, :], pattern=[[1, NB]], base=0, channel_multiplier=0,
                               allow_small_or_imprecise_dtypes=True).then_inc(consts, 1)
                nc.gpsimd.iota(iota_b, pattern=[[1, BK + 2]], base=0, channel_multiplier=0,
                               allow_small_or_imprecise_dtypes=True).then_inc(consts, 1)
                for h in range(2):
                    nc.gpsimd.iota(gidx[h], pattern=[[1, TABP[h]]], base=0, channel_multiplier=TABP[h],
                                   allow_small_or_imprecise_dtypes=True).then_inc(consts, 1)
                pool.wait_ge(consts, 7)
                nc.gpsimd.affine_select(out=ident[:, :], in_=ident[:, :], compare_op=ALU.not_equal, fill=1.0,
                                        base=0, pattern=[[-1, P]], channel_multiplier=1).then_inc(consts, 1)
                nc.gpsimd.affine_select(out=tri, in_=onesf, compare_op=ALU.is_gt, fill=0.0,
                                        base=0, pattern=[[1, P]], channel_multiplier=-1).then_inc(consts, 1)
                pool.wait_ge(recs_ready, 1)

                def step(m):
                    i = m.mod(2)
                    stage_records(pool, 0, m, i, m.per(2, 16 * SC[0], 0), staged, scat[0])
                    wait_apart(pool, staged, m.of(1, 1), passed_pool)
                    for c in range(SC[0]):
                        scatter_column(pool, 0, i, c, scat[0])
                groups = [(w.stop - w.start) // SC[0] for w in SEGS[0]]
                pipeline(pool, groups[0], 0, 2, step)
                pool.wait_ge(recs_ready, 2)
                with pool.Fori(0, groups[1] // 2) as it:
                    for c in range(2):
                        step(Step(it, 2, groups[0] + c))
                for i in range(2):
                    pool.wait_ge(scat[0][i], 16 * ECP[0] // 2)
                pool.sem_inc(scat_done, 1)

            @block.vector
            def _(dve):
                done = [0]

                def link(ins):
                    done[0] += 1
                    ins.then_inc(rk, 1)
                    dve.wait_ge(rk, done[0])

                v = nc.vector
                e = slice(0, NB)
                dve.wait_ge(edges_in, 48)
                link(v.tensor_copy(srcf[e], srci[e]))
                link(v.tensor_scalar(blkf[e], srcf[e], -float(NB // 2), 1.0 / NB, ALU.add, ALU.mult))
                link(v.tensor_scalar(blkf[e], blkf[e], RND, None, ALU.add))
                link(v.tensor_scalar(blkf[e], blkf[e], RND, None, ALU.subtract))
                link(v.tensor_copy(blkh[e], blkf[e]))
                link(v.memset(pos[e], 0.0))
                link(v.memset(base[e, BK:BK + 1], 0.0))
                dve.wait_ge(consts, 9)
                link(v.tensor_copy(identh[:, :], ident[:, :]))
                for h in range(2):
                    w = slice(EC0[h], EC0[h] + ECP[h])
                    def tally(b, c):
                        v.tensor_scalar(mask[c][e, w], blkh[e, w], iota_b[e, b], 0.0, ALU.is_equal, ALU.add,
                                        accum_out=cnt[e, b]).then_inc(cnt_ready, 1)

                    for c in range(2):
                        tally(bass.ds(c, 1), c)
                    with dve.Fori(0, BK // UB - 1) as it:
                        for c in range(UB):
                            dve.wait_ge(cnt_ready, it * UB + c + 1 + BK * h)
                            tally(bass.ds(it * UB + c + 2, 1), c % 2)
                    for c in range(BK - UB + 2, BK):
                        dve.wait_ge(cnt_ready, c - 1 + BK * h)
                        tally(bass.ds(c, 1), c % 2)
                    if h == 0:
                        dve.wait_ge(pads_out, 32)
                    link(v.scalar_tensor_tensor(out=recE[h][:, :, 0], in0=blkf[e, w], scalar=-float(NB), in1=srcf[e, w],
                                                op0=ALU.mult, op1=ALU.add))
                    link(v.tensor_copy(recE[h][:, :, 1].bitcast(i32), dsti[e, w]))
                    link(v.tensor_copy(recE[h][:, :, 2], dwt[e, w]))
                    dve.wait_ge(pre_ready, 2 * h + 2)
                    link(v.tensor_scalar(ntilei, ps[:, 1, 0:BK], float(P - 1), None, ALU.add))
                    link(v.tensor_scalar(ntilei, ntilei, 7, None, ALU.arith_shift_right))
                    link(v.tensor_copy(ntile, ntilei))
                    link(v.tensor_tensor_scan(start, ones[:, 0:BK], ntile, 0.0, ALU.mult, ALU.add))
                    link(v.tensor_tensor(start, start, ntile, ALU.subtract))
                    link(v.tensor_scalar(base[e, 0:BK], start[e], float(P), -1.0, ALU.mult, ALU.add))
                    link(v.tensor_tensor(base[e, 0:BK], base[e, 0:BK], ps[e, 0, 0:BK], ALU.add))
                    nt = TABP[h]
                    ge = cmp[:, 0:nt * BK].rearrange("p (k b) -> p k b", k=nt)
                    link(v.tensor_tensor(ge, start.unsqueeze(1).to_broadcast([P, nt, BK]),
                                         gidx[h].unsqueeze(2).to_broadcast([P, nt, BK]), ALU.is_le))
                    link(v.tensor_reduce(out=tblk[:, 0:nt], in_=ge, axis=AX.X, op=ALU.add))
                    v.tensor_scalar(tblki[h], tblk[:, 0:nt], -1.0, float(D), ALU.add, ALU.mult).then_inc(blk_ready, 1)

                    def match(b, c):
                        return v.tensor_scalar(mask[c][e, g], blkh[e, g], iota_b[e, b], None, ALU.is_equal)

                    def count(b, c):
                        return v.tensor_tensor_scan(rank[c][e, g], ones[e, g], mask[c][e, g], base[e, b], ALU.mult, ALU.add)

                    for g in SEGS[h]:
                        more = g.stop < w.stop
                        per = 4 if more else 3
                        link(match(bass.ds(0, 1), 0))
                        link(count(bass.ds(0, 1), 0))
                        before = done[0]
                        link(match(bass.ds(1, 1), 1))
                        with dve.Fori(0, BK // UB) as it:
                            for j in range(UB):
                                c, at0 = j % 2, it * (per * UB) + before + per * j
                                wait_apart(dve, rk, at0, passed_dve)
                                v.copy_predicated(pos[e, g], mask[c][e, g].bitcast(i16), rank[c][e, g]).then_inc(rk, 1)
                                if more:
                                    v.tensor_copy(base[e, bass.ds(it * UB + j, 1)],
                                                  rank[c][e, g.stop - 1:g.stop]).then_inc(rk, 1)
                                dve.wait_ge(rk, at0 + 1)
                                count(bass.ds(it * UB + j + 1, 1), 1 - c).then_inc(rk, 1)
                                dve.wait_ge(rk, at0 + 2)
                                match(bass.ds(it * UB + j + 2, 1), c).then_inc(rk, 1)
                        done[0] += per * BK
                        link(v.tensor_copy(posi[e, g], pos[e, g]))
                        link(v.tensor_scalar(lowi[e, g], posi[e, g], P - 1, None, ALU.bitwise_and))
                        link(v.tensor_scalar(posi[e, g], posi[e, g], 7, None, ALU.arith_shift_right))
                        slots = recE[h][:, g.start - w.start:g.stop - w.start, 3]
                        v.scalar_tensor_tensor(out=slots.bitcast(i32), in0=lowi[e, g], scalar=float(GP[h]), in1=posi[e, g],
                                               op0=ALU.mult, op1=ALU.add).then_inc(recs_ready, 1)

                dve.wait_ge(x_in, 80)
                stats = rank[0][:, 0:12].rearrange("p (h s) -> p h s", h=2)
                pair = rank[0][:, 12:16].rearrange("p (h s) -> p h s", h=2)
                before = done[0]
                with dve.Fori(0, BK // 2) as it:
                    for h in range(2):
                        v.bn_stats(stats[e, h], agg[e, bass.ds(it * 2 + h, 1), :].rearrange("p t f -> p (t f)")).then_inc(rk, 1)
                    wait_apart(dve, rk, it * 5 + before + 2, passed_dve)
                    for h in range(2):
                        v.bn_aggr(pair[e, h], stats[e, h]).then_inc(rk, 1)
                    dve.wait_ge(rk, it * 5 + before + 4)
                    v.tensor_copy(mv1[e, bass.ds(it * 2, 2), :], pair[e]).then_inc(rk, 1)
                    dve.wait_ge(rk, it * 5 + before + 5)
                done[0] += 5 * (BK // 2)
                v.tensor_scalar(mv1[e, :, 1], mv1[e, :, 1], EPS, None, ALU.add).then_inc(var_ready, 1)
                dve.wait_ge(w_in, 16 * 8)
                o = slice(0, 1)
                link(v.tensor_copy(wcp[o, 0], w1c[o]))
                link(v.tensor_tensor(w1c[o], w1c[o], wcp[o, 0], ALU.subtract))
                link(v.tensor_copy(wcp[o, 1], w1c[o]))
                link(v.tensor_tensor(w1c[o], w1c[o], wcp[o, 1], ALU.subtract))
                v.tensor_copy(wcp[o, 2], w1c[o]).then_inc(wcol_ready, 1)
                dve.wait_ge(w2_in, 16)
                for k in range(KC):
                    v.tensor_scalar(W2g[:, k], W2raw[:, k * D:(k + 1) * D], lng[:, k:k + 1], None,
                                    ALU.mult).then_inc(w2g_ready, 1)
                    v.tensor_scalar(lnbb[:, k], onesf, lnb[:, k:k + 1], None, ALU.mult).then_inc(w2g_ready, 1)
                dve.wait_ge(w2m_ready, 1)
                for k in range(KC):
                    v.scalar_tensor_tensor(out=W2c[:, k], in0=ps[:, 0, 0:D], scalar=-1.0 / D, in1=W2g[:, k],
                                           op0=ALU.mult, op1=ALU.add)
                link(v.tensor_tensor(b2c[:, :], b2c[:, :], ps[:, 1, 0:D], ALU.add))
                dve.wait_ge(std_ready, 1)
                link(v.reciprocal(mv1[e, :, 1], mv1[e, :, 1]))

                def step(m):
                    if m.within(BK):
                        s = m.mod(2)
                        wait(dve, hn_tr, m.of(1, -1))
                        t = bass.ds(m.of(), 1)
                        v.tensor_scalar(hn[s][e], agg[e, t, :].rearrange("p t f -> p (t f)"),
                                        mv1[e, t, 0], mv1[e, t, 1], ALU.subtract, ALU.mult).then_inc(hn_ready, 1)
                    a = m - 2
                    if a.within(BK):
                        s = a.mod(2)
                        dve.wait_ge(ab_ready, a.of(1, 1))
                        t = bass.ds(a.of(D), D)
                        tmp = atmp[s][e]
                        v.tensor_tensor(tmp, ps[e, 2 + s, 0:D], mb1b[e], ALU.add).then_inc(a_taken, 1)
                        dve.wait_ge(a_taken, a.of(1, 1))
                        for k in range(2):
                            v.tensor_copy(ablk[e, k, t], tmp).then_inc(nd, 1)
                            dve.wait_ge(nd, a.of(5, 2 * k + 1))
                            v.tensor_tensor(tmp, tmp, ablk[e, k, t], ALU.subtract).then_inc(nd, 1)
                            dve.wait_ge(nd, a.of(5, 2 * k + 2))
                        v.tensor_copy(ablk[e, 2, t], tmp).then_inc(nd, 1)

                pipeline(dve, BK, 2, 2, step)

            @block.scalar
            def _(act):
                act.wait_ge(var_ready, 1)
                nc.scalar.activation(mv1[0:NB, :, 1], mv1[0:NB, :, 1], ACT.Sqrt).then_inc(std_ready, 1)

                def step(m):
                    s = m.mod(2)
                    if m.within(BK):
                        act.wait_ge(hn_tr, m.of(1, 1))
                        wait(act, ab_ready, m.of(1, -1))
                        wait(act, u_ps, m.of(1, -1))
                        nc.scalar.activation(hnT[s], ps[:, 4 + s, 0:KC * NB].rearrange("p (k n) -> p k n", k=KC),
                                             ACT.Copy).then_inc(hnT_ready, 1)
                    b = m - 2
                    if b.within(BK):
                        act.wait_ge(u_ps, b.of(1, 1))
                        wait(act, u_stored[b.mod(2)], b.per(2, 16, 0))
                        nc.scalar.activation(uout[b.mod(2)], ps[:, 6 + b.mod(2), 0:KC * NB].rearrange("p (f n) -> p f n", f=KC),
                                             ACT.Copy).then_inc(u_copied, 1)
                        act.wait_ge(a_taken, b.of(1, 1))
                        wait(act, b_stored[b.mod(2)], b.per(2, 16, 0))
                        nc.scalar.activation(bout[b.mod(2)][0:NB], ps[0:NB, 2 + b.mod(2), D:2 * D],
                                             ACT.Copy).then_inc(b_copied, 1)

                pipeline(act, BK, 2, 2, step, peel=2)

            @block.tensor
            def _(pe):
                for h in range(2):
                    pe.wait_ge(cnt_ready, BK * (h + 1))
                    nc.tensor.matmul(ps[:, 0, 0:BK], tri[0:NB, :], cnt[0:NB], start=True, stop=True).then_inc(pre_ready, 1)
                    nc.tensor.matmul(ps[:, 1, 0:BK], onesf[0:NB], cnt[0:NB], start=True, stop=True).then_inc(pre_ready, 1)
                pe.wait_ge(w2g_ready, 2 * KC)
                for k in range(KC):
                    nc.tensor.matmul(ps[:, 0, 0:D], onesf, W2g[:, k], start=(k == 0), stop=(k == KC - 1))
                for k in range(KC):
                    last = nc.tensor.matmul(ps[:, 1, 0:D], lnbb[:, k], W2raw[:, k * D:(k + 1) * D],
                                            start=(k == 0), stop=(k == KC - 1))
                last.then_inc(w2m_ready, 1)

                def step(m):
                    if m.within(BK):
                        s = m.mod(2)
                        pe.wait_ge(hn_ready, m.of(1, 1))
                        wait(pe, hnT_ready, m.of(1, -1))
                        for k in range(KC):
                            last = nc.tensor.transpose(ps[:, 4 + s, k * NB:(k + 1) * NB],
                                                       hn[s][0:NB, k * P:(k + 1) * P], ident[0:NB, 0:NB])
                        last.then_inc(hn_tr, 1)
                    a = m - 1
                    if a.within(BK):
                        s = a.mod(2)
                        pe.wait_ge(hnT_ready, a.of(1, 1))
                        wait(pe, a_taken, a.of(1, -1))
                        wait(pe, b_copied, a.of(1, -1))
                        for k in range(KC):
                            last = nc.tensor.matmul(ps[0:NB, 2 + s, :], hnT[s][:, k, :], W1ab[:, k, :],
                                                    start=(k == 0), stop=(k == KC - 1))
                        last.then_inc(ab_ready, 1)
                        wait(pe, u_copied, a.of(1, -1))
                        for f in range(KC):
                            for k in range(KC):
                                last = nc.tensor.matmul(ps[:, 6 + s, f * NB:(f + 1) * NB], uW1h[:, k, f * P:(f + 1) * P],
                                                        hnT[s][:, k, :], start=(k == 0), stop=(k == KC - 1))
                        last.then_inc(u_ps, 1)

                pe.wait_ge(u_in, 16)
                pipeline(pe, BK, 1, 2, step)

        RE, RB, RT = 8, 8, 4
        eh = cut(RE * 2 * NB, "p (r u n) -> p r u n", restart=True, r=RE, u=2)
        bg = cut(RB * 2 * D, "p (r u n) -> p r u n", r=RB, u=2)
        sa = cut(RT * 2 * D, "p (r u n) -> p r u n", r=RT, u=2)
        sT = cut(RT * 2 * D, "p (r u k n) -> p r u k n", r=RT, u=2, k=KC)
        zb = cut(2 * D, "p (u n) -> p u n", u=2)
        junk = cut(D)
        msg = cut(2 * 2 * D, "p (r u n) -> p r u n", r=2, u=2)
        ohT = cut(2 * P, "p (r u n) -> p r u n", dt=bf16, r=2, u=2)
        ssum = cut(RE * 2, "p (r u) -> p r u", r=RE)
        ssq = cut(RE * 2, "p (r u) -> p r u", r=RE)
        rstd = cut(RE * 2, "p (r u) -> p r u", r=RE)
        mean = cut(4, "p (r u) -> p r u", r=2)
        var = cut(8, "p (i r u) -> p i r u", i=2, r=2)
        half = cut(4, "p (r u) -> p r u", r=2)
        dres = [agg[:, 0:4, :].rearrange("p t f -> p (t f)")[:, 0:GP[0]], cut(GP[1])]

        LT, LA, LS, LX, LQ, LM, LZ, LG = 1, 2, 3, 4, 5, 5, 6, 7
        staged1 = sem("staged1")

        oh_bank = ps[:, 0, 0:P].bitcast(bf16)

        def messages(h):
            n_pairs = PAIRS[h]
            mine = slice(G0[h], G0[h] + GP[h])
            rech, dparth, tabrow = rec[:, mine], dpart[:, mine], tabrows[h]
            own = []

            def sem(name):
                own.append(nc.alloc_semaphore(name=name))
                return own[-1]

            split = sem(f"split_chain{h}")
            oh_ready = sem(f"oh_ready{h}")
            oh_tr = sem(f"oh_tr{h}")
            eh_ready = sem(f"sum_one_hots_ready{h}")
            ohT_ready = sem(f"ohT_ready{h}")
            pre_ps = sem(f"pre_ps{h}")
            pre_sb = sem(f"pre_sb{h}")
            idx_st = sem(f"idx_staged{h}")
            gath = [sem(f"gathered{h}_{r}") for r in range(RB)]
            s_ready = sem(f"s_ready{h}")
            s_tr = sem(f"s_tr{h}")
            sT_ready = sem(f"sT_ready{h}")
            sq_done = sem(f"squares_done{h}")
            half_ready = sem(f"half_ready{h}")
            var_ready = sem(f"var_ready{h}")
            nrm = sem(f"norm_chain{h}")
            rstd_ready = sem(f"rstd_ready{h}")
            z_ps = sem(f"z_ps{h}")
            z_sb = sem(f"z_sb{h}")
            msg_ready = sem(f"msg_ready{h}")
            agg_ps = sem(f"agg_ps{h}")
            agg_add = sem(f"agg_add{h}")

            with nc.Block() as block:
                if h == 0:
                    @block.sync
                    def _(sp):
                        load_records(sp, 1)

                @block.gpsimd
                def _(pool):
                    nc.gpsimd.memset(half[:, :, :], -0.5).then_inc(half_ready, 1)
                    pool.wait_ge(half_ready, 1)

                    def stage_idx(m):
                        i = m.mod(RB) // 4
                        n = 8 if not isinstance(m.it, int) else min(8, 2 * (n_pairs - m.c))
                        if not isinstance(m.it, int) or m.c >= RB:
                            for r in range(4 * i, 4 * i + 4):
                                pool.wait_ge(gath[r], m.per(RB, 32, 0))
                        nc.gpsimd.tensor_copy(stage_i[:, i * 8:i * 8 + n], rec[:, bass.ds(m.of(2, G0[h]), n), 1].bitcast(i32)).then_inc(idx_st, 1)

                    def gather(m):
                        r = m.mod(RB)
                        wait_apart(pool, s_ready, m.of(2, 2 - 2 * RB), passed_pool)
                        for u in range(2):
                            c = (r * 2 + u)
                            pool.indirect_dma_start(bg[:, r, u, :], None, dstd,
                                                    bass.IndirectOffsetOnAxis(ap=stage_i[:, c:c + 1], axis=0)).then_inc(gath[r], 16)

                    def rsqrt(m):
                        r = m.mod(RE)
                        n = 2 if not isinstance(m.it, int) else min(2, n_pairs - m.c)
                        pool.wait_ge(var_ready, m.per(2, 1, 1))
                        nc.gpsimd.tensor_tensor(rstd[:, r:r + n, :], var[:, m.mod(4) // 2, 0:n, :], half[:, 0:n, :],
                                                ALU.pow).then_inc(rstd_ready, 1)

                    def place(m):
                        for k in ((0, 1), (2,), (3,), (4,))[m.mod(4)]:
                            scatter_column(pool, 1, m.mod(8) // 4, k, scat[1])

                    def step(m):
                        placing = h == 0 and m.within(n_pairs // 8 * 8)
                        if placing and m.mod(4) == 0:
                            stage_records(pool, 1, m, m.mod(8) // 4, m.per(8, 16 * SC[1], 0), staged1, scat[1])
                        if m.within(n_pairs):
                            gather(m)
                        if m.mod(4) == 3 and (m + 1).within(n_pairs):
                            stage_idx(m + 1)
                        if placing:
                            if m.mod(4) == 0:
                                wait_apart(pool, staged1, m.per(4, 1, 1), passed_pool)
                            place(m)
                        q = m - AHEAD
                        if q.within(n_pairs) and q.mod(2) == 0:
                            rsqrt(q)
                        if m.mod(4) == 3 and (m + 1).within(n_pairs):
                            wait_apart(pool, idx_st, (m + 1).per(4, 1, 1), passed_pool)

                    AHEAD = 5
                    stage_idx(Step(0, RE, 0))
                    pool.wait_ge(idx_st, 1)
                    pipeline(pool, n_pairs, AHEAD, RE, step, peel=2)
                    if h == 0:
                        for i in range(2):
                            pool.wait_ge(scat[1][i], 16 * ECP[1] // 2)
                        pool.sem_inc(scat_done, 1)

                @block.vector
                def _(dve):
                    v = nc.vector
                    done = [0]

                    def link(ins):
                        done[0] += 1
                        ins.then_inc(split, 1)
                        dve.wait_ge(split, done[0])

                    link(v.tensor_copy(dparth[:, :, 0], rech[:, :, 2]))
                    link(v.tensor_tensor(dres[h], rech[:, :, 2], dparth[:, :, 0], ALU.subtract))
                    link(v.tensor_copy(dparth[:, :, 1], dres[h]))
                    link(v.tensor_tensor(dres[h], dres[h], dparth[:, :, 1], ALU.subtract))
                    link(v.tensor_copy(dparth[:, :, 2], dres[h]))
                    if h == 0:
                        link(v.memset(agg[:, :, :], 0.0))
                    regs = [v.alloc_register(f"block_of_tile{h}_{j}") for j in range(16)]
                    offs = [None] * 16

                    def enter(it):
                        if isinstance(it, int) and it == 0:
                            return
                        v.load(regs, tabrow[0:1, bass.ds(it * 16 + PADT - 16, 16)])
                        offs[:] = [v.snap(r, min_val=0, max_val=(BK - 1) * D) for r in regs]

                    aggf = agg[:, :, :].rearrange("p t f -> p (t f)")

                    def add_sums(a, u):
                        wait(dve, agg_add, a.of(2, u))
                        d = aggf[0:NB, bass.ds(offs[2 * a.mod(RE) + u], D)]
                        v.tensor_tensor(d, d, ps[0:NB, 7, u * D:(u + 1) * D], ALU.add).then_inc(agg_add, 1)

                    def norm(m, part):
                        if not (m.within(n_pairs) and m.mod(2) == 0):
                            return
                        r = m.mod(RE)
                        n = 2 if not isinstance(m.it, int) else min(2, n_pairs - m.c)
                        me, va = mean[:, 0:n, :], var[:, m.mod(4) // 2, 0:n, :]
                        if part:
                            dve.wait_ge(nrm, m.per(2, 2, part))
                        else:
                            dve.wait_ge(sq_done, m.of(2, 2 * n))
                            wait(dve, rstd_ready, m.per(2, 1, -1))
                        if part == 0:
                            v.scalar_tensor_tensor(out=me, in0=ssum[:, r:r + n, :], scalar=1.0 / D ** 2, in1=ssum[:, r:r + n, :],
                                                   op0=ALU.mult, op1=ALU.mult).then_inc(nrm, 1)
                        elif part == 1:
                            v.scalar_tensor_tensor(out=va, in0=ssq[:, r:r + n, :], scalar=1.0 / D, in1=me,
                                                   op0=ALU.mult, op1=ALU.subtract).then_inc(nrm, 1)
                        else:
                            v.tensor_scalar(va, va, 0.0, EPS, ALU.max, ALU.add).then_inc(var_ready, 1)

                    def step(m):
                        g, z, b, q = m - RE, m - LZ, m - LA, m - LQ
                        norm(q, 0)
                        if g.within(n_pairs):
                            dve.wait_ge(agg_ps, g.of(1, 1))
                            add_sums(g, 0)
                        norm(q, 1)
                        if m.within(n_pairs):
                            s = m.mod(2)
                            wait(dve, oh_tr, m.of(1, -1))
                            t = bass.ds(m.of(2), 2)
                            v.tensor_tensor(ebf[:, s, :, 0:NB], iota_n[:, :].unsqueeze(1).to_broadcast([P, 2, NB]),
                                            rech[:, t, 0:1].to_broadcast([P, 2, NB]), ALU.is_equal)
                            norm(q, 2)
                            v.tensor_copy(ebf[:, s, :, NB:P], dparth[:, t, :]).then_inc(oh_ready, 1)
                        else:
                            norm(q, 2)
                        if g.within(n_pairs):
                            add_sums(g, 1)
                        if z.within(n_pairs):
                            s = z.mod(2)
                            dve.wait_ge(z_ps, z.of(1, 1))
                            dve.wait_ge(rstd_ready, z.per(2, 1, 1))
                            wait(dve, msg_ready, z.of(1, 0))
                            for u in range(2):
                                last = v.scalar_tensor_tensor(out=zb[:, u], in0=ps[:, 5 + s, u * D:(u + 1) * D],
                                                              scalar=rstd[:, z.mod(RE), u:u + 1], in1=b2c[:, :],
                                                              op0=ALU.mult, op1=ALU.add)
                            last.then_inc(z_sb, 1)
                        if b.within(n_pairs):
                            r, s = b.mod(RB), b.mod(2)
                            dve.wait_ge(pre_ps, b.of(1, 1))
                            dve.wait_ge(gath[r], b.per(RB, 32, 32))
                            v.tensor_tensor(bg[:, r].rearrange("p u n -> p (u n)"), ps[:, 1 + s, :],
                                            bg[:, r].rearrange("p u n -> p (u n)"), ALU.add).then_inc(pre_sb, 1)
                        if m.within(n_pairs):
                            wait(dve, agg_ps, m.of(1, 1 - RE))
                            v.tensor_tensor(eh[:, m.mod(RE)], iota_n[:, :].unsqueeze(1).to_broadcast([P, 2, NB]),
                                            rech[:, bass.ds(m.of(2), 2), 0:1].to_broadcast([P, 2, NB]),
                                            ALU.is_equal).then_inc(eh_ready, 1)

                    pipeline(dve, n_pairs, RE, RE, step, enter, peel=2)

                @block.scalar
                def _(act):
                    def step(m):
                        a = m - LT
                        if a.within(n_pairs):
                            act.wait_ge(oh_tr, a.of(1, 1))
                            wait(act, pre_ps, a.of(1, -1))
                            nc.scalar.activation(ohT[:, a.mod(2)], oh_bank.rearrange("p (u n) -> p u n", u=2),
                                                 ACT.Copy).then_inc(ohT_ready, 1)
                        a = m - LZ
                        if a.within(n_pairs):
                            act.wait_ge(z_sb, a.of(1, 1))
                            wait(act, agg_ps, a.of(1, -1))
                            nc.scalar.activation(msg[:, a.mod(2)], zb[:, :, :], ACT.Silu).then_inc(msg_ready, 1)
                        a = m - LS
                        if a.within(n_pairs):
                            act.wait_ge(s_ready, a.of(2, 2))
                            for u in range(2):
                                wait(act, sq_done, a.of(2, u))
                                nc.scalar.activation(junk, sa[:, a.mod(RT), u], ACT.Square,
                                                     accum_out=ssq[:, a.mod(RE), u:u + 1]).then_inc(sq_done, 1)
                        a = m - LX
                        if a.within(n_pairs):
                            act.wait_ge(s_tr, a.of(1, 1))
                            wait(act, z_ps, a.of(1, 1 - RT))
                            nc.scalar.activation(sT[:, a.mod(RT)].rearrange("p u k n -> p (u k n)"), ps[:, 3 + a.mod(2), :],
                                                 ACT.Copy).then_inc(sT_ready, 1)
                        a = m - LA
                        if a.within(n_pairs):
                            act.wait_ge(pre_sb, a.of(1, 1))
                            wait(act, s_tr, a.of(1, 1 - RT))
                            wait(act, sq_done, a.of(2, 2 - 2 * RT))
                            wait(act, rstd_ready, a.per(2, 1, 1 - RE // 2))
                            for u in range(2):
                                nc.scalar.activation(sa[:, a.mod(RT), u], bg[:, a.mod(RB), u], ACT.Silu,
                                                     accum_out=ssum[:, a.mod(RE), u:u + 1]).then_inc(s_ready, 1)

                    pipeline(act, n_pairs, RE, RE, step, peel=2)

                @block.tensor
                def _(pe):
                    t_ = nc.tensor
                    regs = [t_.alloc_register(f"block_of_tile{h}_{j}") for j in range(16)]
                    offs = [None] * 16

                    def enter(it):
                        t_.load(regs, tabrow[0:1, bass.ds(it * 16 + PADT - 2 * LA, 16)])
                        offs[:] = [t_.snap(r, min_val=0, max_val=(BK - 1) * D) for r in regs]

                    def step(m):
                        a = m - LT
                        if a.within(n_pairs):
                            s = a.mod(2)
                            pe.wait_ge(oh_ready, a.of(1, 1))
                            wait(pe, ohT_ready, a.of(1, 0))
                            for u in range(2):
                                last = t_.transpose(oh_bank[:, u * P:(u + 1) * P], ebf[:, a.mod(2), u], identh[:, :])
                            last.then_inc(oh_tr, 1)
                        a = m - LA
                        if a.within(n_pairs):
                            s = a.mod(2)
                            pe.wait_ge(ohT_ready, a.of(1, 1))
                            wait(pe, pre_sb, a.of(1, -1))
                            for u in range(2):
                                o = offs[(2 * (a.mod(RE) + LA) + u) % 16]
                                for k in range(3):
                                    last = t_.matmul(ps[:, 1 + s, u * D:(u + 1) * D], ohT[:, s, u], ablk[:, k, bass.ds(o, D)],
                                                     start=(k == 0), stop=(k == 2))
                            last.then_inc(pre_ps, 1)
                        a = m - LX
                        if a.within(n_pairs):
                            s = a.mod(2)
                            pe.wait_ge(s_ready, a.of(2, 2))
                            wait(pe, sT_ready, a.of(1, -1))
                            for u in range(2):
                                for k in range(KC):
                                    c = (u * KC + k) * P
                                    last = t_.transpose(ps[:, 3 + s, c:c + P], sa[:, a.mod(RT), u, k * P:(k + 1) * P], ident[:, :])
                            last.then_inc(s_tr, 1)
                        a = m - LM
                        if a.within(n_pairs):
                            s = a.mod(2)
                            pe.wait_ge(sT_ready, a.of(1, 1))
                            wait(pe, z_sb, a.of(1, -1))
                            for u in range(2):
                                for k in range(KC):
                                    last = t_.matmul(ps[:, 5 + s, u * D:(u + 1) * D], sT[:, a.mod(RT), u, k], W2c[:, k],
                                                     start=(k == 0), stop=(k == KC - 1))
                            last.then_inc(z_ps, 1)
                        a = m - LG
                        if a.within(n_pairs):
                            pe.wait_ge(msg_ready, a.of(1, 1))
                            pe.wait_ge(eh_ready, a.of(1, 1))
                            wait(pe, agg_add, a.of(2, 0))
                            for u in range(2):
                                last = t_.matmul(ps[0:NB, 7, u * D:(u + 1) * D], eh[:, a.mod(RE), u], msg[:, a.mod(2), u],
                                                 start=True, stop=True)
                            last.then_inc(agg_ps, 1)

                    pipeline(pe, n_pairs, RE, RE, step, enter)

            nc.clear_and_free_semaphores(own)
            nc.all_engine_barrier()

        for h in range(2):
            messages(h)

        wts = ablk[:, :, :].rearrange("p k n -> p (k n)").bitcast(f32)
        wat = [0]

        def wcut(floats, shape=None, **dims):
            a = wts[:, wat[0]:wat[0] + floats]
            wat[0] += floats
            assert wat[0] <= 3 * BK * D // 2
            return a.rearrange(shape, **dims) if shape else a

        uW1s = wcut(KC * D, "p (k n) -> p k n", k=KC)
        uW2s = wcut(KC * D, "p (k n) -> p k n", k=KC)
        w1s = wcut(X * KC * D, "p (k e n) -> p k e n", e=X, k=KC)
        w2s = wcut(X * KC * D, "p (k e n) -> p k e n", e=X, k=KC)
        b1b = wcut(X * D)
        b2b = wcut(X * D)
        rws = wcut(KC * X, "p (k e) -> p k e", k=KC)
        rwr = wcut(D)
        ub1T = wcut(KC)
        lg = wcut(BK * X, "p (t e) -> p t e", t=BK)
        pr = wcut(BK * X, "p (t e) -> p t e", t=BK)
        oh1 = wcut(BK * X, "p (t e) -> p t e", t=BK)
        oh2 = wcut(BK * X, "p (t e) -> p t e", t=BK)
        cand = wcut(BK * X, "p (t e) -> p t e", t=BK)
        iox = wcut(X)
        m1 = wcut(BK)
        m2 = wcut(BK)
        isel = wcut(BK)
        rsum = wcut(BK)
        mv3 = wcut(BK * 2, "p (t s) -> p t s", t=BK)

        def two(shape="p (u n) -> p u n", floats=2 * D, **dims):
            return [cut(floats, shape, **dims) for _ in range(2)]

        cut(0, restart=True)
        xp = two(u=2)
        hp = two(u=2)
        RH = 4
        xh = [cut(2 * D, "p (u n) -> p u n", u=2) for _ in range(RH)]
        aggT = two("p (k n) -> p k n", KC * 2 * NB, k=KC)
        un = two("p (k n) -> p k n", KC * 2 * NB, k=KC)
        y1b = cut(KC * 2 * NB, "p (k n) -> p k n", k=KC)
        y1T = two("p (k n) -> p k n", KC * 2 * NB, k=KC)
        aggcp = two(u=2)
        tb = two(u=2)
        tT = two("p (k n) -> p k n", KC * 2 * NB, k=KC)
        padrow = cut(XD * XW, "p (d w) -> p d w", d=XD)
        raw3 = cut(12, "p (u s) -> p u s", u=2)
        pair3 = two("p (u s) -> p u s", 4, u=2)
        var3 = two("p u -> p u", 2)
        rstd3 = two("p u -> p u", 2)
        half3 = cut(2)

        padrow_set = sem("padrow_set")
        xpads_out = sem("routed_pads_out")
        uw_in = sem("uw_in")
        fw_in = sem("fw_in")
        xp_in = [sem("xp_in0"), sem("xp_in1")]
        un_in = [sem("un_in0"), sem("un_in1")]
        hp_ready = sem("hp_ready")
        xh_ready = sem("xh_ready")
        agg_tr = sem("agg_tr")
        aggT_ready = sem("aggT_ready")
        y1_ps = sem("y1_ps")
        y1b_ready = sem("y1b_ready")
        y1_ready = sem("y1_ready")
        y2_ps = sem("y2_ps")
        x1_ready = sem("x1_ready")
        raw3_ready = sem("raw3_ready")
        pair3_ready = sem("pair3_ready")
        var3_ready = sem("var3_ready")
        rstd3_ready = sem("rstd3_ready")
        half3_ready = sem("half3_ready")
        x1_kept = sem("x1_kept")
        sx = sem("xh_chain")
        aggcp_ready = sem("aggcp_ready")
        rw_tr = sem("rw_tr")
        rwT_ready = sem("rwT_ready")
        tb_ready = sem("tb_ready")
        tb_tr = sem("tb_tr")
        tT_ready = sem("tT_ready")
        lg_ps = sem("lg_ps")
        lg_ready = sem("lg_ready")

        n_ = slice(0, NB)
        UA, U1, U2, UT, UL = 1, 2, 3, 4, 5

        def update(eng, step):
            pipeline(eng, NP2, UL, RH, step, peel=2)

        with nc.Block() as block:
            @block.sync
            def _(sp):
                sp.dma_start(uW1s, uW1[D:2 * D, :].rearrange("(k p) n -> p k n", p=P)).then_inc(uw_in, 16)
                sp.dma_start(uW2s, uW2.rearrange("(k p) n -> p k n", p=P)).then_inc(uw_in, 16)
                sp.dma_start(ub1T, ub1.rearrange("(k p) -> p k", p=P)).then_inc(uw_in, 16)
                sp.dma_start(rwr[0:X], router_w).then_inc(uw_in, 16)
                sp.wait_ge(padrow_set, 2)
                xsv = xsd.rearrange("(g p) f -> p g f", p=P)

                def empty_slots(m):
                    half = padrow[:, XD // 2 * m.mod(2):XD // 2 * (m.mod(2) + 1)]
                    sp.dma_start(xsv[:, bass.ds(m.of(XD // 2), XD // 2), :], half).then_inc(xpads_out, 16)

                def step(m):
                    a = m - UA
                    if a.within(NP2):
                        wait(sp, y1b_ready, a.of(1, -1))
                        sp.dma_start(un[a.mod(2)], ud[bass.ds(a.of(), 1)].rearrange("t p k u n -> (t p) k (u n)")).then_inc(un_in[a.mod(2)], 16)
                    s = m.mod(2)
                    if m.within(NP2):
                        wait(sp, xh_ready, m.of(1, -1))
                        sp.dma_start(xp[s][n_], x[bass.ds(m.of(2 * NB), 2 * NB), :].rearrange("(u p) f -> p u f", p=NB)).then_inc(xp_in[s], 16)
                        empty_slots(m)
                pipeline(sp, NP2, UA, 2, step, peel=2)
                for g in range(NP2 * XD // 2, XT, XD // 2):
                    d, o = min(XD // 2, XT - g), g % XD
                    sp.dma_start(xsv[:, g:g + d, :], padrow[:, o:o + d]).then_inc(xpads_out, 16)
                for k in range(KC):
                    sp.dma_start(w1s[:, k], w1[:, k * P:(k + 1) * P, :].rearrange("e p n -> p e n")).then_inc(fw_in, 16)
                    sp.dma_start(w2s[:, k], w2[:, k * P:(k + 1) * P, :].rearrange("e p n -> p e n")).then_inc(fw_in, 16)
                sp.dma_start(b1b, b1.rearrange("e n -> (e n)").partition_broadcast(P)).then_inc(fw_in, 16)
                sp.dma_start(b2b, b2.rearrange("e n -> (e n)").partition_broadcast(P)).then_inc(fw_in, 16)
                sp.wait_ge(fw_in, 16 * (2 * KC + 2))
                sp.wait_ge(xpads_out, 16 * -(-XT // (XD // 2)))

            @block.gpsimd
            def _(pool):
                nc.gpsimd.memset(padrow, 0.0).then_inc(padrow_set, 1)
                pool.wait_ge(padrow_set, 1)
                nc.gpsimd.iota(padrow[:, :, D].bitcast(i32), pattern=[[P, XD]], base=K2 * N,
                               channel_multiplier=1).then_inc(padrow_set, 1)
                nc.gpsimd.memset(half3, -0.5).then_inc(half3_ready, 1)
                pool.wait_ge(half3_ready, 1)

                def step(m):
                    b = m - UA
                    s = b.mod(2)
                    if b.within(NP2):
                        h = b.mod(RH)
                        pool.wait_ge(hp_ready, b.of(1, 1))
                        wait(pool, x1_kept, b.of(1, 1 - RH))
                        wait(pool, tb_ready, b.of(1, 1 - RH))
                        nc.gpsimd.tensor_tensor(xh[h][n_], xp[s][n_], hp[s][n_], ALU.add).then_inc(sx, 1)
                        pool.wait_ge(sx, b.of(1, 1))
                        nc.gpsimd.tensor_tensor(xh[h][n_], xh[h][n_],
                                                ub2b[n_, :].unsqueeze(1).to_broadcast([NB, 2, D]), ALU.add).then_inc(xh_ready, 1)
                    a = m - U2
                    if a.within(NP2):
                        s = a.mod(2)
                        pool.wait_ge(var3_ready, a.of(1, 1))
                        wait(pool, tb_ready, a.of(1, -1))
                        nc.gpsimd.tensor_tensor(rstd3[s][n_], var3[s][n_], half3[n_], ALU.pow).then_inc(rstd3_ready, 1)
                update(pool, step)

            @block.vector
            def _(dve):
                v = nc.vector

                def step(m):
                    s = m.mod(2)
                    a = m - UT
                    if a.within(NP2):
                        r = a.mod(2)
                        dve.wait_ge(rstd3_ready, a.of(1, 1))
                        wait(dve, tb_tr, a.of(1, -1))
                        both = bass.ds(a.of(2), 2)
                        v.tensor_copy(mv3[n_, both, 0], pair3[r][n_, :, 0])
                        v.tensor_copy(mv3[n_, both, 1], rstd3[r][n_])
                        for u in range(2):
                            last = v.tensor_scalar(tb[r][n_, u], xh[a.mod(RH)][n_, u], pair3[r][n_, u, 0:1],
                                                   rstd3[r][n_, u:u + 1], ALU.subtract, ALU.mult)
                        last.then_inc(tb_ready, 1)
                    a = m - U2
                    if a.within(NP2):
                        r, h = a.mod(2), a.mod(RH)
                        dve.wait_ge(y2_ps, a.of(1, 1))
                        dve.wait_ge(xh_ready, a.of(1, 1))
                        v.tensor_tensor(xh[h][n_].rearrange("p u n -> p (u n)"), ps[n_, 4, :],
                                        xh[h][n_].rearrange("p u n -> p (u n)"), ALU.add).then_inc(x1_ready, 1)
                        dve.wait_ge(x1_ready, a.of(1, 1))
                        for u in range(2):
                            v.bn_stats(raw3[n_, u], xh[h][n_, u]).then_inc(raw3_ready, 1)
                        wait_apart(dve, raw3_ready, a.of(2, 2), passed_dve)
                        for u in range(2):
                            v.bn_aggr(pair3[r][n_, u], raw3[n_, u]).then_inc(pair3_ready, 1)
                    a = m - U1
                    if a.within(NP2):
                        r = a.mod(2)
                        dve.wait_ge(y1_ps, a.of(1, 1))
                        dve.wait_ge(un_in[r], a.per(2, 16, 16))
                        wait(dve, y1_ready, a.of(1, 0))
                        v.tensor_tensor(y1b, ps[:, 2, 0:4 * NB].rearrange("p (k n) -> p k n", k=KC), un[r], ALU.add).then_inc(y1b_ready, 1)
                    a = m - U2
                    if a.within(NP2):
                        dve.wait_ge(pair3_ready, a.of(2, 2))
                        v.tensor_scalar(var3[a.mod(2)][n_], pair3[a.mod(2)][n_, :, 1], EPS, None, ALU.add).then_inc(var3_ready, 1)
                    if m.within(NP2):
                        dve.wait_ge(xp_in[s], m.per(2, 16, 16))
                        wait(dve, xh_ready, m.of(1, -1))
                        for u in range(2):
                            t = bass.ds(m.of(2, u), 1)
                            last = v.tensor_scalar(hp[s][n_, u], xp[s][n_, u], mv1[n_, t, 0], mv1[n_, t, 1],
                                                   ALU.subtract, ALU.mult)
                        last.then_inc(hp_ready, 1)

                update(dve, step)

            @block.scalar
            def _(act):
                act.wait_ge(uw_in, 64)
                act.wait_ge(rw_tr, 1)
                nc.scalar.activation(rws, ps[:, 7, 0:KC * X].rearrange("p (k e) -> p k e", k=KC), ACT.Copy).then_inc(rwT_ready, 1)

                def step(m):
                    if m.within(NP2):
                        wait_apart(act, agg_tr, m.of(1, -1), passed_act)
                        nc.scalar.activation(aggcp[m.mod(2)][n_], agg[n_, bass.ds(m.of(2), 2), :], ACT.Copy).then_inc(aggcp_ready, 1)
                    a = m - UA
                    if a.within(NP2):
                        act.wait_ge(agg_tr, a.of(1, 1))
                        wait(act, y1_ps, a.of(1, -1))
                        nc.scalar.activation(aggT[a.mod(2)], ps[:, a.mod(2), 0:4 * NB].rearrange("p (k n) -> p k n", k=KC),
                                             ACT.Copy).then_inc(aggT_ready, 1)
                    a = m - U2
                    if a.within(NP2):
                        wait_apart(act, x1_ready, a.of(1, 1), passed_act)
                        nc.scalar.activation(agg[n_, bass.ds(a.of(2), 2), :], xh[a.mod(RH)][n_], ACT.Copy).then_inc(x1_kept, 1)
                    a = m - U1
                    if a.within(NP2):
                        act.wait_ge(y1b_ready, a.of(1, 1))
                        wait(act, y2_ps, a.of(1, -1))
                        for k in range(KC):
                            last = nc.scalar.activation(y1T[a.mod(2)][:, k], y1b[:, k], ACT.Silu, bias=ub1T[:, k:k + 1])
                        last.then_inc(y1_ready, 1)
                    a = m - UL
                    if a.within(NP2):
                        wait_apart(act, lg_ps, a.of(1, 1), passed_act)
                        nc.scalar.activation(lg[n_, bass.ds(a.of(2), 2), :],
                                             ps[n_, 5, 0:2 * X].rearrange("p (u e) -> p u e", u=2), ACT.Copy).then_inc(lg_ready, 1)
                    a = m - UT
                    if a.within(NP2):
                        act.wait_ge(tb_tr, a.of(1, 1))
                        wait(act, lg_ps, a.of(1, -1))
                        nc.scalar.activation(tT[a.mod(2)], ps[:, 3, 0:4 * NB].rearrange("p (k n) -> p k n", k=KC),
                                             ACT.Copy).then_inc(tT_ready, 1)
                update(act, step)

            @block.tensor
            def _(pe):
                t_ = nc.tensor
                pe.wait_ge(uw_in, 64)
                for k in range(KC):
                    last = t_.transpose(ps[:, 7, k * X:(k + 1) * X], rwr[0:X, k * P:(k + 1) * P], ident[0:X, 0:X])
                last.then_inc(rw_tr, 1)
                pe.wait_ge(rwT_ready, 1)

                def transposes(bank, rows, done):
                    for u in range(2):
                        for k in range(KC):
                            c = k * 2 * NB + u * NB
                            last = t_.transpose(ps[:, bank, c:c + NB], rows[n_, u, k * P:(k + 1) * P], ident[n_, n_])
                    last.then_inc(done, 1)

                def step(m):
                    a = m - UA
                    if a.within(NP2):
                        pe.wait_ge(aggcp_ready, a.of(1, 1))
                        wait(pe, aggT_ready, a.of(1, -1))
                        transposes(a.mod(2), aggcp[a.mod(2)], agg_tr)
                    a = m - U2
                    if a.within(NP2):
                        pe.wait_ge(y1_ready, a.of(1, 1))
                        wait(pe, x1_ready, a.of(1, 0))
                        for u in range(2):
                            for k in range(KC):
                                last = t_.matmul(ps[n_, 4, u * D:(u + 1) * D], y1T[a.mod(2)][:, k, u * NB:(u + 1) * NB], uW2s[:, k],
                                                 start=(k == 0), stop=(k == KC - 1))
                        last.then_inc(y2_ps, 1)
                    a = m - U1
                    if a.within(NP2):
                        pe.wait_ge(aggT_ready, a.of(1, 1))
                        wait(pe, y1b_ready, a.of(1, 0))
                        for f in range(KC):
                            for k in range(KC):
                                last = t_.matmul(ps[:, 2, f * 2 * NB:(f + 1) * 2 * NB], uW1s[:, k, f * P:(f + 1) * P],
                                                 aggT[a.mod(2)][:, k], start=(k == 0), stop=(k == KC - 1))
                        last.then_inc(y1_ps, 1)
                    a = m - UL
                    if a.within(NP2):
                        pe.wait_ge(tT_ready, a.of(1, 1))
                        wait(pe, lg_ready, a.of(1, 0))
                        for u in range(2):
                            for k in range(KC):
                                last = t_.matmul(ps[n_, 5, u * X:(u + 1) * X], tT[a.mod(2)][:, k, u * NB:(u + 1) * NB], rws[:, k],
                                                 start=(k == 0), stop=(k == KC - 1))
                        last.then_inc(lg_ps, 1)
                    a = m - UT
                    if a.within(NP2):
                        pe.wait_ge(tb_ready, a.of(1, 1))
                        wait(pe, tT_ready, a.of(1, 0))
                        transposes(3, tb[a.mod(2)], tb_tr)
                update(pe, step)

        cut(0, restart=True)
        taken = cut(X * K2 * BK, "p (e k t) -> p e k t", e=X, k=K2)
        slot = cut(X * K2 * BK, "p (e k t) -> p e k t", e=X, k=K2)
        onex = cut(X * K2 * BK)
        tri2 = cut(P)
        ones2 = cut(P)
        xcnt = cut(X)
        xtiles = cut(X)
        xtilesi = cut(X, dt=i32)
        xstart = cut(X)
        xbase = cut(X)
        xcmp = cut(X)
        xtab = cut(1)
        xtabi = cut(1, dt=i32)
        pidx = cut(1)
        xposf = cut(K2 * BK, "p (k t) -> p k t", k=K2)
        xposi = rec[:, :, :].rearrange("p g f -> p (g f)")[:, 0:K2 * BK].bitcast(i32).rearrange("p (t k) -> p t k", k=K2)
        home = rec[:, :, :].rearrange("p g f -> p (g f)")[:, K2 * BK:2 * K2 * BK].bitcast(i32).rearrange("p (t k) -> p t k", k=K2)

        iox_ready = sem("iox_ready")
        tk = sem("top2_chain")
        sh_ready = sem("shifted_ready")
        ex_ready = sem("exp_ready")
        xcnt_ready = sem("xcnt_ready")
        xpre_ready = sem("xpre_ready")
        xtab_ready = sem("xtab_ready")
        xtab_out = sem("xtab_out")
        xtab_in = sem("xtab_in")

        with nc.Block() as block:
            @block.gpsimd
            def _(pool):
                nc.gpsimd.iota(iox, pattern=[[1, X]], base=0, channel_multiplier=0,
                               allow_small_or_imprecise_dtypes=True).then_inc(iox_ready, 1)
                nc.gpsimd.iota(pidx, pattern=[[1, 1]], base=0, channel_multiplier=1,
                               allow_small_or_imprecise_dtypes=True).then_inc(iox_ready, 1)
                nc.gpsimd.iota(home, pattern=[[K2 * NB, BK], [1, K2]], base=0, channel_multiplier=K2).then_inc(iox_ready, 1)
                nc.gpsimd.memset(onex, 1.0).then_inc(iox_ready, 1)
                nc.gpsimd.memset(ones2, 1.0).then_inc(iox_ready, 1)
                pool.wait_ge(iox_ready, 5)
                nc.gpsimd.affine_select(out=tri2, in_=ones2, compare_op=ALU.is_gt, fill=0.0,
                                        base=0, pattern=[[1, P]], channel_multiplier=-1).then_inc(iox_ready, 1)

            @block.sync
            def _(sp):
                sp.wait_ge(xtab_ready, 1)
                sp.dma_start(xtabd, xtabi).then_inc(xtab_out, 16)
                sp.wait_ge(xtab_out, 16)
                sp.dma_start(tabrows[0][0:1, PADT:PADT + P],
                             xtabd.rearrange("p k -> (p k)").rearrange("(a n) -> a n", a=1)).then_inc(xtab_in, 16)
                sp.wait_ge(xtab_in, 16)

            @block.vector
            def _(dve):
                v = nc.vector
                done = [0]

                def link(ins):
                    done[0] += 1
                    ins.then_inc(tk, 1)
                    dve.wait_ge(tk, done[0])

                def wide(a):
                    return a[n_].unsqueeze(2).to_broadcast([NB, BK, X])

                iow = iox[n_].unsqueeze(1).to_broadcast([NB, BK, X])
                dve.wait_ge(iox_ready, 6)
                link(v.tensor_reduce(out=m1[n_], in_=lg[n_], axis=AX.X, op=ALU.max))
                v.tensor_tensor(lg[n_], lg[n_], wide(m1), ALU.subtract).then_inc(sh_ready, 1)
                dve.wait_ge(ex_ready, 1)
                link(v.tensor_reduce(out=rsum[n_], in_=pr[n_], axis=AX.X, op=ALU.add))
                link(v.reciprocal(rsum[n_], rsum[n_]))
                link(v.tensor_tensor(pr[n_], pr[n_], wide(rsum), ALU.mult))
                for top, oh in ((m1, oh1), (m2, oh2)):
                    link(v.tensor_reduce(out=top[n_], in_=pr[n_], axis=AX.X, op=ALU.max))
                    link(v.tensor_tensor(cand[n_], pr[n_], wide(top), ALU.is_lt))
                    link(v.scalar_tensor_tensor(out=cand[n_], in0=cand[n_], scalar=float(X), in1=iow,
                                                op0=ALU.mult, op1=ALU.add))
                    link(v.tensor_reduce(out=isel[n_], in_=cand[n_], axis=AX.X, op=ALU.min))
                    link(v.tensor_tensor(oh[n_], iow, wide(isel), ALU.is_equal))
                    if oh is oh1:
                        link(v.scalar_tensor_tensor(out=pr[n_], in0=oh[n_], scalar=-2.0, in1=pr[n_],
                                                    op0=ALU.mult, op1=ALU.add))
                link(v.tensor_tensor(rsum[n_], m1[n_], m2[n_], ALU.add))
                link(v.tensor_scalar(rsum[n_], rsum[n_], 1e-12, None, ALU.max))
                link(v.reciprocal(rsum[n_], rsum[n_]))
                link(v.tensor_tensor(m1[n_], m1[n_], rsum[n_], ALU.mult))
                link(v.tensor_tensor(m2[n_], m2[n_], rsum[n_], ALU.mult))
                for k, oh in ((0, oh1), (1, oh2)):
                    link(v.tensor_copy(taken[n_, :, k, :], oh[n_].rearrange("p t e -> p e t")))
                v.tensor_reduce(out=xcnt[n_], in_=taken[n_].rearrange("p e k t -> p e (k t)"), axis=AX.X,
                                op=ALU.add).then_inc(xcnt_ready, 1)
                takf, slotf = (a.rearrange("p e k t -> p (e k t)") for a in (taken[n_], slot[n_]))
                link(v.tensor_tensor_scan(slotf, onex[n_], takf, 0.0, ALU.mult, ALU.add))
                dve.wait_ge(xpre_ready, 2)
                link(v.tensor_scalar(xtilesi, ps[:, 5, 0:X], float(P - 1), None, ALU.add))
                link(v.tensor_scalar(xtilesi, xtilesi, 7, None, ALU.arith_shift_right))
                link(v.tensor_copy(xtiles, xtilesi))
                link(v.tensor_tensor_scan(xstart, onex[:, 0:X], xtiles, 0.0, ALU.mult, ALU.add))
                link(v.tensor_tensor(xstart, xstart, xtiles, ALU.subtract))
                link(v.tensor_scalar(xcmp, xstart, pidx, None, ALU.is_le))
                link(v.tensor_reduce(out=xtab, in_=xcmp, axis=AX.X, op=ALU.add))
                v.tensor_scalar(xtabi, xtab, -1.0, float(D), ALU.add, ALU.mult).then_inc(xtab_ready, 1)
                link(v.tensor_scalar(xbase[n_], xstart[n_], float(P), -1.0, ALU.mult, ALU.add))
                link(v.tensor_tensor(xbase[n_], xbase[n_], ps[n_, 4, 0:X], ALU.add))
                link(v.tensor_tensor(xbase[n_], xbase[n_], slot[n_, :, 0, 0], ALU.subtract))
                link(v.tensor_tensor(xbase[n_], xbase[n_], taken[n_, :, 0, 0], ALU.add))
                link(v.tensor_tensor(slot[n_].rearrange("p e k t -> p e (k t)"), slot[n_].rearrange("p e k t -> p e (k t)"),
                                     xbase[n_].unsqueeze(2).to_broadcast([NB, X, K2 * BK]), ALU.add))
                link(v.tensor_tensor(slotf, slotf, takf, ALU.mult))
                link(v.tensor_reduce(out=xposf[n_].rearrange("p k t -> p (k t)"),
                                     in_=slot[n_].rearrange("p e k t -> p (k t) e"), axis=AX.X, op=ALU.add))
                link(v.tensor_copy(xposi[n_], xposf[n_].rearrange("p k t -> p t k")))

            @block.scalar
            def _(act):
                act.wait_ge(sh_ready, 1)
                nc.scalar.activation(pr[n_], lg[n_], ACT.Exp).then_inc(ex_ready, 1)

            @block.tensor
            def _(pe):
                t_ = nc.tensor
                pe.wait_ge(xcnt_ready, 1)
                t_.matmul(ps[:, 4, 0:X], tri2[n_, :], xcnt[n_], start=True, stop=True).then_inc(xpre_ready, 1)
                t_.matmul(ps[:, 5, 0:X], ones2[n_], xcnt[n_], start=True, stop=True).then_inc(xpre_ready, 1)

        XP = XT // 2
        RX, RY, RS = 8, 4, 4
        L1, L2H, L2 = 1, 2, 3
        cut(0, restart=True)
        ts = cut(RS * K2 * XW, "p (r k w) -> p r k w", r=RS, k=K2)
        tslot = cut(RS * K2, "p (r k) -> p r k", dt=i32, r=RS)
        xs = cut(RX * 2 * XW, "p (r u w) -> p r u w", r=RX, u=2)
        yb = cut(RY * 2 * D, "p (r u n) -> p r u n", r=RY, u=2)
        xsT = cut(2 * 2 * D, "p (r n) -> p r n", r=2)
        hb = cut(2 * D, "p (u n) -> p u n", u=2)
        hg = cut(2 * 2 * D, "p (r u n) -> p r u n", r=2, u=2)
        hT = cut(2 * 2 * D, "p (r n) -> p r n", r=2)
        tsr = ts.bitcast(i32)
        xsr = xs.bitcast(i32)
        w1f = w1s.rearrange("p k e n -> p k (e n)")
        w2f = w2s.rearrange("p k e n -> p k (e n)")

        ts_parts = sem("ts_parts")
        ts_ready = sem("ts_ready")
        xt_added = sem("xt_added")
        ts_out = [sem(f"ts_out{r}") for r in range(RS)]
        xs_in = [sem(f"xs_in{r}") for r in range(RX)]
        xs_tr = sem("xs_tr")
        xsT_ready = sem("xsT_ready")
        h_ps = sem("h_ps")
        hb_ready = sem("hb_ready")
        hg_ready = sem("hg_ready")
        h_tr = sem("h_tr")
        hT_ready = sem("hT_ready")
        y_ps = sem("y_ps")
        yb_ready = sem("yb_ready")
        y_out = [sem(f"y_out{r}") for r in range(RY)]

        with nc.Block() as block:
            @block.sync
            def _(sp):
                for r in range(RS):
                    sp.wait_ge(ts_out[r], 16 * K2 * len(range(r, BK, RS)))

                def step(m):
                    r = m.mod(RX)
                    wait(sp, y_out[m.mod(RY)], m.per(RY, 32, -32))
                    sp.dma_start(xs[:, r], xsd[bass.ds(m.of(2 * P), 2 * P), :].rearrange("(u p) w -> p u w", p=P)).then_inc(xs_in[r], 16)
                pipeline(sp, XP, 0, RX, step)

            @block.gpsimd
            def _(pool):
                def route(m):
                    r = m.mod(RS)
                    wait_apart(pool, ts_ready, m.of(1, 1), passed_pool)
                    for k in range(K2):
                        pool.indirect_dma_start(xsd, bass.IndirectOffsetOnAxis(ap=tslot[n_, r, k:k + 1], axis=0),
                                                ts[n_, r, k], None).then_inc(ts_out[r], 16)
                pipeline(pool, BK, 0, RS, route)

                def step(m):
                    y = m - L2
                    if y.within(XP):
                        r = y.mod(RY)
                        wait_apart(pool, yb_ready, y.of(1, 1), passed_pool)
                        for u in range(2):
                            pool.indirect_dma_start(yd, bass.IndirectOffsetOnAxis(ap=xsr[:, y.mod(RX), u, D:XW], axis=0),
                                                    yb[:, r, u], None).then_inc(y_out[r], 16)
                pipeline(pool, XP, L2, RX, step)
                for r in range(RY):
                    pool.wait_ge(y_out[r], 32 * len(range(r, XP, RY)))

            @block.vector
            def _(dve):
                v = nc.vector

                def route(m):
                    r = m.mod(RS)
                    wait(dve, ts_out[r], m.per(RS, 16 * K2, 0))
                    wait(dve, xt_added, m.of(1, 1 - RS))
                    t = bass.ds(m.of(), 1)
                    v.tensor_scalar(ts[n_, r, :, 0:D], agg[n_, t, :].to_broadcast([NB, K2, D]),
                                    mv3[n_, t, 0], mv3[n_, t, 1], ALU.subtract, ALU.mult).then_inc(ts_parts, 1)
                    v.tensor_copy(tsr[n_, r, :, D], home[n_, t, :].rearrange("p t k -> p (t k)"))
                    v.tensor_copy(tslot[n_, r], xposi[n_, t, :].rearrange("p t k -> p (t k)")).then_inc(ts_ready, 1)
                    dve.wait_ge(ts_parts, m.of(1, 1))
                    v.tensor_tensor(agg[n_, t, :].rearrange("p t f -> p (t f)"), agg[n_, t, :].rearrange("p t f -> p (t f)"),
                                    ts[n_, r, 0, 0:D], ALU.add).then_inc(xt_added, 1)
                pipeline(dve, BK, 0, RS, route)

                regs = [v.alloc_register(f"expert_of_tile{j}") for j in range(2 * (RX + L2))]
                offs = [None] * (2 * (RX + L2))

                def enter(it):
                    v.load(regs, tabrows[0][0:1, bass.ds(it * (2 * RX) + PADT - 2 * L2, 2 * (RX + L2))])
                    offs[:] = [v.snap(r, min_val=0, max_val=(X - 1) * D) for r in regs]

                def step(m):
                    b = m.c % RX if isinstance(m.it, int) else m.c - RX
                    a = m - L1
                    if a.within(XP):
                        dve.wait_ge(h_ps, a.of(1, 1))
                        wait(dve, hg_ready, a.of(1, 0))
                        for u in range(2):
                            o = offs[2 * (b + L2 - L1) + u]
                            last = v.tensor_tensor(hb[:, u], ps[:, 1, u * D:(u + 1) * D], b1b[:, bass.ds(o, D)], ALU.add)
                        last.then_inc(hb_ready, 1)
                    a = m - L2
                    if a.within(XP):
                        r = a.mod(RY)
                        dve.wait_ge(y_ps, a.of(1, 1))
                        wait(dve, y_out[r], a.per(RY, 32, 0))
                        for u in range(2):
                            o = offs[2 * b + u]
                            last = v.tensor_tensor(yb[:, r, u], ps[:, 3, u * D:(u + 1) * D], b2b[:, bass.ds(o, D)], ALU.add)
                        last.then_inc(yb_ready, 1)
                pipeline(dve, XP, L2, RX, step, enter)

            @block.scalar
            def _(act):
                def step(m):
                    if m.within(XP):
                        act.wait_ge(xs_tr, m.of(1, 1))
                        wait(act, h_ps, m.of(1, -1))
                        nc.scalar.activation(xsT[:, m.mod(2)], ps[:, 0, :], ACT.Copy).then_inc(xsT_ready, 1)
                    a = m - L1
                    if a.within(XP):
                        act.wait_ge(hb_ready, a.of(1, 1))
                        wait(act, h_tr, a.of(1, -1))
                        nc.scalar.activation(hg[:, a.mod(2)], hb, ACT.Gelu).then_inc(hg_ready, 1)
                    a = m - L2H
                    if a.within(XP):
                        act.wait_ge(h_tr, a.of(1, 1))
                        wait(act, y_ps, a.of(1, -1))
                        nc.scalar.activation(hT[:, a.mod(2)], ps[:, 2, :], ACT.Copy).then_inc(hT_ready, 1)
                pipeline(act, XP, L2, RX, step)

            @block.tensor
            def _(pe):
                t_ = nc.tensor
                regs = [t_.alloc_register(f"expert_of_tile{j}") for j in range(2 * (RX + L2))]
                offs = [None] * (2 * (RX + L2))

                def enter(it):
                    t_.load(regs, tabrows[0][0:1, bass.ds(it * (2 * RX) + PADT - 2 * L2, 2 * (RX + L2))])
                    offs[:] = [t_.snap(r, min_val=0, max_val=(X - 1) * D) for r in regs]

                def step(m):
                    b = m.c % RX if isinstance(m.it, int) else m.c - RX
                    if m.within(XP):
                        r = m.mod(RX)
                        pe.wait_ge(xs_in[r], m.per(RX, 16, 16))
                        wait(pe, xsT_ready, m.of(1, 0))
                        for u in range(2):
                            for k in range(KC):
                                c = (u * KC + k) * P
                                last = t_.transpose(ps[:, 0, c:c + P], xs[:, r, u, k * P:(k + 1) * P], ident[:, :])
                        last.then_inc(xs_tr, 1)
                    a = m - L1
                    if a.within(XP):
                        pe.wait_ge(xsT_ready, a.of(1, 1))
                        wait(pe, hb_ready, a.of(1, 0))
                        for u in range(2):
                            o = offs[2 * (b + L2 - L1) + u]
                            for k in range(KC):
                                c = (u * KC + k) * P
                                last = t_.matmul(ps[:, 1, u * D:(u + 1) * D], xsT[:, a.mod(2), c:c + P], w1f[:, k, bass.ds(o, D)],
                                                 start=(k == 0), stop=(k == KC - 1))
                        last.then_inc(h_ps, 1)
                    a = m - L2
                    if a.within(XP):
                        pe.wait_ge(hT_ready, a.of(1, 1))
                        wait(pe, yb_ready, a.of(1, 0))
                        for u in range(2):
                            o = offs[2 * b + u]
                            for k in range(KC):
                                c = (u * KC + k) * P
                                last = t_.matmul(ps[:, 3, u * D:(u + 1) * D], hT[:, a.mod(2), c:c + P], w2f[:, k, bass.ds(o, D)],
                                                 start=(k == 0), stop=(k == KC - 1))
                        last.then_inc(y_ps, 1)
                    a = m - L2H
                    if a.within(XP):
                        pe.wait_ge(hg_ready, a.of(1, 1))
                        wait(pe, hT_ready, a.of(1, 0))
                        for u in range(2):
                            for k in range(KC):
                                c = (u * KC + k) * P
                                last = t_.transpose(ps[:, 2, c:c + P], hg[:, a.mod(2), u, k * P:(k + 1) * P], ident[:, :])
                        last.then_inc(h_tr, 1)
                pipeline(pe, XP, L2, RX, step, enter)

        RF = 4
        cut(0, restart=True)
        yin = cut(RF * 2 * K2 * D, "p (r u k n) -> p r u k n", r=RF, u=2, k=K2)
        acc = cut(RF * 2 * D, "p (r u n) -> p r u n", r=RF, u=2)
        yin_in = [sem(f"yin_in{r}") for r in range(RF)]
        acc_add = sem("acc_added")
        o_out = [sem(f"o_out{r}") for r in range(RF)]

        with nc.Block() as block:
            @block.sync
            def _(sp):
                def step(m):
                    r = m.mod(RF)
                    wait(sp, acc_add, m.of(4, 4 - 4 * RF))
                    rows = yd[bass.ds(m.of(2 * NB * K2), 2 * NB * K2), :]
                    sp.dma_start(yin[n_, r], rows.rearrange("(u p k) n -> p u k n", p=NB, k=K2)).then_inc(yin_in[r], 16)
                pipeline(sp, NP2, 0, RF, step)

            @block.scalar
            def _(act):
                def step(m):
                    r = m.mod(RF)
                    act.wait_ge(acc_add, m.of(4, 4))
                    act.dma_start(out[bass.ds(m.of(2 * NB), 2 * NB), :].rearrange("(u p) f -> p u f", p=NB), acc[n_, r]).then_inc(o_out[r], 16)
                pipeline(act, NP2, 0, RF, step)
                for r in range(RF):
                    act.wait_ge(o_out[r], 16 * len(range(r, NP2, RF)))

            @block.vector
            def _(dve):
                v = nc.vector

                def step(m):
                    r = m.mod(RF)
                    dve.wait_ge(yin_in[r], m.per(RF, 16, 16))
                    wait(dve, o_out[r], m.per(RF, 16, 0))
                    for k in range(K2):
                        for u in range(2):
                            t = bass.ds(m.of(2, u), 1)
                            if k:
                                dve.wait_ge(acc_add, m.of(4, u + 1))
                            before = acc[n_, r, u] if k else agg[n_, t, :].rearrange("p t f -> p (t f)")
                            v.scalar_tensor_tensor(out=acc[n_, r, u], in0=yin[n_, r, u, k], scalar=(m1, m2)[k][n_, t],
                                                   in1=before, op0=ALU.mult, op1=ALU.add).then_inc(acc_add, 1)
                pipeline(dve, NP2, 0, RF, step)


_INS = ["x", "src", "dst", "edge_weight1", "L0_gnn_mW1", "L0_gnn_mb1", "L0_gnn_ln_g", "L0_gnn_ln_b", "L0_gnn_mW2",
        "L0_gnn_mb2", "L0_gnn_uW1", "L0_gnn_ub1", "L0_gnn_uW2", "L0_gnn_ub2", "L0_ffn_router_w", "L0_ffn_w1",
        "L0_ffn_b1", "L0_ffn_w2", "L0_ffn_b2"]


def kernel(**inputs):
    import concourse.bacc as bacc
    from concourse.bass_utils import run_bass_kernel_spmd

    nc = bacc.Bacc("TRN2", target_bir_lowering=False, num_devices=1)
    arrays, args = {}, []
    for name in _INS:
        a = np.ascontiguousarray(inputs[name])
        arrays[f"in_{name}"] = a
        args.append(nc.dram_tensor(f"in_{name}", a.shape, mybir.dt.from_np(a.dtype), kind="ExternalInput").ap())
    args.append(nc.dram_tensor("out", (N, D), f32, kind="ExternalOutput").ap())
    gnn_moe_kernel(nc, *args)
    r = run_bass_kernel_spmd(nc, [arrays], core_ids=[0])
    return r.results[0]["out"]
```
